# Optimizing a Trainium2 kernel written in Bass

```python
import numpy as np
import jax
import jax.numpy as jnp

def _softmax(x, axis=-1):
    return jax.nn.softmax(x, axis=axis)

def _gelu(x):
    return jax.nn.gelu(x, approximate=True)

def _silu(x):
    return jax.nn.silu(x)

def _sigmoid(x):
    return jax.nn.sigmoid(x)

def _layernorm(x, axis=-1, eps=1e-05):
    m = jnp.mean(x, axis=axis, keepdims=True)
    v = jnp.var(x, axis=axis, keepdims=True)
    return (x - m) / jnp.sqrt(v + eps)

def _scatter_add(tgt, idx, src, axis=0):
    return tgt.at[idx].add(src)

def _segment_sum(src, seg, n):
    return jax.ops.segment_sum(src, seg, n)
kernel_name = 'mk_perceiver_d2_seqx_r4_8b2197'

def setup_inputs(seed: int=0):
    np.random.seed(seed)
    _w = jnp.asarray

    def _rec_inputs():
        import jax
        import jax.numpy as jnp
        _rk = jax.random.key(seed)
        x = 7.22e-05 + 1 * jax.random.normal(jax.random.fold_in(_rk, 1), (32, 64, 256), jnp.float32)
        _lenS = 64 - jax.random.randint(jax.random.fold_in(_rk, 7), (32,), 0, max(1, 64 // 4) + 1, jnp.int32)
        _lenS2 = 1601 - jax.random.randint(jax.random.fold_in(_rk, 8), (32,), 0, max(1, 1601 // 4) + 1, jnp.int32)
        _ctx_1024P = jax.random.normal(jax.random.fold_in(_rk, 11), (32, 16, 256), jnp.float32)
        _ctx_1024c = jax.random.dirichlet(jax.random.fold_in(_rk, 511), 0.3 * jnp.ones((16,), jnp.float32), (32, 1601))
        _ctx_1024t = jnp.einsum('bsk,bkd->bsd', _ctx_1024c, _ctx_1024P)
        _ctx_1024t = _ctx_1024t * jax.lax.rsqrt(jnp.mean(jnp.square(_ctx_1024t)) + 1e-12) * 0.953939
        ctx_1024 = -0.000514642 + 1.00011 * (_ctx_1024t + 0.3 * jax.random.normal(jax.random.fold_in(_rk, 611), (32, 1601, 256), jnp.float32))
        return (x, ctx_1024)
    x, ctx_1024 = _rec_inputs()

    def _L0_xattn_setup():
        import jax, jax.numpy as jnp
        import numpy as np
        B, L_ENC, L_DEC, D = (16, 128, 128, 256)
        key = jax.random.key(seed)
        k1, k2, k3, k4, k5, k6 = jax.random.split(key, 6)
        encoder_hc = jax.random.normal(k1, (B, L_ENC, D), dtype=jnp.float32)
        decoder_hq = jax.random.normal(k2, (B, L_DEC, D), dtype=jnp.float32)
        w_sim = jax.random.normal(k3, (3 * D,), dtype=jnp.float32) * 0.02
        b_sim = jax.random.normal(k4, (1,), dtype=jnp.float32) * 0.02
        W_qv = jax.random.normal(k5, (4 * D, D), dtype=jnp.float32) * 0.02
        b_qv = jax.random.normal(k6, (D,), dtype=jnp.float32) * 0.02
        return {'encoder_hc': encoder_hc, 'decoder_hq': decoder_hq, 'w_sim': w_sim, 'b_sim': b_sim, 'W_qv': W_qv, 'b_qv': b_qv}
    _L0_xattn_all = _L0_xattn_setup()
    _L0_xattn_in = {k: v for k, v in _L0_xattn_all.items() if k in ('w_sim', 'b_sim', 'W_qv', 'b_qv')}
    del _L0_xattn_all

    def _L0_attn_setup():
        import jax, jax.numpy as jnp
        import numpy as np
        import math
        EMBED = 256
        HEADS = 16
        HEAD_DIM = EMBED // HEADS
        B, N = (2, 512)
        key = jax.random.key(seed)
        ks = jax.random.split(key, 8)
        s = 1.0 / math.sqrt(EMBED)
        Wq = jax.random.uniform(ks[0], (EMBED, EMBED), jnp.float32, -s, s)
        bq = jax.random.uniform(ks[1], (EMBED,), jnp.float32, -s, s)
        Wk = jax.random.uniform(ks[2], (EMBED, EMBED), jnp.float32, -s, s)
        bk = jax.random.uniform(ks[3], (EMBED,), jnp.float32, -s, s)
        Wv = jax.random.uniform(ks[4], (EMBED, EMBED), jnp.float32, -s, s)
        bv = jax.random.uniform(ks[5], (EMBED,), jnp.float32, -s, s)
        Wp = jax.random.normal(ks[6], (HEAD_DIM, HEAD_DIM), jnp.float32)
        x = jax.random.normal(ks[7], (B, N, EMBED), jnp.float32)
        return {'x': x, 'Wq': Wq, 'bq': bq, 'Wk': Wk, 'bk': bk, 'Wv': Wv, 'bv': bv, 'Wp': Wp}
    _L0_attn_all = _L0_attn_setup()
    _L0_attn_in = {k: v for k, v in _L0_attn_all.items() if k in ('Wq', 'bq', 'Wk', 'bk', 'Wv', 'bv', 'Wp')}
    del _L0_attn_all

    def _L0_ffn_setup():
        import jax, jax.numpy as jnp
        import numpy as np
        D = 256
        H = 512
        E = 8
        TOP_K = 2
        N_SHARED = 1
        B, S = (2, 256)
        key = jax.random.key(seed)
        ks = jax.random.split(key, 12)
        sc = 0.02
        return {'hidden': jax.random.normal(ks[0], (B, S, D), jnp.float32), 'router_w': jax.random.normal(ks[1], (D, E), jnp.float32) * sc, 'router_b': jnp.zeros((E,), jnp.float32), 'sw1': jax.random.normal(ks[2], (D, H), jnp.float32) * sc, 'sb1': jnp.zeros((H,), jnp.float32), 'sw2': jax.random.normal(ks[3], (H, D), jnp.float32) * sc, 'sb2': jnp.zeros((D,), jnp.float32), 'rw1': jax.random.normal(ks[4], (E, D, H), jnp.float32) * sc, 'rb1': jnp.zeros((E, H), jnp.float32), 'rw2': jax.random.normal(ks[5], (E, H, D), jnp.float32) * sc, 'rb2': jnp.zeros((E, D), jnp.float32)}
    _L0_ffn_all = _L0_ffn_setup()
    _L0_ffn_in = {k: v for k, v in _L0_ffn_all.items() if k in ('router_w', 'router_b', 'sw1', 'sb1', 'sw2', 'sb2', 'rw1', 'rb1', 'rw2', 'rb2')}
    del _L0_ffn_all

    def _L1_xattn_setup():
        import jax, jax.numpy as jnp
        import numpy as np
        N_HEAD = 16
        key = jax.random.key(seed)
        ks = jax.random.split(key, 5)
        b, l, d = (4, 512, 256)
        dh = d // N_HEAD
        return {'q': jax.random.normal(ks[0], (b, l, d), dtype=jnp.float32), 'kv': jax.random.normal(ks[1], (b, l, d), dtype=jnp.float32), 'Wq': jax.random.normal(ks[2], (d, d), dtype=jnp.float32) * 0.02, 'Wkv': jax.random.normal(ks[3], (2 * dh, d), dtype=jnp.float32) * 0.02, 'Wc': jax.random.normal(ks[4], (d, d), dtype=jnp.float32) * 0.02}
    _L1_xattn_all = _L1_xattn_setup()
    _L1_xattn_in = {k: v for k, v in _L1_xattn_all.items() if k in ('Wq', 'Wkv', 'Wc')}
    del _L1_xattn_all

    def _L1_attn_setup():
        import jax, jax.numpy as jnp
        import numpy as np
        D = 256
        HS = 128
        NKV = 2

        def apply_rope(x):
            d = x.shape[-1]
            T = x.shape[-2]
            positions = jnp.arange(0, d, 2, dtype=jnp.float32)
            theta = 10000.0 ** (-2.0 * positions / d)
            angles = jnp.arange(T, dtype=jnp.float32)[:, None] * theta[None, :]
            cos, sin = (jnp.cos(angles), jnp.sin(angles))
            xr = x.reshape(x.shape[:-1] + (d // 2, 2))
            out = jnp.stack([xr[..., 0] * cos - xr[..., 1] * sin, xr[..., 1] * cos + xr[..., 0] * sin], axis=-1)
            return out.reshape(x.shape)
        key = jax.random.key(seed)
        k1, k2, k3, k4, k5 = jax.random.split(key, 5)
        B, T = (4, 512)
        x = jax.random.normal(k1, (B, T, D), dtype=jnp.float32)
        s = 1.0 / np.sqrt(D)
        Wq = jax.random.normal(k2, (NKV, HS, D), dtype=jnp.float32) * s
        Wk = jax.random.normal(k3, (HS, D), dtype=jnp.float32) * s
        Wv = jax.random.normal(k4, (HS, D), dtype=jnp.float32) * s
        Wo = jax.random.normal(k5, (D, NKV * HS), dtype=jnp.float32) * (1.0 / np.sqrt(NKV * HS))
        return {'x': x, 'Wq': Wq, 'Wk': Wk, 'Wv': Wv, 'Wo': Wo}
    _L1_attn_all = _L1_attn_setup()
    _L1_attn_in = {k: v for k, v in _L1_attn_all.items() if k in ('Wq', 'Wk', 'Wv', 'Wo')}
    del _L1_attn_all

    def _L1_ffn_setup():
        import jax, jax.numpy as jnp
        import numpy as np
        IN_DIM, OUT_DIM, N_PROTO, RANK = (256, 256, 32, 16)
        key = jax.random.key(seed)
        ks = jax.random.split(key, 5)
        x = jax.random.normal(ks[0], (2, 1024, IN_DIM), dtype=jnp.float32)
        prototypes = jax.random.normal(ks[1], (N_PROTO, IN_DIM), dtype=jnp.float32) * 0.02
        B = jax.random.normal(ks[2], (N_PROTO, RANK, IN_DIM), dtype=jnp.float32) * 0.02
        A = jax.random.normal(ks[3], (N_PROTO, OUT_DIM, RANK), dtype=jnp.float32) * 0.02
        bias = jnp.zeros((N_PROTO, OUT_DIM), dtype=jnp.float32)
        temp = jnp.asarray(1.0, dtype=jnp.float32)
        return {'x': x, 'prototypes': prototypes, 'B': B, 'A': A, 'bias': bias, 'temp': temp}
    _L1_ffn_all = _L1_ffn_setup()
    _L1_ffn_in = {k: v for k, v in _L1_ffn_all.items() if k in ('prototypes', 'B', 'A', 'bias', 'temp')}
    del _L1_ffn_all
    return {'x': x, 'ctx_1024': ctx_1024, 'L0_xattn_w_sim': _L0_xattn_in['w_sim'], 'L0_xattn_b_sim': _L0_xattn_in['b_sim'], 'L0_xattn_W_qv': _L0_xattn_in['W_qv'], 'L0_xattn_b_qv': _L0_xattn_in['b_qv'], 'L0_attn_Wq': _L0_attn_in['Wq'], 'L0_attn_bq': _L0_attn_in['bq'], 'L0_attn_Wk': _L0_attn_in['Wk'], 'L0_attn_bk': _L0_attn_in['bk'], 'L0_attn_Wv': _L0_attn_in['Wv'], 'L0_attn_bv': _L0_attn_in['bv'], 'L0_attn_Wp': _L0_attn_in['Wp'], 'L0_ffn_router_w': _L0_ffn_in['router_w'], 'L0_ffn_router_b': _L0_ffn_in['router_b'], 'L0_ffn_sw1': _L0_ffn_in['sw1'], 'L0_ffn_sb1': _L0_ffn_in['sb1'], 'L0_ffn_sw2': _L0_ffn_in['sw2'], 'L0_ffn_sb2': _L0_ffn_in['sb2'], 'L0_ffn_rw1': _L0_ffn_in['rw1'], 'L0_ffn_rb1': _L0_ffn_in['rb1'], 'L0_ffn_rw2': _L0_ffn_in['rw2'], 'L0_ffn_rb2': _L0_ffn_in['rb2'], 'L1_xattn_Wq': _L1_xattn_in['Wq'], 'L1_xattn_Wkv': _L1_xattn_in['Wkv'], 'L1_xattn_Wc': _L1_xattn_in['Wc'], 'L1_attn_Wq': _L1_attn_in['Wq'], 'L1_attn_Wk': _L1_attn_in['Wk'], 'L1_attn_Wv': _L1_attn_in['Wv'], 'L1_attn_Wo': _L1_attn_in['Wo'], 'L1_ffn_prototypes': _L1_ffn_in['prototypes'], 'L1_ffn_B': _L1_ffn_in['B'], 'L1_ffn_A': _L1_ffn_in['A'], 'L1_ffn_bias': _L1_ffn_in['bias'], 'L1_ffn_temp': _L1_ffn_in['temp']}

def reference(x, ctx_1024, L0_xattn_w_sim, L0_xattn_b_sim, L0_xattn_W_qv, L0_xattn_b_qv, L0_attn_Wq, L0_attn_bq, L0_attn_Wk, L0_attn_bk, L0_attn_Wv, L0_attn_bv, L0_attn_Wp, L0_ffn_router_w, L0_ffn_router_b, L0_ffn_sw1, L0_ffn_sb1, L0_ffn_sw2, L0_ffn_sb2, L0_ffn_rw1, L0_ffn_rb1, L0_ffn_rw2, L0_ffn_rb2, L1_xattn_Wq, L1_xattn_Wkv, L1_xattn_Wc, L1_attn_Wq, L1_attn_Wk, L1_attn_Wv, L1_attn_Wo, L1_ffn_prototypes, L1_ffn_B, L1_ffn_A, L1_ffn_bias, L1_ffn_temp):
    import jax
    import jax.numpy as jnp

    def _L0_xattn_ref(encoder_hc, decoder_hq, w_sim, b_sim, W_qv, b_qv):
        import jax, jax.numpy as jnp
        import numpy as np
        B, L_ENC, L_DEC, D = (16, 128, 128, 256)
        d = encoder_hc.shape[-1]
        w1, w2, w3 = (w_sim[:d], w_sim[d:2 * d], w_sim[2 * d:])
        Sim = (encoder_hc @ w1)[:, :, None] + (decoder_hq @ w2)[:, None, :] + jnp.einsum('bid,bjd->bij', encoder_hc * w3, decoder_hq) + b_sim[0]
        A = jax.nn.softmax(Sim, axis=2)
        hq_hat = jnp.einsum('bij,bjd->bid', A, decoder_hq)
        Batt = jax.nn.softmax(jnp.max(Sim, axis=2), axis=1)
        hc_bar = jnp.einsum('bi,bid->bd', Batt, encoder_hc)[:, None, :]
        hc_hat = jnp.broadcast_to(hc_bar, encoder_hc.shape)
        feats = jnp.concatenate([encoder_hc, hq_hat, encoder_hc * hq_hat, encoder_hc * hc_hat], axis=-1)
        hcq = feats @ W_qv + b_qv
        return hcq

    def _L0_attn_ref(x, Wq, bq, Wk, bk, Wv, bv, Wp):
        import jax, jax.numpy as jnp
        import numpy as np
        import math
        EMBED = 256
        HEADS = 16
        HEAD_DIM = EMBED // HEADS
        B, N = (2, 512)
        Bb, Nn, E = x.shape
        H, D = (HEADS, HEAD_DIM)
        q = (x @ Wq + bq).reshape(Bb, Nn, H, D)
        k = (x @ Wk + bk).reshape(Bb, Nn, H, D)
        v = (x @ Wv + bv).reshape(Bb, Nn, H, D)
        q = jnp.einsum('bnhe,ei->bnhi', q, Wp)
        k = jnp.einsum('bnhe,ei->bnhi', k, Wp)
        scores = jnp.einsum('bnhi,bmhi->bnhm', q, k) / math.sqrt(D)
        attn = jax.nn.softmax(scores, axis=-1)
        out = jnp.einsum('bnhm,bmhe->bnhe', attn, v).reshape(Bb, Nn, E)
        return out

    def _L0_ffn_ref(hidden, router_w, router_b, sw1, sb1, sw2, sb2, rw1, rb1, rw2, rb2):
        import jax, jax.numpy as jnp
        import numpy as np
        D = 256
        H = 512
        E = 8
        TOP_K = 2
        N_SHARED = 1
        B, S = (2, 256)
        b, s, d = hidden.shape
        T = b * s
        flat = hidden.reshape(T, d)
        router_logits = flat @ router_w + router_b
        router_probs = jax.nn.softmax(router_logits, axis=-1)
        topk_probs, topk_idx = jax.lax.top_k(router_probs, TOP_K)
        weights = jnp.zeros_like(router_probs).at[jnp.arange(T)[:, None], topk_idx].add(topk_probs)
        sh = jax.nn.gelu(flat @ sw1 + sb1, approximate=False)
        shared_out = (sh @ sw2 + sb2) / N_SHARED
        h1 = jax.nn.gelu(jnp.einsum('td,edh->teh', flat, rw1) + rb1[None], approximate=False)
        expert_out = jnp.einsum('teh,ehd->ted', h1, rw2) + rb2[None]
        mixed = jnp.einsum('ted,te->td', expert_out, weights)
        return (shared_out + mixed).reshape(b, s, d)

    def _L1_xattn_ref(q, kv, Wq, Wkv, Wc):
        import jax, jax.numpy as jnp
        import numpy as np
        N_HEAD = 16
        b, l, d = q.shape
        h = N_HEAD
        dh = d // h
        qp = jnp.einsum('bld,ed->ble', q, Wq)
        scores = jnp.einsum('bld,bmd->blm', qp, kv)
        idx = jnp.argmax(scores, axis=-1)
        mem = jnp.take_along_axis(kv, idx[..., None], axis=1)
        mkv = jnp.einsum('bld,ed->ble', mem, Wkv)
        mk, mv = jnp.split(mkv, 2, axis=-1)
        qh = qp.reshape(b, l, h, dh).transpose(0, 2, 1, 3)
        scale = 1.0 / np.sqrt(dh).astype(np.float32)
        logits = jnp.einsum('bhld,bmd->bhlm', qh, mk) * scale
        attn = jax.nn.softmax(logits, axis=-1)
        out = jnp.einsum('bhlm,bmd->bhld', attn, mv)
        out = out.transpose(0, 2, 1, 3).reshape(b, l, d)
        return jnp.einsum('bld,ed->ble', out, Wc)

    def _L1_attn_ref(x, Wq, Wk, Wv, Wo):
        import jax, jax.numpy as jnp
        import numpy as np
        D = 256
        HS = 128
        NKV = 2

        def apply_rope(x):
            d = x.shape[-1]
            T = x.shape[-2]
            positions = jnp.arange(0, d, 2, dtype=jnp.float32)
            theta = 10000.0 ** (-2.0 * positions / d)
            angles = jnp.arange(T, dtype=jnp.float32)[:, None] * theta[None, :]
            cos, sin = (jnp.cos(angles), jnp.sin(angles))
            xr = x.reshape(x.shape[:-1] + (d // 2, 2))
            out = jnp.stack([xr[..., 0] * cos - xr[..., 1] * sin, xr[..., 1] * cos + xr[..., 0] * sin], axis=-1)
            return out.reshape(x.shape)
        B, T, _ = x.shape
        k = apply_rope(x @ Wk.T)
        v = x @ Wv.T
        q = jnp.einsum('btd,hkd->bhtk', x, Wq)
        q = apply_rope(q)
        scale = HS ** (-0.5)
        scores = jnp.einsum('bhtk,bsk->bhts', q, k) * scale
        causal = jnp.tril(jnp.ones((T, T), dtype=bool))
        scores = jnp.where(causal, scores, -jnp.inf)
        w = jax.nn.softmax(scores, axis=-1)
        out = jnp.einsum('bhts,bsk->bhtk', w, v)
        out = out.transpose(0, 2, 1, 3).reshape(B, T, NKV * HS)
        return out @ Wo.T

    def _L1_ffn_ref(x, prototypes, B, A, bias, temp):
        import jax, jax.numpy as jnp
        import numpy as np
        IN_DIM, OUT_DIM, N_PROTO, RANK = (256, 256, 32, 16)
        lead = x.shape[:-1]
        xf = x.reshape(-1, IN_DIM)
        x2 = jnp.sum(xf * xf, axis=1, keepdims=True)
        p2 = jnp.sum(prototypes * prototypes, axis=1)
        d2 = x2 + p2[None, :] - 2.0 * (xf @ prototypes.T)
        dists = jnp.sqrt(jnp.maximum(d2, 0.0))
        t = jnp.maximum(jnp.abs(temp), 0.1)
        w = jax.nn.softmax(-dists / t, axis=1)
        topw, topi = jax.lax.top_k(w, 2)
        topw = topw / jnp.sum(topw, axis=1, keepdims=True)
        out = jnp.zeros((xf.shape[0], OUT_DIM), dtype=xf.dtype)
        for tslot in range(2):
            idx = topi[:, tslot]
            wt = topw[:, tslot:tslot + 1]
            h = jnp.einsum('nri,ni->nr', B[idx], xf)
            y = jnp.einsum('nor,nr->no', A[idx], h) + bias[idx]
            out = out + wt * y
        return out.reshape(*lead, OUT_DIM)
    x = x + _L0_xattn_ref(_layernorm(x, axis=-1), ctx_1024, L0_xattn_w_sim, L0_xattn_b_sim, L0_xattn_W_qv, L0_xattn_b_qv)
    x = x + _L0_attn_ref(_layernorm(x, axis=-1), L0_attn_Wq, L0_attn_bq, L0_attn_Wk, L0_attn_bk, L0_attn_Wv, L0_attn_bv, L0_attn_Wp)
    x = x + _L0_ffn_ref(_layernorm(x, axis=-1), L0_ffn_router_w, L0_ffn_router_b, L0_ffn_sw1, L0_ffn_sb1, L0_ffn_sw2, L0_ffn_sb2, L0_ffn_rw1, L0_ffn_rb1, L0_ffn_rw2, L0_ffn_rb2)
    x = x + _L1_xattn_ref(_layernorm(x, axis=-1), ctx_1024, L1_xattn_Wq, L1_xattn_Wkv, L1_xattn_Wc)
    x = x + _L1_attn_ref(_layernorm(x, axis=-1), L1_attn_Wq, L1_attn_Wk, L1_attn_Wv, L1_attn_Wo)
    x = x + _L1_ffn_ref(_layernorm(x, axis=-1), L1_ffn_prototypes, L1_ffn_B, L1_ffn_A, L1_ffn_bias, L1_ffn_temp)
    return x

_drawn_inputs = setup_inputs


def setup_inputs(seed=0):
    import zlib

    import numpy as np

    out = dict(_drawn_inputs(seed))
    spreads = {'L0_ffn_router_b': (0.0, 0.575),
     'L0_ffn_sb1': (0.0, 0.28),
     'L0_ffn_sb2': (0.0, 0.1),
     'L0_ffn_rb1': (0.0, 0.8),
     'L0_ffn_rb2': (0.0, 0.303),
     'L1_ffn_bias': (0.0, 0.1)}
    factors = {'L0_attn_bk': 8.0,
     'L0_ffn_rw1': 2.947,
     'L0_ffn_rw2': 2.677,
     'L1_ffn_B': 4.008,
     'L1_ffn_A': 3.996}
    for name, (base, spread) in spreads.items():
        noise = np.random.default_rng([zlib.crc32(name.encode()), seed]).standard_normal(out[name].shape)
        drawn = base * np.exp(spread * noise) if base else spread * noise
        out[name] = jnp.asarray(drawn.astype(out[name].dtype))
    for name, factor in factors.items():
        out[name] = (out[name] * factor).astype(out[name].dtype)
    return out
```

```python
from contextlib import ExitStack

import numpy as np
import concourse.bass as bass
from concourse import mybir

P = 128
B, N, D = 32, 64, 256
M = 1601
TILES = B * N // P
DC = D // P
MC = -(-M // P)
MT = M - (MC - 1) * P
BANK = 512
HEADS, HD = 16, 16
H8 = P // HD
EXPERTS, HID = 8, 512
HC = HID // P
PROTOS, RANK = 32, 16
K1 = 128
F32, U32 = mybir.dt.float32, mybir.dt.uint32
ALU, ACT, AX = mybir.AluOpType, mybir.ActivationFunctionType, mybir.AxisListType
EPS = 1e-5
NEG = -1.0e30

C_ID, C_BLK, C_HEAD, C_HALF = 0, 128, 256, 264
C_COS, C_SIN, C_CAUSAL, C_ONES, C_OFFS, C_EXP, C_END = 266, 266 + 128, 266 + 256, 266 + 320, 266 + 448, 266 + 449, 266 + 451


class Signal:

    def __init__(self, sem, per=1):
        self.sem, self.per = sem, per

    def at(self, tile, k=None):
        return tile * self.per + (self.per if k is None else k)


class Chain:

    def __init__(self, eng, sem, per):
        self.eng, self.sem, self.per, self.tile, self.n = eng, sem, per, None, 0

    def begin(self, tile):
        self.tile, self.n = tile, 0

    def __call__(self, ins, before_wait=None):
        self.n += 1
        ins.then_inc(self.sem, 1)
        value = self.tile * self.per + self.n
        if before_wait:
            value = before_wait(self.eng, value)
        self.eng.wait_ge(self.sem, value)

    def end(self):
        assert self.n == self.per, self.n


def build(nc, a):
    ctx = ExitStack()
    with ctx:
        def sb(name, shape, dt=F32):
            return ctx.enter_context(nc.sbuf_tensor(name, shape, dt))

        def S(name, per=1):
            return Signal(ctx.enter_context(nc.semaphore(name)), per)

        ps = ctx.enter_context(nc.psum_tensor("ps", [P, 8, BANK], F32))
        wide = ps[:, 0:4, :].rearrange("p a b -> p (a b)")[:, 0:M]

        con = sb("con", [P, C_END])
        ident, blockmask = con[:, C_ID:C_ID + P], con[:, C_BLK:C_BLK + P]
        headmask, halfmask = con[:, C_HEAD:C_HEAD + H8], con[:, C_HALF:C_HALF + 2]
        cos, sin = con[:, C_COS:C_COS + K1], con[:, C_SIN:C_SIN + K1]
        causal, ones = con[:, C_CAUSAL:C_CAUSAL + N], con[:, C_ONES:C_ONES + P]
        offs0 = con[:, C_OFFS:C_OFFS + 1]
        minus_half, half = con[:, C_EXP:C_EXP + 1], con[:, C_EXP + 1:C_EXP + 2]
        cols = sb("cols", [P, 6 + 4 + 1 + 36 + 1])
        wsim, bqk, bsim = cols[:, 0:6], cols[:, 6:10], cols[:, 10:11]
        hbias, temp = cols[:, 11:47], cols[:, 47:48]
        rows = sb("rows", [P, 2 * D + EXPERTS])
        bqv, bv, rb = rows[:, 0:D], rows[:, D:2 * D], rows[:, 2 * D:]
        wqv = sb("wqv", [P, 4 * DC, D])
        wqkp = sb("wqkp", [P, DC, 2, D])
        wv0 = sb("wv0", [P, DC, D])
        wrout = sb("wrout", [P, DC, EXPERTS])
        sw1 = sb("sw1", [P, DC, HID])
        sw2 = sb("sw2", [P, HC, D])
        rw1 = sb("rw1", [P, DC, EXPERTS, HID])
        rw2 = sb("rw2", [P, HC, EXPERTS, D])
        ebias = sb("ebias", [EXPERTS + 1, D])
        wq1 = sb("wq1", [P, DC, D])
        wkrep = sb("wkrep", [P, DC, H8, HD])
        wv1 = sb("wv1", [P, DC, HD])
        wc1 = sb("wc1", [P, DC, D])
        wqkv = sb("wqkv", [P, DC, 4 * K1])
        wo = sb("wo", [P, 2, D])
        prot = sb("prot", [P, DC, PROTOS])
        bT = sb("bT", [P, DC, PROTOS * RANK])
        aT = sb("aT", [P, 4, D])
        pbias = sb("pbias", [PROTOS, D])
        p2 = sb("p2", [P, PROTOS])
        tneg = sb("tneg", [P, 1])
        bqkp = sb("bqkp", [P, 4])

        ctxN = sb("ctxN", [P, 2, MC, D])
        ctxT = sb("ctxT", [P, DC, 2, M])
        share = sb("share", [P, M + MC * P])
        prob, probT = share[:, 0:M], share[:, M:].rearrange("p (c n) -> p c n", c=MC)
        P0, PT0 = share[:, 0:1024], share[:, 1024:2048].rearrange("p (g n) -> p g n", g=8)
        kbd0 = share[:, 1024:3072].rearrange("p (c b h n) -> p c b h n", c=DC, b=2, h=H8)
        h1T = share[:, 0:2 * HID].rearrange("p (s c n) -> p s c n", s=2, c=HC)

        xin, xq, xp, xo = (sb(n, [P, D]) for n in ("xin", "xq", "xp", "xo"))
        h0 = sb("h0", [P, D + 1])
        tmp = sb("tmp", [P, D])
        hT = sb("hT", [P, DC, P])
        turns = sb("turns", [P, 12 * P])
        simq = turns[:, 0:DC * P].rearrange("p (c n) -> p c n", c=DC)
        feats = turns[:, 0:6 * P].rearrange("p (a d) -> p a d", a=3)
        featsT = turns[:, 6 * P:12 * P].rearrange("p (i n) -> p i n", i=6)
        hTd = turns[:, 0:4 * P].rearrange("p (c b e n) -> p c b e n", c=DC, b=2, e=2)
        qT0 = turns[:, 4 * P:6 * P].rearrange("p (c n) -> p c n", c=DC)
        kT0 = turns[:, 6 * P:8 * P].rearrange("p (c n) -> p c n", c=DC)
        vb0 = sb("vb0", [P, 2, 8, 2, HD])
        diag = sb("diag", [P, P])
        sq = sb("sq", [P, 64])
        sp_ = sb("sp", [P, 64])
        mx0, rs0 = sb("mx0", [P, HEADS]), sb("rs0", [P, HEADS])
        mx1, rs1 = sb("mx1", [P, HEADS]), sb("rs1", [P, HEADS])
        pext = sb("pext", [P, 16])
        top, topv = sb("top", [P, 8]), sb("topv", [P, 8])
        rest = sb("rest", [P, 16])
        w9 = sb("w9", [P, EXPERTS + 1])
        wT9 = diag[0:EXPERTS + 1, :]

        hp, tmp1 = sb("hp", [P, D]), sb("tmp1", [P, 2 * D])
        hTp, qpT = (sb(n, [P, DC, P]) for n in ("hTp", "qpT"))
        am, ai, gidx = sb("am", [P, 8]), sb("ai", [P, 8], U32), sb("gidx", [P, 1], U32)
        offs = sb("offs", [P, 1])
        vb1 = sb("vb1", [P, 2, 2, HD])
        P1 = sb("P1", [P, 1024])
        kbd1 = P1[:, :].rearrange("p (b h n) -> p b h n", b=2, h=H8)
        rot, vsb = P1[:, P:4 * P], P1[:, 7 * P:8 * P]
        rqT = P1[:, 4 * P:6 * P].rearrange("p (b h n) -> p b h n", b=2, h=2)
        rkT = P1[:, 6 * P:7 * P]
        PT1 = sb("PT1", [P, 8, P])
        pt1 = PT1[:, :, :].rearrange("p g n -> p (g n)")
        mem = pt1[:, 0:D]
        memT = pt1[:, D:2 * D].rearrange("p (c n) -> p c n", c=DC)
        memTd = pt1[:, 2 * D:4 * D].rearrange("p (c b e n) -> p c b e n", c=DC, b=2, e=2)
        w32 = sb("w32", [P, PROTOS])
        wf, restf = sb("wf", [P, PROTOS + 8]), sb("restf", [P, PROTOS + 8])
        topf, topvf = sb("topf", [P, 8]), sb("topvf", [P, 8])
        wT32 = sb("wT32", [PROTOS, P])
        setup = share[:, 0:2 * DC * D].rearrange("p (w c n) -> p w c n", w=2, c=DC)
        headw = share[:, 2 * DC * D:2 * DC * D + P]

        const_in, attn0_w_in, ffn0_w_in, l1_w_in = S("const_in"), S("attn0_w_in"), S("ffn0_w_in"), S("l1_w_in")
        headw_zero, headw_in = S("headw_zero"), S("headw_in")
        setup_mm, setup_done, sets_dve = S("setup_mm"), S("setup_done"), S("sets_dve")
        x_in, ctx_in = S("x_in", 16), S("ctx_in", 64)
        out_stored = S("out_stored", 16)
        x0_var, x0_rstd = S("x0_var"), S("x0_rstd")
        xa_var, xa_rstd = S("xa_var"), S("xa_rstd")
        xf_var, xf_rstd = S("xf_var"), S("xf_rstd")
        x1_var, x1_rstd = S("x1_var"), S("x1_rstd")
        xr_var, xr_rstd = S("xr_var"), S("xr_rstd")
        xg_var, xg_rstd = S("xg_var"), S("xg_rstd")
        d2_ready, root_ready = S("d2_ready"), S("root_ready")
        h0_ready, h0T_ps, h0T_ready, simq_ready = S("h0_ready"), S("h0T_ps"), S("h0T_ready"), S("simq_ready", 2)
        ctxT_ps, ctxT_act, ctxT_dve = S("ctxT_ps", 13), S("ctxT_act", 7), S("ctxT_dve", 6)
        sim_ps, sim_max, prob_ready = S("sim_ps"), S("sim_max"), S("prob_ready")
        probT_ps, probT_act, probT_dve = S("probT_ps", 4), S("probT_act", 2), S("probT_dve", 2)
        hq_ps = S("hq_ps")
        diag_ready, rowmax_ps, gmax_ready = S("diag_ready"), S("rowmax_ps"), S("gmax_ready")
        batt_ready, battw_ready, hc_ps = S("batt_ready"), S("battw_ready"), S("hc_ps")
        feats_ready, featsT_ps, featsT_act, featsT_dve = S("feats_ready"), S("featsT_ps"), S("featsT_act"), S("featsT_dve")
        xattn0_ps = S("xattn0_ps")
        ha_ready, haT_ps, haT_ready, haTd_ready = S("ha_ready"), S("haT_ps"), S("haT_ready"), S("haTd_ready", 2)
        qk_ps, v_ps, qT_ready, kT_ready = S("qk_ps"), S("v_ps"), S("qT_ready", 2), S("kT_ready", 2)
        vb0_ready, kbd0_pool, kbd0_dve = S("vb0_ready", 2), S("kbd0_pool"), S("kbd0_dve")
        s0_ps, d0_ready, e0_ready = S("s0_ps"), S("d0_ready"), S("e0_ready")
        pT0_ps, pT0_act, pT0_dve, o0_ps = S("pT0_ps", 2), S("pT0_act"), S("pT0_dve"), S("o0_ps")
        hf0_ready, hf0T_ps, hf0T_ready = S("hf0_ready"), S("hf0T_ps"), S("hf0T_ready")
        router_ps, rmax_ready, rexp_ready = S("router_ps"), S("rmax_ready"), S("rexp_ready")
        gate_ready, gateT_ps, gateT_ready = S("gate_ready"), S("gateT_ps"), S("gateT_ready")
        hid_ps, gelu_ready, eout_ps, eout_used = S("hid_ps", 9), S("gelu_ready", 9), S("eout_ps", 9), S("eout_used", 9)
        h1_ready, h1T_ps, h1T_ready = S("h1_ready"), S("h1T_ps"), S("h1T_ready")
        qp_ps, qp_ready, scores_ps, amax_done = S("qp_ps"), S("qp_ready"), S("scores_ps"), S("amax_done")
        gidx_ready, mem_in = S("gidx_ready"), S("mem_in", 16)
        memT_ps, memT_ready, memTd_ready = S("memT_ps"), S("memT_ready"), S("memTd_ready", 2)
        mkv_ps, vb1_ready, kbd1_ready = S("mkv_ps"), S("vb1_ready"), S("kbd1_ready")
        s1_ps, d1_ready, e1_ready = S("s1_ps"), S("d1_ready"), S("e1_ready")
        pT1_ps, pT1_act, pT1_dve, o1_ps = S("pT1_ps", 2), S("pT1_act"), S("pT1_dve"), S("o1_ps")
        o1_ready, o1T_ps, o1T_ready, xattn1_ps = S("o1_ready"), S("o1T_ps"), S("o1T_ready"), S("xattn1_ps")
        hr_ready, hrT_ps, hrT_ready, qkv_ps = S("hr_ready"), S("hrT_ps"), S("hrT_ready"), S("qkv_ps")
        rot_ready, v1_ready, qkT_ps, qkT_ready = S("rot_ready"), S("v1_ready"), S("qkT_ps"), S("qkT_ready", 2)
        rs_ps, rd_ready, re_ready, rp_ready = S("rs_ps"), S("rd_ready"), S("re_ready"), S("rp_ready")
        rpT_ps, rpT_ready, ro_ps, ro_act, ro_dve = S("rpT_ps"), S("rpT_ready"), S("ro_ps"), S("ro_act"), S("ro_dve")
        attn1_ps = S("attn1_ps")
        hg_ready, hgT_ps, hgT_ready, dist_ps = S("hg_ready"), S("hgT_ps"), S("hgT_ready"), S("dist_ps")
        low_ps, fs_ready, fe_ready, wt_ready = S("low_ps"), S("fs_ready"), S("fe_ready"), S("wt_ready")
        wtT_ps, wtT_ready = S("wtT_ps"), S("wtT_ready")
        low_ready, lowT_ps, lowT_ready, ffn1_ps, out_ready = S("low_ready"), S("lowT_ps"), S("lowT_ready"), S("ffn1_ps"), S("out_ready")
        q_chain, p_chain = S("q_chain", 28), S("p_chain", 30)

        ctx_rows = a["ctx_1024"]
        x_rows = a["x"].rearrange("b n d -> (b n) d")
        out_rows = a["out"].rearrange("b n d -> (b n) d")
        N_CONST, N_ATTN0, N_FFN0, N_L1 = 3, 5, 7, 10

        def chunked(ap, p=P):
            return ap.rearrange("(c p) n -> p c n", p=p)

        def settle(eng, value):
            if not isinstance(value, int):
                eng.lower_val(value)
            eng.wait_ge(const_in.sem, 16)
            return value

        def block_keys(eng, out, src):
            return eng.tensor_tensor(out, src.rearrange("p (b n) -> p b n", b=2).unsqueeze(2).to_broadcast([P, 2, H8, N]),
                                     headmask.unsqueeze(1).unsqueeze(3).to_broadcast([P, 2, H8, N]), ALU.mult)

        block = ctx.enter_context(nc.Block())

        @block.sync
        def _(sp):
            def load_ctx(u):
                for b in range(2):
                    src = ctx_rows[bass.ds(u * 2 + b, 1), :, :].rearrange("o m d -> (o m) d")
                    sp.dma_start(ctxN[:, b, 0:MC - 1, :], src[0:(MC - 1) * P, :].rearrange("(c p) d -> p c d", p=P)
                                 ).then_inc(ctx_in.sem, 16)
                    sp.dma_start(ctxN[0:MT, b, MC - 1, :], src[(MC - 1) * P:M, :]).then_inc(ctx_in.sem, 16)

            def load_x(u):
                sp.dma_start(xin[:, :], x_rows[bass.ds(u * P, P), :]).then_inc(x_in.sem, 16)

            for dst, src in ((con, a["consts"]), (cols, a["cols"]), (rows, a["rows"])):
                sp.dma_start(dst[:, :], src).then_inc(const_in.sem, 16)
            load_x(0)
            load_ctx(0)
            sp.dma_start(wqv[:, :, :], chunked(a["L0_xattn_W_qv"])).then_inc(attn0_w_in.sem, 16)
            sp.dma_start(setup[:, 0], chunked(a["wq0T"])).then_inc(attn0_w_in.sem, 16)
            sp.dma_start(setup[:, 1], chunked(a["wk0T"])).then_inc(attn0_w_in.sem, 16)
            sp.dma_start(wv0[:, :, :], chunked(a["L0_attn_Wv"])).then_inc(attn0_w_in.sem, 16)
            sp.wait_ge(headw_zero.sem, 1)
            for i in range(H8):
                sp.dma_start(headw[i * HD:(i + 1) * HD, i * HD:(i + 1) * HD], a["L0_attn_Wp"]).then_inc(headw_in.sem, 16)
            sp.dma_start(wrout[:, :, :], chunked(a["L0_ffn_router_w"])).then_inc(ffn0_w_in.sem, 16)
            sp.dma_start(ebias[:, :], a["ebias"]).then_inc(ffn0_w_in.sem, 16)
            sp.dma_start(sw1[:, :, :], chunked(a["L0_ffn_sw1"])).then_inc(ffn0_w_in.sem, 16)
            sp.dma_start(sw2[:, :, :], chunked(a["L0_ffn_sw2"])).then_inc(ffn0_w_in.sem, 16)
            for dc in range(DC):
                sp.dma_start(rw1[:, dc], a["L0_ffn_rw1"].rearrange("e (c p) h -> p c e h", p=P)[:, dc]
                             ).then_inc(ffn0_w_in.sem, 16)
            for hc in range(HC):
                sp.dma_start(rw2[:, hc], a["L0_ffn_rw2"].rearrange("e (c p) d -> p c e d", p=P)[:, hc]
                             ).then_inc(ffn0_w_in.sem, 16)
            sp.dma_start(wq1[:, :, :], chunked(a["wq1T"])).then_inc(l1_w_in.sem, 16)
            for i in range(H8):
                sp.dma_start(wkrep[:, :, i, :], chunked(a["wkv1T"])[:, :, 0:HD]).then_inc(l1_w_in.sem, 16)
            sp.dma_start(wv1[:, :, :], chunked(a["wkv1T"])[:, :, HD:2 * HD]).then_inc(l1_w_in.sem, 16)
            sp.dma_start(wc1[:, :, :], chunked(a["wc1T"])).then_inc(l1_w_in.sem, 16)
            sp.dma_start(wqkv[:, :, :], chunked(a["wqkvT"])).then_inc(l1_w_in.sem, 16)
            sp.dma_start(wo[:, :, :], chunked(a["woT"])).then_inc(l1_w_in.sem, 16)
            sp.dma_start(prot[:, :, :], chunked(a["protT"])).then_inc(l1_w_in.sem, 16)
            sp.dma_start(bT[:, :, :], chunked(a["bT"])).then_inc(l1_w_in.sem, 16)
            sp.dma_start(aT[:, :, :], chunked(a["aT"])).then_inc(l1_w_in.sem, 16)
            sp.dma_start(pbias[:, :], a["L1_ffn_bias"]).then_inc(l1_w_in.sem, 16)

            def prefetch(u):
                sp.wait_ge(hq_ps.sem, hq_ps.at(u - 1))
                load_ctx(u)
                sp.wait_ge(ha_ready.sem, ha_ready.at(u - 1))
                load_x(u)

            def store(t):
                sp.wait_ge(out_ready.sem, out_ready.at(t))
                sp.dma_start(out_rows[bass.ds(t * P, P), :], xo[:, :]).then_inc(out_stored.sem, 16)

            prefetch(1)
            with sp.Fori(0, TILES - 2) as t:
                store(t)
                prefetch(t + 2)
            store(TILES - 2)
            store(TILES - 1)
            sp.wait_ge(out_stored.sem, out_stored.at(TILES - 1))

        @block.tensor
        def _(pe):
            def wait(sig, tile, k=None):
                pe.wait_ge(sig.sem, sig.at(tile, k))

            def transposes(bank, src, n, sig, width=P, col=0):
                for i in range(n):
                    last = nc.tensor.transpose(ps[0:width, bank, col + i * P:col + (i + 1) * P],
                                               src[:, i * width:(i + 1) * width], ident)
                last.then_inc(sig.sem, 1)

            def setup_weights():
                pe.wait_ge(const_in.sem, 16 * N_CONST)
                pe.wait_ge(attn0_w_in.sem, 16 * 4)
                pe.wait_ge(headw_in.sem, 16 * H8)
                for w in range(2):
                    for dc in range(DC):
                        for c in range(DC):
                            last = nc.tensor.matmul(ps[:, w, dc * D + c * P:dc * D + (c + 1) * P],
                                                    setup[:, w, c, dc * P:(dc + 1) * P], headw, start=True, stop=True)
                for k in range(4):
                    last = nc.tensor.matmul(ps[:, 2, k:k + 1], headw, bqk[:, k:k + 1], start=True, stop=True)
                last.then_inc(setup_mm.sem, 1)

            def setup_protos():
                pe.wait_ge(sets_dve.sem, 3)
                for dc in range(DC):
                    last = nc.tensor.matmul(ps[:, 3, 0:PROTOS], ones, tmp1[:, dc * PROTOS:(dc + 1) * PROTOS],
                                            start=(dc == 0), stop=(dc == DC - 1))
                last.then_inc(setup_mm.sem, 1)
                pe.wait_ge(sets_dve.sem, 4)

            def ctx_transposes(u):
                wait(ctx_in, u)
                wait(simq_ready, u)
                wait(h0T_ready, u)
                n = 0
                for b in range(2):
                    for dc in range(DC):
                        for g in range(3):
                            if n >= 2:
                                wait(ctxT_act if n % 2 == 0 else ctxT_dve, u, (n - 2) // 2 + 1)
                            for i in range(4):
                                last = nc.tensor.transpose(ps[:, 4 + n % 2, i * P:(i + 1) * P],
                                                           ctxN[:, b, 4 * g + i, dc * P:(dc + 1) * P], ident)
                            last.then_inc(ctxT_ps.sem, 1)
                            n += 1
                wait(ctxT_act, u, 6)
                for dc in range(DC):
                    for b in range(2):
                        i = dc * 2 + b
                        last = nc.tensor.transpose(ps[:, 4, i * MT:(i + 1) * MT],
                                                   ctxN[0:MT, b, MC - 1, dc * P:(dc + 1) * P], ident[0:MT, 0:MT])
                last.then_inc(ctxT_ps.sem, 1)

            def wide_scores(q):
                for k in range(4):
                    n = min(BANK, M - k * BANK)
                    for dc in range(DC):
                        for b in range(2):
                            last = nc.tensor.matmul(ps[b * N:(b + 1) * N, k, 0:n], q[:, dc, b * N:(b + 1) * N],
                                                    ctxT[:, dc, b, k * BANK:k * BANK + n],
                                                    start=(dc == 0), stop=(dc == DC - 1))
                return last

            def core_scores(qT, kbd, shared, bank, sig):
                for c in range(DC):
                    for b in range(2):
                        k = kbd[:, b] if shared else kbd[:, c, b]
                        last = nc.tensor.matmul(ps[b * N:(b + 1) * N, bank + c, :], qT[:, c, b * N:(b + 1) * N],
                                                k, start=True, stop=True)
                last.then_inc(sig.sem, 1)

            def core_transposes(src, bank, sig):
                for half in range(2):
                    transposes(bank + half, src[:, half * BANK:(half + 1) * BANK], 4, sig)

            def core_values(PT, vb, shared, bank, sig):
                for g in range(8):
                    for b in range(2):
                        v = vb[:, b] if shared else vb[:, b, g]
                        last = nc.tensor.matmul(ps[b * N:(b + 1) * N, bank, g * 32:(g + 1) * 32],
                                                PT[:, g, b * N:(b + 1) * N], v, start=True, stop=True)
                last.then_inc(sig.sem, 1)

            def q_norm(u):
                wait(h0_ready, u)
                transposes(4, h0[:, 0:D], 2, h0T_ps)

            def q_sim(u, first):
                wait(ctxT_act, u)
                wait(ctxT_dve, u)
                if not first:
                    wait(amax_done, u - 1)
                wide_scores(simq)
                for dc in range(DC):
                    last = nc.tensor.matmul(ps[:, 4, 0:1], hT[:, dc, :], wsim[:, dc:dc + 1],
                                            start=(dc == 0), stop=(dc == DC - 1))
                last.then_inc(sim_ps.sem, 1)

            def q_batt_max(u):
                wait(diag_ready, u)
                nc.tensor.matmul(ps[:, 5, 0:P], ones, diag[:, :], start=True, stop=True).then_inc(rowmax_ps.sem, 1)

            def q_batt_sum(u):
                wait(battw_ready, u)
                nc.tensor.matmul(ps[:, 5, 0:D + 1], diag[:, :], h0[:, :], start=True, stop=True).then_inc(hc_ps.sem, 1)

            def q_probT(u):
                wait(prob_ready, u)
                for n in range(4):
                    if n >= 2:
                        wait(probT_act if n % 2 == 0 else probT_dve, u, 1)
                    bank = 2 + n % 2
                    if n < 3:
                        transposes(bank, prob[:, n * BANK:(n + 1) * BANK], 4, probT_ps)
                    else:
                        nc.tensor.transpose(ps[0:MT, bank, 0:P], prob[:, n * BANK:M], ident).then_inc(probT_ps.sem, 1)

            def q_hq(u):
                wait(probT_act, u)
                wait(probT_dve, u)
                for c in range(MC):
                    r = P if c < MC - 1 else MT
                    for b in range(2):
                        last = nc.tensor.matmul(ps[b * N:(b + 1) * N, 0, 0:D], probT[0:r, c, b * N:(b + 1) * N],
                                                ctxN[0:r, b, c, :], start=(c == 0), stop=(c == MC - 1))
                last.then_inc(hq_ps.sem, 1)

            def q_feats(u):
                wait(feats_ready, u)
                f = feats[:, :, :].rearrange("p a b -> p (a b)")
                for i in range(6):
                    last = nc.tensor.transpose(ps[:, 2 + i // 4, (i % 4) * P:(i % 4 + 1) * P], f[:, i * P:(i + 1) * P], ident)
                last.then_inc(featsT_ps.sem, 1)
                wait(featsT_act, u)
                wait(featsT_dve, u)
                for i in range(8):
                    src = hT[:, i] if i < 2 else featsT[:, i - 2]
                    last = nc.tensor.matmul(ps[:, 1, 0:D], src, wqv[:, i, :], start=(i == 0), stop=(i == 7))
                last.then_inc(xattn0_ps.sem, 1)

            def q_attn_proj(u):
                wait(ha_ready, u)
                transposes(4, h0[:, 0:D], 2, haT_ps)
                wait(haT_ready, u)
                for w in range(2):
                    for c in range(DC):
                        for dc in range(DC):
                            last = nc.tensor.matmul(ps[:, 5, (2 * w + c) * P:(2 * w + c + 1) * P],
                                                    wqkp[:, dc, w, c * P:(c + 1) * P], hT[:, dc, :],
                                                    start=(dc == 0), stop=(dc == DC - 1))
                last.then_inc(qk_ps.sem, 1)
                wait(haTd_ready, u)
                for b in range(2):
                    for dc in range(DC):
                        last = nc.tensor.matmul(ps[:, 4, b * D:(b + 1) * D], hTd[:, dc, b], wv0[:, dc, :],
                                                start=(dc == 0), stop=(dc == DC - 1))
                last.then_inc(v_ps.sem, 1)

            def q_attn_scores(u):
                wait(qT_ready, u)
                wait(kbd0_pool, u)
                wait(kbd0_dve, u)
                core_scores(qT0, kbd0, False, 0, s0_ps)

            def q_attn_out(u):
                wait(e0_ready, u)
                core_transposes(P0, 2, pT0_ps)
                wait(pT0_act, u)
                wait(pT0_dve, u)
                wait(vb0_ready, u)
                core_values(PT0, vb0, False, 4, o0_ps)

            def q_experts(u):
                wait(hf0_ready, u)
                transposes(4, h0[:, 0:D], 2, hf0T_ps)
                wait(hf0T_ready, u)
                for dc in range(DC):
                    last = nc.tensor.matmul(ps[:, 5, 0:EXPERTS], hT[:, dc, :], wrout[:, dc, :],
                                            start=(dc == 0), stop=(dc == DC - 1))
                last.then_inc(router_ps.sem, 1)

                def hidden(n):
                    if n >= 2:
                        wait(gelu_ready, u, n - 1)
                    for hc in range(HC):
                        for dc in range(DC):
                            w = sw1[:, dc, hc * P:(hc + 1) * P] if n == 0 else rw1[:, dc, n - 1, hc * P:(hc + 1) * P]
                            last = nc.tensor.matmul(ps[:, n % 2, hc * P:(hc + 1) * P], w, hT[:, dc, :],
                                                    start=(dc == 0), stop=(dc == DC - 1))
                    last.then_inc(hid_ps.sem, 1)

                def output(n):
                    if n >= 2:
                        wait(eout_used, u, n - 1)
                    wait(gelu_ready, u, n + 1)
                    if n == 0:
                        wait(gateT_ready, u)
                        nc.tensor.matmul(ps[:, 2, 0:D], wT9, ebias[:, :], start=True, stop=False)
                    for hc in range(HC):
                        w = sw2[:, hc, :] if n == 0 else rw2[:, hc, n - 1, :]
                        last = nc.tensor.matmul(ps[:, 2 + n % 2, 0:D], h1T[:, n % 2, hc, :], w,
                                                start=(hc == 0 and n > 0), stop=(hc == HC - 1))
                    last.then_inc(eout_ps.sem, 1)

                hidden(0)
                hidden(1)
                wait(gate_ready, u)
                nc.tensor.transpose(ps[0:EXPERTS + 1, 5, 0:P], w9[:, :], ident).then_inc(gateT_ps.sem, 1)
                for n in range(9):
                    output(n)
                    if n + 2 < 9:
                        hidden(n + 2)

            def p_scores(t):
                wait(h1_ready, t)
                transposes(6, hp, 2, h1T_ps)
                wait(h1T_ready, t)
                for c in range(DC):
                    for dc in range(DC):
                        last = nc.tensor.matmul(ps[:, 7, c * P:(c + 1) * P], wq1[:, dc, c * P:(c + 1) * P],
                                                hTp[:, dc, :], start=(dc == 0), stop=(dc == DC - 1))
                last.then_inc(qp_ps.sem, 1)
                wait(qp_ready, t)
                wide_scores(qpT).then_inc(scores_ps.sem, 1)

            def p_mem(t):
                wait(mem_in, t)
                transposes(6, mem, 2, memT_ps)
                wait(memT_ready, t)
                wait(memTd_ready, t)
                for dc in range(DC):
                    nc.tensor.matmul(ps[:, 7, 0:P], wkrep[:, dc], memT[:, dc, :],
                                     start=(dc == 0), stop=(dc == DC - 1))
                for b in range(2):
                    for dc in range(DC):
                        last = nc.tensor.matmul(ps[:, 7, P + b * HD:P + (b + 1) * HD], memTd[:, dc, b], wv1[:, dc, :],
                                                start=(dc == 0), stop=(dc == DC - 1))
                last.then_inc(mkv_ps.sem, 1)

            def p_xattn_scores(t):
                wait(kbd1_ready, t)
                wait(vb1_ready, t)
                core_scores(qpT, kbd1, True, 6, s1_ps)

            def p_xattn_out(t):
                wait(e1_ready, t)
                core_transposes(P1, 6, pT1_ps)
                wait(pT1_act, t)
                wait(pT1_dve, t)
                core_values(PT1, vb1, True, 6, o1_ps)

            def p_xattn_proj(t):
                wait(o1_ready, t)
                transposes(7, hp, 2, o1T_ps)
                wait(o1T_ready, t)
                for dc in range(DC):
                    last = nc.tensor.matmul(ps[:, 6, 0:D], hTp[:, dc, :], wc1[:, dc, :],
                                            start=(dc == 0), stop=(dc == DC - 1))
                last.then_inc(xattn1_ps.sem, 1)

            def p_rot_proj(t):
                wait(hr_ready, t)
                transposes(7, hp, 2, hrT_ps)
                wait(hrT_ready, t)
                for dc in range(DC):
                    last = nc.tensor.matmul(ps[:, 6, :], hTp[:, dc, :], wqkv[:, dc, :],
                                            start=(dc == 0), stop=(dc == DC - 1))
                last.then_inc(qkv_ps.sem, 1)

            def p_rot_scores(t):
                wait(rot_ready, t)
                transposes(7, rot, 3, qkT_ps)
                wait(qkT_ready, t)
                wait(v1_ready, t)
                for b in range(2):
                    last = nc.tensor.matmul(ps[:, 6, b * N:(b + 1) * N], rqT[:, b].rearrange("p h n -> p (h n)"),
                                            rkT[:, b * N:(b + 1) * N], start=True, stop=True)
                last.then_inc(rs_ps.sem, 1)

            def p_rot_out(t):
                wait(rp_ready, t)
                nc.tensor.transpose(ps[:, 7, 0:P], P1[:, 0:P], ident).then_inc(rpT_ps.sem, 1)
                wait(rpT_ready, t)
                for b in range(2):
                    last = nc.tensor.matmul(ps[:, 6 + b, 0:P], vsb[b * N:(b + 1) * N, :],
                                            PT1[b * N:(b + 1) * N, 0, :], start=True, stop=True)
                last.then_inc(ro_ps.sem, 1)
                wait(ro_act, t)
                wait(ro_dve, t)
                for h in range(2):
                    last = nc.tensor.matmul(ps[:, 6, 0:D], PT1[:, 1 + h, :], wo[:, h, :], start=(h == 0), stop=(h == 1))
                last.then_inc(attn1_ps.sem, 1)

            def p_proto(t):
                wait(hg_ready, t)
                transposes(7, hp, 2, hgT_ps)
                wait(hgT_ready, t)
                for dc in range(DC):
                    last = nc.tensor.matmul(ps[:, 7, 2 * P:2 * P + PROTOS], hTp[:, dc, :], prot[:, dc, :],
                                            start=(dc == 0), stop=(dc == DC - 1))
                last.then_inc(dist_ps.sem, 1)
                for dc in range(DC):
                    last = nc.tensor.matmul(ps[:, 6, :], hTp[:, dc, :], bT[:, dc, :],
                                            start=(dc == 0), stop=(dc == DC - 1))
                last.then_inc(low_ps.sem, 1)

            def p_proto_out(t):
                wait(wt_ready, t)
                nc.tensor.transpose(ps[0:PROTOS, 7, 0:P], w32[:, :], ident).then_inc(wtT_ps.sem, 1)
                wait(wtT_ready, t)
                wait(low_ready, t)
                transposes(7, tmp1, 4, lowT_ps)
                wait(lowT_ready, t)
                nc.tensor.matmul(ps[:, 6, 0:D], wT32[:, :], pbias[:, :], start=True, stop=False)
                for c in range(4):
                    last = nc.tensor.matmul(ps[:, 6, 0:D], PT1[:, c, :], aT[:, c, :], start=False, stop=(c == 3))
                last.then_inc(ffn1_ps.sem, 1)

            def layer0(u, first=False):
                q_norm(u)
                ctx_transposes(u)
                q_sim(u, first)
                q_batt_max(u)
                q_probT(u)
                q_batt_sum(u)
                q_hq(u)
                q_feats(u)
                q_attn_proj(u)
                q_attn_scores(u)
                q_attn_out(u)

            def layer1(t):
                p_mem(t)
                p_xattn_scores(t)
                p_xattn_out(t)
                p_xattn_proj(t)
                p_rot_proj(t)
                p_rot_scores(t)
                p_rot_out(t)
                p_proto(t)
                p_proto_out(t)

            setup_weights()
            setup_protos()
            layer0(0, True)
            pe.wait_ge(ffn0_w_in.sem, 16 * 10)
            q_experts(0)
            pe.wait_ge(l1_w_in.sem, 16 * 17)
            with pe.Fori(0, TILES - 1) as t:
                p_scores(t)
                layer1(t)
                layer0(t + 1)
                q_experts(t + 1)
            p_scores(TILES - 1)
            layer1(TILES - 1)

        @block.scalar
        def _(act):
            def wait(sig, tile, k=None):
                act.wait_ge(sig.sem, sig.at(tile, k))

            def copy(out, in_, sig):
                nc.scalar.copy(out, in_).then_inc(sig.sem, 1)

            def halves(bank):
                return ps[:, bank, 0:2 * P].rearrange("p (c n) -> p c n", c=2)

            def q_norm(u):
                wait(h0T_ps, u)
                copy(hT[:, :, :], halves(4), h0T_ready)

            def ctx_copies(u):
                n = 0
                for b in range(2):
                    for dc in range(DC):
                        for g in range(3):
                            if n % 2 == 0:
                                wait(ctxT_ps, u, n + 1)
                                copy(ctxT[:, dc, b, g * BANK:(g + 1) * BANK], ps[:, 4, :], ctxT_act)
                            n += 1
                wait(ctxT_ps, u, 13)
                copy(ctxT[:, :, :, (MC - 1) * P:M], ps[:, 4, 0:4 * MT].rearrange("p (c b n) -> p c b n", c=2, b=2), ctxT_act)

            def q_exp(u):
                wait(sim_max, u)
                nc.scalar.activation(prob, wide, ACT.Exp, bias=sq[:, 4:5], accum_out=sq[:, 5:6]).then_inc(prob_ready.sem, 1)

            def q_batt(u):
                wait(gmax_ready, u)
                nc.scalar.activation(sq[:, 8:9], sq[:, 6:7], ACT.Exp, bias=sq[:, 7:8]).then_inc(batt_ready.sem, 1)

            def q_probT(u):
                for n in (0, 2):
                    wait(probT_ps, u, n + 1)
                    copy(probT[:, 4 * n:4 * n + 4, :], ps[:, 2, :].rearrange("p (c n) -> p c n", c=4), probT_act)

            def q_feats(u):
                wait(featsT_ps, u)
                copy(featsT[:, 0:4, :], ps[:, 2, :].rearrange("p (c n) -> p c n", c=4), featsT_act)

            def q_attn_proj(u):
                wait(haT_ps, u)
                copy(hT[:, :, :], halves(4), haT_ready)
                wait(qk_ps, u)
                for c in range(DC):
                    nc.scalar.activation(kT0[:, c, :], ps[:, 5, (2 + c) * P:(3 + c) * P], ACT.Identity,
                                         bias=bqkp[:, 2 + c:3 + c]).then_inc(kT_ready.sem, 1)
                for c in range(DC):
                    nc.scalar.activation(qT0[:, c, :], ps[:, 5, c * P:(c + 1) * P], ACT.Identity,
                                         bias=bqkp[:, c:c + 1]).then_inc(qT_ready.sem, 1)

            def q_attn(u):
                wait(d0_ready, u)
                nc.scalar.activation(P0, P0, ACT.Exp, scale=HD ** -0.5).then_inc(e0_ready.sem, 1)
                wait(pT0_ps, u, 1)
                copy(PT0[:, 0:4, :], ps[:, 2, :].rearrange("p (c n) -> p c n", c=4), pT0_act)

            def q_experts(u):
                wait(hf0T_ps, u)
                copy(hT[:, :, :], halves(4), hf0T_ready)
                wait(rmax_ready, u)
                nc.scalar.activation(sq[:, 16:24], sq[:, 24:32], ACT.Exp, bias=sq[:, 4:5],
                                     accum_out=sq[:, 5:6]).then_inc(rexp_ready.sem, 1)
                for n in range(9):
                    wait(hid_ps, u, n + 1)
                    if n >= 2:
                        wait(eout_ps, u, n - 1)
                    for hc in range(HC):
                        k = n * HC + hc
                        last = nc.scalar.activation(h1T[:, n % 2, hc, :], ps[:, n % 2, hc * P:(hc + 1) * P], ACT.Gelu,
                                                    bias=hbias[:, k:k + 1])
                    last.then_inc(gelu_ready.sem, 1)

            def p_scores(t):
                wait(h1T_ps, t)
                copy(hTp[:, :, :], halves(6), h1T_ready)
                wait(qp_ps, t)
                copy(qpT[:, :, :], halves(7), qp_ready)

            def p_mem(t):
                wait(memT_ps, t)
                copy(memT[:, :, :], halves(6), memT_ready)

            def p_xattn(t):
                wait(d1_ready, t)
                nc.scalar.activation(P1[:, :], P1[:, :], ACT.Exp, scale=HD ** -0.5).then_inc(e1_ready.sem, 1)
                wait(pT1_ps, t, 1)
                copy(PT1[:, 0:4, :], ps[:, 6, :].rearrange("p (c n) -> p c n", c=4), pT1_act)
                wait(o1T_ps, t)
                copy(hTp[:, :, :], halves(7), o1T_ready)

            def p_rot(t):
                wait(hrT_ps, t)
                copy(hTp[:, :, :], halves(7), hrT_ready)
                wait(rot_ready, t)
                copy(vsb[:, :], ps[:, 6, 384:512], v1_ready)
                wait(qkT_ps, t)
                copy(rqT, ps[:, 7, 0:2 * P].rearrange("p (h b n) -> p b h n", h=2, b=2), qkT_ready)
                copy(rkT, ps[:, 7, 2 * P:3 * P], qkT_ready)
                wait(rd_ready, t)
                nc.scalar.activation(P1[:, 0:P], P1[:, 0:P], ACT.Exp, scale=K1 ** -0.5).then_inc(re_ready.sem, 1)
                wait(rpT_ps, t)
                copy(PT1[:, 0, :], ps[:, 7, 0:P], rpT_ready)
                wait(ro_ps, t)
                copy(PT1[:, 1:3, 0:N], ps[:, 6, 0:P].rearrange("p (h n) -> p h n", h=2), ro_act)

            def p_proto(t):
                wait(hgT_ps, t)
                copy(hTp[:, :, :], halves(7), hgT_ready)
                wait(fs_ready, t)
                nc.scalar.activation(w32[:, :], sp_[:, 0:PROTOS], ACT.Exp, bias=sp_[:, 40:41],
                                     accum_out=sp_[:, 41:42]).then_inc(fe_ready.sem, 1)
                wait(wtT_ps, t)
                copy(wT32[:, :], ps[0:PROTOS, 7, 0:P], wtT_ready)
                wait(lowT_ps, t)
                copy(PT1[:, 0:4, :], ps[:, 7, :].rearrange("p (c n) -> p c n", c=4), lowT_ready)

            def layer0(u):
                q_norm(u)
                ctx_copies(u)
                q_exp(u)
                q_batt(u)
                q_probT(u)
                q_feats(u)
                q_attn_proj(u)
                q_attn(u)

            def layer1(t):
                p_mem(t)
                p_xattn(t)
                p_rot(t)
                p_proto(t)

            act.wait_ge(const_in.sem, 16 * N_CONST)
            act.wait_ge(setup_done.sem, 1)
            layer0(0)
            q_experts(0)
            with act.Fori(0, TILES - 1) as t:
                p_scores(t)
                layer1(t)
                layer0(t + 1)
                q_experts(t + 1)
            p_scores(TILES - 1)
            layer1(TILES - 1)

        @block.vector
        def _(dve):
            v = nc.vector
            ql = Chain(dve, q_chain.sem, q_chain.per)
            pl = Chain(dve, p_chain.sem, p_chain.per)

            def wait(sig, tile, k=None):
                dve.wait_ge(sig.sem, sig.at(tile, k))

            def sync(ins, sig, tile, k=None):
                ins.then_inc(sig.sem, 1)
                wait(sig, tile, k)

            def layernorm(link, tile, col, x, h, var_sig, rstd_sig):
                link(v.bn_stats(col[:, 50:56], x), settle)
                link(v.bn_aggr(col[:, 56:58], col[:, 50:56]))
                v.tensor_scalar(col[:, 57:58], col[:, 57:58], EPS, None, ALU.add).then_inc(var_sig.sem, 1)
                wait(rstd_sig, tile)
                return v.tensor_scalar(h, x, col[:, 56:57], col[:, 58:59], ALU.subtract, ALU.mult)

            def heads(ap):
                return ap.rearrange("p (h m) -> p h m", h=HEADS)

            def each_head(col, n):
                return col[:, :].unsqueeze(2).to_broadcast([P, HEADS, n])

            def q_norm(u):
                ql.begin(u)
                wait(x_in, u)
                layernorm(ql, u, sq, xin[:, :], h0[:, 0:D], x0_var, x0_rstd).then_inc(h0_ready.sem, 1)
                wait(h0T_ready, u)
                for dc in range(DC):
                    v.tensor_scalar(simq[:, dc, :], hT[:, dc, :], wsim[:, 4 + dc:5 + dc],
                                    wsim[:, 2 + dc:3 + dc], ALU.mult, ALU.add).then_inc(simq_ready.sem, 1)

            def ctx_copies(u):
                n = 0
                for b in range(2):
                    for dc in range(DC):
                        for g in range(3):
                            if n % 2 == 1:
                                wait(ctxT_ps, u, n + 1)
                                v.tensor_copy(ctxT[:, dc, b, g * BANK:(g + 1) * BANK], ps[:, 5, :]).then_inc(ctxT_dve.sem, 1)
                            n += 1

            def q_sim(u):
                wait(sim_ps, u)
                ql(v.reduce_max(sq[:, 3:4], wide, AX.X))
                v.tensor_scalar(sq[:, 4:5], sq[:, 3:4], -1.0, None, ALU.mult).then_inc(sim_max.sem, 1)
                ql(v.tensor_scalar(sq[:, 6:7], ps[:, 4, 0:1], sq[:, 3:4], bsim, ALU.add, ALU.add))
                v.tensor_scalar(diag[:, :], ident, sq[:, 6:7], None, ALU.mult).then_inc(diag_ready.sem, 1)
                wait(rowmax_ps, u)
                for b in range(2):
                    i = slice(b * N, (b + 1) * N)
                    ql(v.reduce_max(sq[i, 9:10], ps[i, 5, b * N:(b + 1) * N], AX.X))
                v.tensor_scalar(sq[:, 7:8], sq[:, 9:10], -1.0, None, ALU.mult).then_inc(gmax_ready.sem, 1)
                wait(batt_ready, u)
                v.tensor_scalar(diag[:, :], blockmask, sq[:, 8:9], None, ALU.mult).then_inc(battw_ready.sem, 1)

            def q_probT(u):
                wait(probT_ps, u, 2)
                v.tensor_copy(probT[:, 4:8, :], ps[:, 3, :].rearrange("p (c n) -> p c n", c=4)).then_inc(probT_dve.sem, 1)
                wait(probT_ps, u, 4)
                v.tensor_copy(probT[0:MT, MC - 1, :], ps[0:MT, 3, 0:P]).then_inc(probT_dve.sem, 1)

            def q_feats(u):
                wait(hc_ps, u)
                ql(v.reciprocal(sq[:, 10:11], ps[:, 5, D:D + 1]))
                v.scalar_tensor_tensor(feats[:, 2, :], ps[:, 5, 0:D], sq[:, 10:11], h0[:, 0:D], ALU.mult, ALU.mult)
                wait(prob_ready, u)
                ql(v.reciprocal(sq[:, 11:12], sq[:, 5:6]))
                wait(hq_ps, u)
                ql(v.tensor_scalar(feats[:, 0, :], ps[:, 0, 0:D], sq[:, 11:12], None, ALU.mult))
                v.tensor_tensor(feats[:, 1, :], feats[:, 0, :], h0[:, 0:D], ALU.mult).then_inc(feats_ready.sem, 1)
                wait(featsT_ps, u)
                v.tensor_copy(featsT[:, 4:6, :], ps[:, 3, 0:2 * P].rearrange("p (c n) -> p c n", c=2)).then_inc(featsT_dve.sem, 1)
                wait(xattn0_ps, u)
                ql(v.tensor_tensor(tmp[:, :], ps[:, 1, 0:D], bqv, ALU.add))
                ql(v.tensor_tensor(xq[:, :], tmp[:, :], xin[:, :], ALU.add))

            def q_attn_proj(u):
                layernorm(ql, u, sq, xq[:, :], h0[:, 0:D], xa_var, xa_rstd).then_inc(ha_ready.sem, 1)
                wait(haT_ready, u)
                for dc in range(DC):
                    src = hT[:, dc, :].rearrange("p (b n) -> p b n", b=2)
                    v.tensor_copy(hTd[:, dc], src.unsqueeze(2).to_broadcast([P, 2, 2, N])).then_inc(haTd_ready.sem, 1)
                wait(v_ps, u)
                for b in range(2):
                    src = ps[:, 4, b * D:(b + 1) * D].rearrange("p (g h e) -> p g h e", g=8, h=2)
                    v.tensor_tensor(vb0[:, b], src, halfmask.unsqueeze(1).unsqueeze(3).to_broadcast([P, 8, 2, HD]),
                                    ALU.mult).then_inc(vb0_ready.sem, 1)
                wait(kT_ready, u)
                block_keys(v, kbd0[:, 1], kT0[:, 1, :]).then_inc(kbd0_dve.sem, 1)

            def core_softmax(link, tile, s_sig, bank, mx, prb, d_sig, e_sig, rs):
                wait(s_sig, tile)
                sc = ps[:, bank:bank + 2, :].rearrange("p c (h m) -> p (c h) m", m=N)
                link(v.tensor_reduce(mx[:, :], sc, AX.X, ALU.max))
                v.tensor_tensor(heads(prb), sc, each_head(mx, N), ALU.subtract).then_inc(d_sig.sem, 1)
                wait(e_sig, tile)
                link(v.tensor_reduce(rs[:, :], heads(prb), AX.X, ALU.add))
                link(v.reciprocal(rs[:, :], rs[:, :]))

            def q_attn(u):
                core_softmax(ql, u, s0_ps, 0, mx0, P0, d0_ready, e0_ready, rs0)
                wait(pT0_ps, u, 2)
                v.tensor_copy(PT0[:, 4:8, :], ps[:, 3, :].rearrange("p (c n) -> p c n", c=4)).then_inc(pT0_dve.sem, 1)
                wait(o0_ps, u)
                ql(v.tensor_tensor(heads(tmp[:, :]), heads(ps[:, 4, 0:D]), each_head(rs0, HD), ALU.mult))
                ql(v.tensor_tensor(tmp[:, :], tmp[:, :], bv, ALU.add))
                ql(v.tensor_tensor(xq[:, :], xq[:, :], tmp[:, :], ALU.add))

            def top_two(link, values, ext, tp, tv, rst, n):
                link(v.max(tp[:, :], values))
                link(v.tensor_copy(tv[:, 0:2], tp[:, 0:2]), settle)
                link(v.match_replace(rst[:, :], tv[:, :], ext[:, :], 0.0))

            def q_experts(u):
                layernorm(ql, u, sq, xq[:, :], h0[:, 0:D], xf_var, xf_rstd).then_inc(hf0_ready.sem, 1)
                wait(router_ps, u)
                ql(v.tensor_tensor(sq[:, 24:32], ps[:, 5, 0:EXPERTS], rb, ALU.add))
                ql(v.reduce_max(sq[:, 3:4], sq[:, 24:32], AX.X))
                v.tensor_scalar(sq[:, 4:5], sq[:, 3:4], -1.0, None, ALU.mult).then_inc(rmax_ready.sem, 1)
                wait(rexp_ready, u)
                ql(v.reciprocal(sq[:, 10:11], sq[:, 5:6]))
                ql(v.tensor_scalar(pext[:, 0:8], sq[:, 16:24], sq[:, 10:11], None, ALU.mult), settle)
                top_two(ql, pext[:, 0:8], pext, top, topv, rest, EXPERTS)
                sync(v.tensor_tensor(w9[:, 0:8], pext[:, 0:8], rest[:, 0:8], ALU.subtract), gate_ready, u)
                wait(gateT_ps, u)
                v.tensor_copy(wT9, ps[0:EXPERTS + 1, 5, 0:P]).then_inc(gateT_ready.sem, 1)
                for n in range(9):
                    wait(eout_ps, u, n + 1)
                    dst = xp if n == 8 else xq
                    bank = ps[:, 2 + n % 2, 0:D]
                    if n == 0:
                        ins = v.tensor_tensor(dst[:, :], bank, xq[:, :], ALU.add)
                    else:
                        ins = v.scalar_tensor_tensor(dst[:, :], bank, w9[:, n - 1:n], xq[:, :], ALU.mult, ALU.add)
                    sync(ins, eout_used, u, n + 1)
                ql.end()

            def p_scores(t):
                pl.begin(t)
                layernorm(pl, t, sp_, xp[:, :], hp[:, :], x1_var, x1_rstd).then_inc(h1_ready.sem, 1)
                dve.wait_ge(scores_ps.sem, settle(dve, scores_ps.at(t)))
                pl(v.max(am[:, :], wide), settle)
                sync(v.max_index(ai[:, :], am[:, :], wide), amax_done, t)
                v.tensor_scalar(gidx[:, :], ai[:, 0:1], offs[:, 0:1], None, ALU.add).then_inc(gidx_ready.sem, 1)

            def p_mem(t):
                wait(gidx_ready, t)
                pl(v.tensor_scalar(offs[:, :], offs[:, :], float(2 * M), None, ALU.add))
                wait(memT_ready, t)
                for dc in range(DC):
                    src = memT[:, dc, :].rearrange("p (b n) -> p b n", b=2)
                    v.tensor_copy(memTd[:, dc], src.unsqueeze(2).to_broadcast([P, 2, 2, N])).then_inc(memTd_ready.sem, 1)
                wait(mkv_ps, t)
                src = ps[:, 7, P:P + 2 * HD].rearrange("p (b e) -> p b e", b=2)
                v.tensor_tensor(vb1[:, :, :, :], src.unsqueeze(2).to_broadcast([P, 2, 2, HD]),
                                halfmask.unsqueeze(1).unsqueeze(3).to_broadcast([P, 2, 2, HD]), ALU.mult
                                ).then_inc(vb1_ready.sem, 1)
                block_keys(v, kbd1, ps[:, 7, 0:P]).then_inc(kbd1_ready.sem, 1)

            def p_xattn(t):
                core_softmax(pl, t, s1_ps, 6, mx1, P1[:, :], d1_ready, e1_ready, rs1)
                wait(pT1_ps, t, 2)
                v.tensor_copy(PT1[:, 4:8, :], ps[:, 7, :].rearrange("p (c n) -> p c n", c=4)).then_inc(pT1_dve.sem, 1)
                wait(o1_ps, t)
                v.tensor_tensor(heads(hp[:, :]), heads(ps[:, 6, 0:D]), each_head(rs1, HD), ALU.mult).then_inc(o1_ready.sem, 1)
                wait(xattn1_ps, t)
                pl(v.tensor_tensor(xp[:, :], ps[:, 6, 0:D], xp[:, :], ALU.add))

            def p_rot(t):
                layernorm(pl, t, sp_, xp[:, :], hp[:, :], xr_var, xr_rstd).then_inc(hr_ready.sem, 1)
                wait(qkv_ps, t)
                qk = ps[:, 6, 0:384].rearrange("p (j k two) -> p j k two", j=3, two=2)
                other = tmp1[:, 0:384].rearrange("p (j k two) -> p j k two", j=3, two=2)
                sn = sin.rearrange("p (k two) -> p k two", two=2)
                for e in range(2):
                    v.tensor_tensor(other[:, :, :, e], qk[:, :, :, 1 - e],
                                    sn[:, :, e].unsqueeze(1).to_broadcast([P, 3, K1 // 2]), ALU.mult)
                pl(v.tensor_tensor(rot.rearrange("p (j k) -> p j k", j=3), ps[:, 6, 0:384].rearrange("p (j k) -> p j k", j=3),
                                   cos.unsqueeze(1).to_broadcast([P, 3, K1]), ALU.mult))
                v.tensor_tensor(rot, rot, tmp1[:, 0:384], ALU.add).then_inc(rot_ready.sem, 1)
                wait(rs_ps, t)
                prb = P1[:, 0:P].rearrange("p (b n) -> p b n", b=2)
                pl(v.tensor_tensor(prb, ps[:, 6, 0:P].rearrange("p (b n) -> p b n", b=2),
                                   causal.unsqueeze(1).to_broadcast([P, 2, N]), ALU.add))
                pl(v.tensor_reduce(sp_[:, 0:2], prb, AX.X, ALU.max))
                v.tensor_tensor(prb, prb, sp_[:, 0:2].unsqueeze(2).to_broadcast([P, 2, N]), ALU.subtract
                                ).then_inc(rd_ready.sem, 1)
                wait(re_ready, t)
                pl(v.tensor_reduce(sp_[:, 2:4], prb, AX.X, ALU.add))
                pl(v.reciprocal(sp_[:, 4:6], sp_[:, 2:4]))
                v.tensor_tensor(prb, prb, sp_[:, 4:6].unsqueeze(2).to_broadcast([P, 2, N]), ALU.mult
                                ).then_inc(rp_ready.sem, 1)
                wait(ro_ps, t)
                v.tensor_copy(PT1[:, 1:3, N:2 * N], ps[:, 7, 0:P].rearrange("p (h n) -> p h n", h=2)).then_inc(ro_dve.sem, 1)
                wait(attn1_ps, t)
                pl(v.tensor_tensor(xp[:, :], ps[:, 6, 0:D], xp[:, :], ALU.add))

            def p_proto(t):
                sync(layernorm(pl, t, sp_, xp[:, :], hp[:, :], xg_var, xg_rstd), hg_ready, t)
                pl(v.tensor_tensor_reduce(tmp1[:, 0:D], hp[:, :], hp[:, :], 1.0, 0.0, ALU.mult, ALU.add, sp_[:, 42:43]))
                wait(dist_ps, t)
                dst = sp_[:, 0:PROTOS]
                pl(v.scalar_tensor_tensor(dst, ps[:, 7, 2 * P:2 * P + PROTOS], -2.0, p2[:, :], ALU.mult, ALU.add))
                v.tensor_scalar(dst, dst, sp_[:, 42:43], 0.0, ALU.add, ALU.max).then_inc(d2_ready.sem, 1)
                wait(root_ready, t)
                pl(v.tensor_scalar(dst, dst, tneg[:, 0:1], None, ALU.mult))
                pl(v.reduce_max(sp_[:, 43:44], dst, AX.X))
                v.tensor_scalar(sp_[:, 40:41], sp_[:, 43:44], -1.0, None, ALU.mult).then_inc(fs_ready.sem, 1)
                wait(fe_ready, t)
                pl(v.reciprocal(sp_[:, 44:45], sp_[:, 41:42]))
                pl(v.tensor_scalar(wf[:, 0:PROTOS], w32[:, :], sp_[:, 44:45], None, ALU.mult), settle)
                top_two(pl, wf[:, 0:PROTOS], wf, topf, topvf, restf, PROTOS)
                pl(v.tensor_tensor(w32[:, :], wf[:, 0:PROTOS], restf[:, 0:PROTOS], ALU.subtract))
                pl(v.tensor_tensor(sp_[:, 45:46], topf[:, 0:1], topf[:, 1:2], ALU.add))
                pl(v.reciprocal(sp_[:, 46:47], sp_[:, 45:46]))
                sync(v.tensor_scalar(w32[:, :], w32[:, :], sp_[:, 46:47], None, ALU.mult), wt_ready, t)
                wait(low_ps, t)
                v.tensor_tensor(tmp1[:, :].rearrange("p (k r) -> p k r", r=RANK),
                                ps[:, 6, :].rearrange("p (k r) -> p k r", r=RANK),
                                w32[:, :].unsqueeze(2).to_broadcast([P, PROTOS, RANK]), ALU.mult).then_inc(low_ready.sem, 1)
                wait(ffn1_ps, t)
                v.tensor_tensor(xo[:, :], ps[:, 6, 0:D], xp[:, :], ALU.add).then_inc(out_ready.sem, 1)
                pl.end()

            def layer0(u):
                q_norm(u)
                ctx_copies(u)
                q_sim(u)
                q_probT(u)
                q_feats(u)
                q_attn_proj(u)
                q_attn(u)

            def layer1(t):
                p_mem(t)
                p_xattn(t)
                p_rot(t)
                p_proto(t)

            v.memset(headw, 0.0).then_inc(headw_zero.sem, 1)
            v.memset(pext[:, :], -1.0)
            v.memset(topv[:, :], -1.0)
            v.memset(wf[:, :], -1.0)
            v.memset(topvf[:, :], -1.0)
            v.memset(w9[:, :], 1.0)
            v.memset(h0[:, :], 1.0).then_inc(sets_dve.sem, 1)
            dve.wait_ge(sets_dve.sem, 1)
            dve.wait_ge(const_in.sem, 16 * N_CONST)
            v.tensor_copy(offs[:, :], offs0)
            v.tensor_scalar(sp_[:, 1:2], temp, -1.0, None, ALU.mult).then_inc(sets_dve.sem, 1)
            dve.wait_ge(sets_dve.sem, 2)
            dve.wait_ge(l1_w_in.sem, 16 * 17)
            v.tensor_tensor(tmp1[:, 0:DC * PROTOS].rearrange("p (c n) -> p c n", c=DC), prot[:, :, :], prot[:, :, :],
                            ALU.mult).then_inc(sets_dve.sem, 1)
            dve.wait_ge(setup_mm.sem, 1)
            for w in range(2):
                v.tensor_copy(wqkp[:, :, w, :], ps[:, w, :].rearrange("p (c n) -> p c n", c=DC))
            v.tensor_copy(bqkp[:, :], ps[:, 2, 0:4])
            dve.wait_ge(setup_mm.sem, 2)
            v.tensor_copy(p2[:, :], ps[:, 3, 0:PROTOS]).then_inc(sets_dve.sem, 1)
            dve.wait_ge(sets_dve.sem, 4)
            v.tensor_tensor(sp_[:, 2:3], temp, sp_[:, 1:2], ALU.max).then_inc(sets_dve.sem, 1)
            dve.wait_ge(sets_dve.sem, 5)
            v.tensor_scalar(tneg[:, :], sp_[:, 2:3], 0.1, None, ALU.max).then_inc(sets_dve.sem, 1)
            dve.wait_ge(sets_dve.sem, 6)
            v.reciprocal(sp_[:, 0:1], tneg[:, :]).then_inc(sets_dve.sem, 1)
            dve.wait_ge(sets_dve.sem, 7)
            v.tensor_scalar(tneg[:, :], sp_[:, 0:1], -1.0, None, ALU.mult).then_inc(setup_done.sem, 1)
            layer0(0)
            q_experts(0)
            with dve.Fori(0, TILES - 1) as t:
                p_scores(t)
                layer1(t)
                layer0(t + 1)
                q_experts(t + 1)
                wait(out_stored, t)
            p_scores(TILES - 1)
            layer1(TILES - 1)

        @block.gpsimd
        def _(pool):
            def q_keys(u):
                pool.wait_ge(kT_ready.sem, kT_ready.at(u))
                block_keys(nc.gpsimd, kbd0[:, 0], kT0[:, 0, :]).then_inc(kbd0_pool.sem, 1)

            def p_gather(t):
                pool.wait_ge(gidx_ready.sem, settle(pool, gidx_ready.at(t)))
                pool.indirect_dma_start(mem[:, :], None, ctx_rows.rearrange("b m d -> (b m) d"),
                                        bass.IndirectOffsetOnAxis(gidx[:, 0:1], 0)).then_inc(mem_in.sem, 16)

            def rstd(col, tile, var_sig, rstd_sig):
                pool.wait_ge(var_sig.sem, var_sig.at(tile))
                nc.gpsimd.tensor_tensor(col[:, 58:59], col[:, 57:58], minus_half, ALU.pow).then_inc(rstd_sig.sem, 1)

            def layer0(u):
                rstd(sq, u, x0_var, x0_rstd)
                rstd(sq, u, xa_var, xa_rstd)
                q_keys(u)

            def layer1(t):
                rstd(sp_, t, xr_var, xr_rstd)
                rstd(sp_, t, xg_var, xg_rstd)
                pool.wait_ge(d2_ready.sem, d2_ready.at(t))
                nc.gpsimd.tensor_tensor(sp_[:, 0:PROTOS], sp_[:, 0:PROTOS], half.to_broadcast([P, PROTOS]),
                                        ALU.pow).then_inc(root_ready.sem, 1)

            pool.wait_ge(const_in.sem, 16 * N_CONST)
            layer0(0)
            rstd(sq, 0, xf_var, xf_rstd)
            with pool.Fori(0, TILES - 1) as t:
                rstd(sp_, t, x1_var, x1_rstd)
                p_gather(t)
                layer1(t)
                layer0(t + 1)
                rstd(sq, t + 1, xf_var, xf_rstd)
            rstd(sp_, TILES - 1, x1_var, x1_rstd)
            p_gather(TILES - 1)
            layer1(TILES - 1)


def constants():
    c = np.zeros((P, C_END), np.float32)
    p = np.arange(P)
    c[:, C_ID:C_ID + P] = np.eye(P)
    c[:, C_BLK:C_BLK + P] = p[:, None] // N == p[None] // N
    c[:, C_HEAD:C_HEAD + H8] = p[:, None] // HD == np.arange(H8)[None]
    c[:, C_HALF:C_HALF + 2] = p[:, None] // N == np.arange(2)[None]
    theta = np.float32(10000.0) ** (np.float32(-2.0) * np.arange(0, K1, 2, dtype=np.float32) / np.float32(K1))
    angle = (p % N).astype(np.float32)[:, None] * theta[None]
    c[:, C_COS:C_COS + K1] = np.repeat(np.cos(angle), 2, 1)
    c[:, C_SIN:C_SIN + K1] = np.stack([-np.sin(angle), np.sin(angle)], 2).reshape(P, K1)
    c[:, C_CAUSAL:C_CAUSAL + N] = np.where(np.arange(N)[None] <= (p % N)[:, None], 0.0, NEG)
    c[:, C_ONES:C_ONES + P] = 1.0
    c[:, C_OFFS] = p // N * M
    c[:, C_EXP:C_EXP + 2] = -0.5, 0.5
    return c


_AS_IS = ['x', 'ctx_1024', 'L0_xattn_W_qv', 'L0_attn_Wv', 'L0_attn_Wp', 'L0_ffn_router_w', 'L0_ffn_sw1', 'L0_ffn_sw2',
          'L0_ffn_rw1', 'L0_ffn_rw2', 'L1_ffn_bias']


def kernel(**inputs):
    import numpy as _np
    import concourse.bacc as _bacc
    from concourse import mybir as _mybir
    from concourse.bass_utils import run_bass_kernel_spmd as _run

    i = {k: _np.asarray(v) for k, v in inputs.items()}
    laid = {k: i[k] for k in _AS_IS}
    laid["consts"] = constants()
    hidden = _np.concatenate([i['L0_ffn_sb1'][None], i['L0_ffn_rb1']], 0)
    laid["cols"] = _np.concatenate([
        i['L0_xattn_w_sim'].reshape(6, P).T, i['L0_attn_bq'].reshape(2, P).T, i['L0_attn_bk'].reshape(2, P).T,
        _np.broadcast_to(i['L0_xattn_b_sim'].reshape(1, 1), (P, 1)), hidden.reshape(9 * HC, P).T,
        _np.broadcast_to(i['L1_ffn_temp'].reshape(1, 1), (P, 1))], 1)
    laid["rows"] = _np.broadcast_to(_np.concatenate([i['L0_xattn_b_qv'], i['L0_attn_bv'], i['L0_ffn_router_b']])[None],
                                    (P, 2 * D + EXPERTS))
    laid["ebias"] = _np.concatenate([i['L0_ffn_rb2'], i['L0_ffn_sb2'][None]], 0)
    laid["wq0T"], laid["wk0T"] = i['L0_attn_Wq'].T, i['L0_attn_Wk'].T
    laid["wq1T"], laid["wkv1T"], laid["wc1T"] = i['L1_xattn_Wq'].T, i['L1_xattn_Wkv'].T, i['L1_xattn_Wc'].T
    laid["wqkvT"] = _np.concatenate([i['L1_attn_Wq'].reshape(2 * K1, D), i['L1_attn_Wk'], i['L1_attn_Wv']], 0).T
    laid["woT"] = i['L1_attn_Wo'].T
    laid["protT"] = i['L1_ffn_prototypes'].T
    laid["bT"] = i['L1_ffn_B'].reshape(PROTOS * RANK, D).T
    laid["aT"] = i['L1_ffn_A'].transpose(0, 2, 1).reshape(PROTOS * RANK, D)

    nc = _bacc.Bacc("TRN2", target_bir_lowering=False, num_devices=1)
    arrays, aps = {}, {}
    for name, arr in laid.items():
        arr = _np.ascontiguousarray(arr)
        arrays[f"in_{name}"] = arr
        aps[name] = nc.dram_tensor(f"in_{name}", arr.shape, _mybir.dt.from_np(arr.dtype), kind="ExternalInput").ap()
    aps["out"] = nc.dram_tensor("out_0", (B, N, D), F32, kind="ExternalOutput").ap()
    build(nc, aps)
    r = _run(nc, [arrays], core_ids=[0])
    return r.results[0]["out_0"]
```

```python
from contextlib import ExitStack

import numpy as np
import concourse.bass as bass
from concourse import mybir

P = 128
B, N, D = 32, 64, 256
M = 1601
TILES = B * N // P
DC = D // P
MC = -(-M // P)
MT = M - (MC - 1) * P
BANK = 512
HEADS, HD = 16, 16
H8 = P // HD
EXPERTS, HID = 8, 512
HC = HID // P
PROTOS, RANK = 32, 16
K1 = 128
F32, U32 = mybir.dt.float32, mybir.dt.uint32
ALU, ACT, AX = mybir.AluOpType, mybir.ActivationFunctionType, mybir.AxisListType
EPS = 1e-5
NEG = -1.0e30

C_ID, C_BLK, C_HEAD, C_HALF = 0, 128, 256, 264
C_COS, C_SIN, C_CAUSAL, C_ONES, C_OFFS, C_EXP, C_END = 266, 266 + 128, 266 + 256, 266 + 320, 266 + 448, 266 + 449, 266 + 451


class Signal:

    def __init__(self, sem, per=1):
        self.sem, self.per = sem, per

    def at(self, tile, k=None):
        return tile * self.per + (self.per if k is None else k)


class Chain:

    def __init__(self, eng, sem, per):
        self.eng, self.sem, self.per, self.tile, self.n = eng, sem, per, None, 0

    def begin(self, tile):
        self.tile, self.n = tile, 0

    def __call__(self, ins, before_wait=None):
        self.n += 1
        ins.then_inc(self.sem, 1)
        value = self.tile * self.per + self.n
        if before_wait:
            value = before_wait(self.eng, value)
        self.eng.wait_ge(self.sem, value)

    def end(self):
        assert self.n == self.per, self.n


def build(nc, a):
    ctx = ExitStack()
    with ctx:
        def sb(name, shape, dt=F32):
            return ctx.enter_context(nc.sbuf_tensor(name, shape, dt))

        def S(name, per=1):
            return Signal(ctx.enter_context(nc.semaphore(name)), per)

        ps = ctx.enter_context(nc.psum_tensor("ps", [P, 8, BANK], F32))
        wide = ps[:, 0:4, :].rearrange("p a b -> p (a b)")[:, 0:M]

        con = sb("con", [P, C_END])
        ident, blockmask = con[:, C_ID:C_ID + P], con[:, C_BLK:C_BLK + P]
        headmask, halfmask = con[:, C_HEAD:C_HEAD + H8], con[:, C_HALF:C_HALF + 2]
        cos, sin = con[:, C_COS:C_COS + K1], con[:, C_SIN:C_SIN + K1]
        causal, ones = con[:, C_CAUSAL:C_CAUSAL + N], con[:, C_ONES:C_ONES + P]
        offs0 = con[:, C_OFFS:C_OFFS + 1]
        minus_half, half = con[:, C_EXP:C_EXP + 1], con[:, C_EXP + 1:C_EXP + 2]
        cols = sb("cols", [P, 6 + 4 + 1 + 36 + 1])
        wsim, bqk, bsim = cols[:, 0:6], cols[:, 6:10], cols[:, 10:11]
        hbias, temp = cols[:, 11:47], cols[:, 47:48]
        rows = sb("rows", [P, 2 * D + EXPERTS])
        bqv, bv, rb = rows[:, 0:D], rows[:, D:2 * D], rows[:, 2 * D:]
        wqv = sb("wqv", [P, 4 * DC, D])
        wqkp = sb("wqkp", [P, DC, 2, D])
        wv0 = sb("wv0", [P, DC, D])
        wrout = sb("wrout", [P, DC, EXPERTS])
        sw1 = sb("sw1", [P, DC, HID])
        sw2 = sb("sw2", [P, HC, D])
        rw1 = sb("rw1", [P, DC, EXPERTS, HID])
        rw2 = sb("rw2", [P, HC, EXPERTS, D])
        ebias = sb("ebias", [EXPERTS + 1, D])
        wq1 = sb("wq1", [P, DC, D])
        wkrep = sb("wkrep", [P, DC, H8, HD])
        wv1 = sb("wv1", [P, DC, HD])
        wc1 = sb("wc1", [P, DC, D])
        wqkv = sb("wqkv", [P, DC, 4 * K1])
        wo = sb("wo", [P, 2, D])
        prot = sb("prot", [P, DC, PROTOS])
        bT = sb("bT", [P, DC, PROTOS * RANK])
        aT = sb("aT", [P, 4, D])
        pbias = sb("pbias", [PROTOS, D])
        p2 = sb("p2", [P, PROTOS])
        tneg = sb("tneg", [P, 1])
        bqkp = sb("bqkp", [P, 4])

        ctxN = sb("ctxN", [P, 2, MC, D])
        ctxT = sb("ctxT", [P, DC, 2, M])
        share = sb("share", [P, M + MC * P])
        prob, probT = share[:, 0:M], share[:, M:].rearrange("p (c n) -> p c n", c=MC)
        P0, PT0 = share[:, 0:1024], share[:, 1024:2048].rearrange("p (g n) -> p g n", g=8)
        kbd0 = share[:, 1024:3072].rearrange("p (c b h n) -> p c b h n", c=DC, b=2, h=H8)
        h1T = share[:, 0:2 * HID].rearrange("p (s c n) -> p s c n", s=2, c=HC)

        xin, xq, xp, xo = (sb(n, [P, D]) for n in ("xin", "xq", "xp", "xo"))
        h0 = sb("h0", [P, D])
        tmp = sb("tmp", [P, D])
        hT = sb("hT", [P, DC, P])
        turns = sb("turns", [P, 8 * P])
        simq = turns[:, 0:DC * P].rearrange("p (c n) -> p c n", c=DC)
        featsT = turns[:, 2 * P:8 * P].rearrange("p (i n) -> p i n", i=6)
        hTd = turns[:, 0:4 * P].rearrange("p (c b e n) -> p c b e n", c=DC, b=2, e=2)
        qT0 = turns[:, 4 * P:6 * P].rearrange("p (c n) -> p c n", c=DC)
        kT0 = turns[:, 6 * P:8 * P].rearrange("p (c n) -> p c n", c=DC)
        vb0 = sb("vb0", [P, 2, 8, 2, HD])
        diag = sb("diag", [P, P])
        sq = sb("sq", [P, 64])
        sp_ = sb("sp", [P, 64])
        mx0, rs0 = sb("mx0", [P, HEADS]), sb("rs0", [P, HEADS])
        mx1, rs1 = sb("mx1", [P, HEADS]), sb("rs1", [P, HEADS])
        pext = sb("pext", [P, 16])
        top, topv = sb("top", [P, 8]), sb("topv", [P, 8])
        rest = sb("rest", [P, 16])
        w9 = sb("w9", [P, EXPERTS + 1])
        wT9 = diag[0:EXPERTS + 1, :]

        hp, tmp1 = sb("hp", [P, D]), sb("tmp1", [P, 2 * D])
        hTp, qpT = (sb(n, [P, DC, P]) for n in ("hTp", "qpT"))
        am, ai, gidx = sb("am", [P, 8]), sb("ai", [P, 8], U32), sb("gidx", [P, 1], U32)
        offs = sb("offs", [P, 1])
        vb1 = sb("vb1", [P, 2, 2, HD])
        P1 = sb("P1", [P, 1024])
        kbd1 = P1[:, :].rearrange("p (b h n) -> p b h n", b=2, h=H8)
        rprob = P1[:, 0:P].rearrange("p (b n) -> p b n", b=2)
        rot, vsb = P1[:, P:4 * P], P1[:, 7 * P:8 * P]
        rqT = P1[:, 4 * P:6 * P].rearrange("p (b h n) -> p b h n", b=2, h=2)
        rkT = P1[:, 6 * P:7 * P]
        PT1 = sb("PT1", [P, 8, P])
        pt1 = PT1[:, :, :].rearrange("p g n -> p (g n)")
        mem = pt1[:, 0:D]
        memT = pt1[:, D:2 * D].rearrange("p (c n) -> p c n", c=DC)
        memTd = pt1[:, 2 * D:4 * D].rearrange("p (c b e n) -> p c b e n", c=DC, b=2, e=2)
        w32 = sb("w32", [P, PROTOS])
        wf, restf = sb("wf", [P, PROTOS + 8]), sb("restf", [P, PROTOS + 8])
        topf, topvf = sb("topf", [P, 8]), sb("topvf", [P, 8])
        wT32 = sb("wT32", [PROTOS, P])
        setup = share[:, 0:2 * DC * D].rearrange("p (w c n) -> p w c n", w=2, c=DC)
        headw = share[:, 2 * DC * D:2 * DC * D + P]

        const_in, attn0_w_in, ffn0_w_in, l1_w_in = S("const_in"), S("attn0_w_in"), S("ffn0_w_in"), S("l1_w_in")
        headw_zero, headw_in = S("headw_zero"), S("headw_in")
        setup_mm, setup_done, sets_dve = S("setup_mm"), S("setup_done"), S("sets_dve")
        x_in, ctx_in = S("x_in", 16), S("ctx_in", 64)
        ctxT_in, ctxT_used = [S(f"ctxT_in{k}", 32) for k in range(4)], S("ctxT_used", 4)
        out_stored = S("out_stored", 16)
        x0_var, x0_rstd = S("x0_var"), S("x0_rstd")
        xa_var, xa_rstd = S("xa_var"), S("xa_rstd")
        xf_var, xf_rstd = S("xf_var"), S("xf_rstd")
        x1_var, x1_rstd = S("x1_var"), S("x1_rstd")
        xr_var, xr_rstd = S("xr_var"), S("xr_rstd")
        xg_var, xg_rstd = S("xg_var"), S("xg_rstd")
        d2_ready, root_ready = S("d2_ready"), S("root_ready")
        h0_ready, h0T_ps, h0T_ready, simq_ready = S("h0_ready"), S("h0T_ps"), S("h0T_ready"), S("simq_ready", 2)
        sim_ps, own_ps, sim_max, prob_ready = S("sim_ps"), S("own_ps"), S("sim_max"), S("prob_ready")
        hqn_ready, hqT_ps = S("hqn_ready"), S("hqT_ps")
        probT_ps, probT_act, probT_dve = S("probT_ps", 4), S("probT_act", 2), S("probT_dve", 2)
        hq_ps = S("hq_ps")
        diag_ready, rowmax_ps, gmax_ready = S("diag_ready"), S("rowmax_ps"), S("gmax_ready")
        batt_ready, battz_ps, battw_ready, hc_ps = S("batt_ready"), S("battz_ps"), S("battw_ready"), S("hc_ps")
        feats_ready = S("feats_ready")
        xattn0_ps = S("xattn0_ps")
        ha_ready, haT_ps, haT_ready, haTd_ready = S("ha_ready"), S("haT_ps"), S("haT_ready"), S("haTd_ready", 2)
        qk_ps, v_ps, qT_ready, kT_ready = S("qk_ps"), S("v_ps"), S("qT_ready", 2), S("kT_ready", 2)
        vb0_ready, kbd0_pool, kbd0_dve = S("vb0_ready", 2), S("kbd0_pool"), S("kbd0_dve")
        s0_ps, d0_ready, e0_ready = S("s0_ps"), S("d0_ready"), S("e0_ready")
        pT0_ps, pT0_act, pT0_dve, o0_ps = S("pT0_ps", 2), S("pT0_act"), S("pT0_dve"), S("o0_ps")
        hf0_ready, hf0T_ps, hf0T_ready = S("hf0_ready"), S("hf0T_ps"), S("hf0T_ready")
        router_ps, rmax_ready, rexp_ready = S("router_ps"), S("rmax_ready"), S("rexp_ready")
        gate_ready, gateT_ps, gateT_ready = S("gate_ready"), S("gateT_ps"), S("gateT_ready")
        hid_ps, gelu_ready, eout_ps, eout_used = S("hid_ps", 9), S("gelu_ready", 9), S("eout_ps", 9), S("eout_used", 9)
        h1_ready, h1T_ps, h1T_ready = S("h1_ready"), S("h1T_ps"), S("h1T_ready")
        qp_ps, qp_ready, amax_done = S("qp_ps"), S("qp_ready"), S("amax_done")
        gidx_ready, mem_in = S("gidx_ready"), S("mem_in", 16)
        memT_ps, memT_ready, memTd_ready = S("memT_ps"), S("memT_ready"), S("memTd_ready", 2)
        mkv_ps, vb1_ready, kbd1_ready = S("mkv_ps"), S("vb1_ready"), S("kbd1_ready")
        s1_ps, d1_ready, e1_ready = S("s1_ps"), S("d1_ready"), S("e1_ready")
        pT1_ps, pT1_act, pT1_dve, o1_ps = S("pT1_ps", 2), S("pT1_act"), S("pT1_dve"), S("o1_ps")
        o1_ready, o1T_ps, o1T_ready, xattn1_ps = S("o1_ready"), S("o1T_ps"), S("o1T_ready"), S("xattn1_ps")
        hr_ready, hrT_ps, hrT_ready, qkv_ps = S("hr_ready"), S("hrT_ps"), S("hrT_ready"), S("qkv_ps")
        rot_ready, v1_ready, qkT_ps, qkT_ready = S("rot_ready"), S("v1_ready"), S("qkT_ps"), S("qkT_ready", 2)
        rs_ps, rd_ready, re_ready, rp_ready = S("rs_ps"), S("rd_ready"), S("re_ready"), S("rp_ready")
        rpT_ps, rpT_ready, ro_ps, ro_act, ro_dve = S("rpT_ps"), S("rpT_ready"), S("ro_ps"), S("ro_act"), S("ro_dve")
        attn1_ps = S("attn1_ps")
        hg_ready, hgT_ps, hgT_ready, dist_ps = S("hg_ready"), S("hgT_ps"), S("hgT_ready"), S("dist_ps")
        low_ps, fs_ready, fe_ready, wt_ready = S("low_ps"), S("fs_ready"), S("fe_ready"), S("wt_ready")
        wtT_ps, wtT_ready = S("wtT_ps"), S("wtT_ready")
        low_ready, lowT_ps, lowT_ready, ffn1_ps, out_ready = S("low_ready"), S("lowT_ps"), S("lowT_ready"), S("ffn1_ps"), S("out_ready")
        q_chain, p_chain = S("q_chain", 28), S("p_chain", 30)

        ctx_rows = a["ctx_1024"]
        x_rows = a["x"].rearrange("b n d -> (b n) d")
        out_rows = a["out"].rearrange("b n d -> (b n) d")
        N_CONST, N_ATTN0, N_FFN0, N_L1 = 3, 5, 7, 10

        def chunked(ap, p=P):
            return ap.rearrange("(c p) n -> p c n", p=p)

        def settle(eng, value):
            if not isinstance(value, int):
                eng.lower_val(value)
            eng.wait_ge(const_in.sem, 16)
            return value

        def block_keys(eng, out, src):
            return eng.tensor_tensor(out, src.rearrange("p (b n) -> p b n", b=2).unsqueeze(2).to_broadcast([P, 2, H8, N]),
                                     headmask.unsqueeze(1).unsqueeze(3).to_broadcast([P, 2, H8, N]), ALU.mult)

        block = ctx.enter_context(nc.Block())

        @block.sync
        def _(sp):
            def load_ctx(u):
                for b in range(2):
                    src = ctx_rows[bass.ds(u * 2 + b, 1), :, :].rearrange("o m d -> (o m) d")
                    sp.dma_start(ctxN[:, b, 0:MC - 1, :], src[0:(MC - 1) * P, :].rearrange("(c p) d -> p c d", p=P)
                                 ).then_inc(ctx_in.sem, 16)
                    sp.dma_start(ctxN[0:MT, b, MC - 1, :], src[(MC - 1) * P:M, :]).then_inc(ctx_in.sem, 16)

            def load_ctxT(u):
                for k in range(4):
                    cols = slice(k * BANK, min((k + 1) * BANK, M))
                    if not isinstance(u, int) or u > 0:
                        sp.wait_ge(ctxT_used.sem, ctxT_used.at(u - 1, k + 1))
                    for b in range(2):
                        src = a["ctxT"][bass.ds(u * 2 + b, 1), :, :].rearrange("o (c p) m -> (o p) c m", p=P)
                        sp.dma_start(ctxT[:, :, b, cols], src[:, :, cols]).then_inc(ctxT_in[k].sem, 16)

            def load_x(u):
                sp.dma_start(xin[:, :], x_rows[bass.ds(u * P, P), :]).then_inc(x_in.sem, 16)

            for dst, src in ((con, a["consts"]), (cols, a["cols"]), (rows, a["rows"])):
                sp.dma_start(dst[:, :], src).then_inc(const_in.sem, 16)
            load_x(0)
            load_ctxT(0)
            load_ctx(0)
            sp.dma_start(wqv[:, :, :], chunked(a["L0_xattn_W_qv"])).then_inc(attn0_w_in.sem, 16)
            sp.dma_start(setup[:, 0], chunked(a["wq0T"])).then_inc(attn0_w_in.sem, 16)
            sp.dma_start(setup[:, 1], chunked(a["wk0T"])).then_inc(attn0_w_in.sem, 16)
            sp.dma_start(wv0[:, :, :], chunked(a["L0_attn_Wv"])).then_inc(attn0_w_in.sem, 16)
            sp.wait_ge(headw_zero.sem, 1)
            for i in range(H8):
                sp.dma_start(headw[i * HD:(i + 1) * HD, i * HD:(i + 1) * HD], a["L0_attn_Wp"]).then_inc(headw_in.sem, 16)
            sp.dma_start(wrout[:, :, :], chunked(a["L0_ffn_router_w"])).then_inc(ffn0_w_in.sem, 16)
            sp.dma_start(ebias[:, :], a["ebias"]).then_inc(ffn0_w_in.sem, 16)
            sp.dma_start(sw1[:, :, :], chunked(a["L0_ffn_sw1"])).then_inc(ffn0_w_in.sem, 16)
            sp.dma_start(sw2[:, :, :], chunked(a["L0_ffn_sw2"])).then_inc(ffn0_w_in.sem, 16)
            for dc in range(DC):
                sp.dma_start(rw1[:, dc], a["L0_ffn_rw1"].rearrange("e (c p) h -> p c e h", p=P)[:, dc]
                             ).then_inc(ffn0_w_in.sem, 16)
            for hc in range(HC):
                sp.dma_start(rw2[:, hc], a["L0_ffn_rw2"].rearrange("e (c p) d -> p c e d", p=P)[:, hc]
                             ).then_inc(ffn0_w_in.sem, 16)
            sp.dma_start(wq1[:, :, :], chunked(a["wq1T"])).then_inc(l1_w_in.sem, 16)
            for i in range(H8):
                sp.dma_start(wkrep[:, :, i, :], chunked(a["wkv1T"])[:, :, 0:HD]).then_inc(l1_w_in.sem, 16)
            sp.dma_start(wv1[:, :, :], chunked(a["wkv1T"])[:, :, HD:2 * HD]).then_inc(l1_w_in.sem, 16)
            sp.dma_start(wc1[:, :, :], chunked(a["wc1T"])).then_inc(l1_w_in.sem, 16)
            sp.dma_start(wqkv[:, :, :], chunked(a["wqkvT"])).then_inc(l1_w_in.sem, 16)
            sp.dma_start(wo[:, :, :], chunked(a["woT"])).then_inc(l1_w_in.sem, 16)
            sp.dma_start(prot[:, :, :], chunked(a["protT"])).then_inc(l1_w_in.sem, 16)
            sp.dma_start(bT[:, :, :], chunked(a["bT"])).then_inc(l1_w_in.sem, 16)
            sp.dma_start(aT[:, :, :], chunked(a["aT"])).then_inc(l1_w_in.sem, 16)
            sp.dma_start(pbias[:, :], a["L1_ffn_bias"]).then_inc(l1_w_in.sem, 16)

            def prefetch(u):
                sp.wait_ge(hq_ps.sem, hq_ps.at(u - 1))
                load_ctx(u)
                sp.wait_ge(ha_ready.sem, ha_ready.at(u - 1))
                load_x(u)

            def store(t):
                sp.wait_ge(out_ready.sem, out_ready.at(t))
                sp.dma_start(out_rows[bass.ds(t * P, P), :], xo[:, :]).then_inc(out_stored.sem, 16)

            prefetch(1)
            with sp.Fori(0, TILES - 2) as t:
                load_ctxT(t + 1)
                prefetch(t + 2)
                store(t)
            load_ctxT(TILES - 1)
            store(TILES - 2)
            store(TILES - 1)
            sp.wait_ge(out_stored.sem, out_stored.at(TILES - 1))

        @block.tensor
        def _(pe):
            def wait(sig, tile, k=None):
                pe.wait_ge(sig.sem, sig.at(tile, k))

            def transposes(bank, src, n, sig, width=P, col=0):
                for i in range(n):
                    last = nc.tensor.transpose(ps[0:width, bank, col + i * P:col + (i + 1) * P],
                                               src[:, i * width:(i + 1) * width], ident)
                last.then_inc(sig.sem, 1)

            def setup_weights():
                pe.wait_ge(const_in.sem, 16 * N_CONST)
                pe.wait_ge(attn0_w_in.sem, 16 * 4)
                pe.wait_ge(headw_in.sem, 16 * H8)
                for w in range(2):
                    for dc in range(DC):
                        for c in range(DC):
                            last = nc.tensor.matmul(ps[:, w, dc * D + c * P:dc * D + (c + 1) * P],
                                                    setup[:, w, c, dc * P:(dc + 1) * P], headw, start=True, stop=True)
                for k in range(4):
                    last = nc.tensor.matmul(ps[:, 2, k:k + 1], headw, bqk[:, k:k + 1], start=True, stop=True)
                last.then_inc(setup_mm.sem, 1)

            def setup_protos():
                pe.wait_ge(sets_dve.sem, 3)
                for dc in range(DC):
                    last = nc.tensor.matmul(ps[:, 3, 0:PROTOS], ones, tmp1[:, dc * PROTOS:(dc + 1) * PROTOS],
                                            start=(dc == 0), stop=(dc == DC - 1))
                last.then_inc(setup_mm.sem, 1)
                pe.wait_ge(sets_dve.sem, 4)

            def wide_scores(q, each_piece):
                for k in range(4):
                    n = min(BANK, M - k * BANK)
                    for dc in range(DC):
                        for b in range(2):
                            last = nc.tensor.matmul(ps[b * N:(b + 1) * N, k, 0:n], q[:, dc, b * N:(b + 1) * N],
                                                    ctxT[:, dc, b, k * BANK:k * BANK + n],
                                                    start=(dc == 0), stop=(dc == DC - 1))
                    each_piece(last, k)

            def core_scores(qT, kbd, shared, bank, sig):
                for c in range(DC):
                    for b in range(2):
                        k = kbd[:, b] if shared else kbd[:, c, b]
                        last = nc.tensor.matmul(ps[b * N:(b + 1) * N, bank + c, :], qT[:, c, b * N:(b + 1) * N],
                                                k, start=True, stop=True)
                last.then_inc(sig.sem, 1)

            def core_transposes(src, bank, sig):
                for half in range(2):
                    transposes(bank + half, src[:, half * BANK:(half + 1) * BANK], 4, sig)

            def core_values(PT, vb, shared, bank, sig):
                for g in range(8):
                    for b in range(2):
                        v = vb[:, b] if shared else vb[:, b, g]
                        last = nc.tensor.matmul(ps[b * N:(b + 1) * N, bank, g * 32:(g + 1) * 32],
                                                PT[:, g, b * N:(b + 1) * N], v, start=True, stop=True)
                last.then_inc(sig.sem, 1)

            def q_norm(u):
                wait(h0_ready, u)
                transposes(4, h0[:, :], 2, h0T_ps)

            def q_scores(u, first):
                wait(simq_ready, u)
                wait(ctxT_in[0], u)
                if not first:
                    wait(amax_done, u - 1)

                def each_piece(last, k):
                    if k < 3:
                        wait(ctxT_in[k + 1], u)
                    else:
                        last.then_inc(sim_ps.sem, 1)

                wide_scores(simq, each_piece)
                for dc in range(DC):
                    last = nc.tensor.matmul(ps[:, 4, 0:1], hT[:, dc, :], wsim[:, dc:dc + 1],
                                            start=(dc == 0), stop=(dc == DC - 1))
                last.then_inc(own_ps.sem, 1)

            def q_batt_max(u):
                wait(diag_ready, u)
                nc.tensor.matmul(ps[:, 5, 0:P], ones, diag[:, :], start=True, stop=True).then_inc(rowmax_ps.sem, 1)

            def q_batt_sum(u):
                wait(batt_ready, u)
                nc.tensor.matmul(ps[:, 5, P:P + 1], blockmask, sq[:, 8:9], start=True, stop=True).then_inc(battz_ps.sem, 1)

            def q_batt_mean(u):
                wait(battw_ready, u)
                for dc in range(DC):
                    last = nc.tensor.matmul(ps[:, 5, 2 * P + dc * P:2 * P + (dc + 1) * P], h0[:, dc * P:(dc + 1) * P],
                                            diag[:, :], start=True, stop=True)
                last.then_inc(hc_ps.sem, 1)

            def q_probT(u):
                wait(prob_ready, u)
                for n in range(4):
                    if n >= 2:
                        wait(probT_act if n % 2 == 0 else probT_dve, u, 1)
                    bank = 2 + n % 2
                    if n < 3:
                        transposes(bank, prob[:, n * BANK:(n + 1) * BANK], 4, probT_ps)
                    else:
                        nc.tensor.transpose(ps[0:MT, bank, 0:P], prob[:, n * BANK:M], ident).then_inc(probT_ps.sem, 1)

            def q_hq(u):
                wait(probT_act, u)
                wait(probT_dve, u)
                wait(ctx_in, u)
                for c in range(MC):
                    r = P if c < MC - 1 else MT
                    for b in range(2):
                        last = nc.tensor.matmul(ps[b * N:(b + 1) * N, 0, 0:D], probT[0:r, c, b * N:(b + 1) * N],
                                                ctxN[0:r, b, c, :], start=(c == 0), stop=(c == MC - 1))
                last.then_inc(hq_ps.sem, 1)

            def q_hqT(u):
                wait(hqn_ready, u)
                transposes(2, tmp, 2, hqT_ps)

            def q_xattn_proj(u):
                wait(feats_ready, u)
                for i in range(8):
                    src = hT[:, i] if i < 2 else featsT[:, i - 2]
                    last = nc.tensor.matmul(ps[:, 1, 0:D], src, wqv[:, i, :], start=(i == 0), stop=(i == 7))
                last.then_inc(xattn0_ps.sem, 1)

            def q_attn_proj(u):
                wait(ha_ready, u)
                transposes(4, h0[:, :], 2, haT_ps)
                wait(haT_ready, u)
                for w in range(2):
                    for c in range(DC):
                        for dc in range(DC):
                            last = nc.tensor.matmul(ps[:, 5, (2 * w + c) * P:(2 * w + c + 1) * P],
                                                    wqkp[:, dc, w, c * P:(c + 1) * P], hT[:, dc, :],
                                                    start=(dc == 0), stop=(dc == DC - 1))
                last.then_inc(qk_ps.sem, 1)
                wait(haTd_ready, u)
                for b in range(2):
                    for dc in range(DC):
                        last = nc.tensor.matmul(ps[:, 4, b * D:(b + 1) * D], hTd[:, dc, b], wv0[:, dc, :],
                                                start=(dc == 0), stop=(dc == DC - 1))
                last.then_inc(v_ps.sem, 1)

            def q_attn_scores(u):
                wait(qT_ready, u)
                wait(kbd0_pool, u)
                wait(kbd0_dve, u)
                core_scores(qT0, kbd0, False, 0, s0_ps)

            def q_attn_out(u):
                wait(e0_ready, u)
                core_transposes(P0, 2, pT0_ps)
                wait(pT0_act, u)
                wait(pT0_dve, u)
                wait(vb0_ready, u)
                core_values(PT0, vb0, False, 4, o0_ps)

            def hidden(u, n):
                if n >= 2:
                    wait(gelu_ready, u, n - 1)
                for hc in range(HC):
                    for dc in range(DC):
                        w = sw1[:, dc, hc * P:(hc + 1) * P] if n == 0 else rw1[:, dc, n - 1, hc * P:(hc + 1) * P]
                        last = nc.tensor.matmul(ps[:, n % 2, hc * P:(hc + 1) * P], w, hT[:, dc, :],
                                                start=(dc == 0), stop=(dc == DC - 1))
                last.then_inc(hid_ps.sem, 1)

            def output(u, n):
                if n >= 2:
                    wait(eout_used, u, n - 1)
                wait(gelu_ready, u, n + 1)
                if n == 0:
                    wait(gateT_ready, u)
                    nc.tensor.matmul(ps[:, 2, 0:D], wT9, ebias[:, :], start=True, stop=False)
                for hc in range(HC):
                    w = sw2[:, hc, :] if n == 0 else rw2[:, hc, n - 1, :]
                    last = nc.tensor.matmul(ps[:, 2 + n % 2, 0:D], h1T[:, n % 2, hc, :], w,
                                            start=(hc == 0 and n > 0), stop=(hc == HC - 1))
                last.then_inc(eout_ps.sem, 1)

            def q_route(u):
                wait(hf0_ready, u)
                transposes(4, h0[:, :], 2, hf0T_ps)
                wait(hf0T_ready, u)
                for dc in range(DC):
                    last = nc.tensor.matmul(ps[:, 5, 0:EXPERTS], hT[:, dc, :], wrout[:, dc, :],
                                            start=(dc == 0), stop=(dc == DC - 1))
                last.then_inc(router_ps.sem, 1)

            def q_gates(u):
                wait(gate_ready, u)
                nc.tensor.transpose(ps[0:EXPERTS + 1, 5, 0:P], w9[:, :], ident).then_inc(gateT_ps.sem, 1)

            def q_experts(u, first, last):
                for n in range(first, last):
                    output(u, n)
                    if n + 2 < 9:
                        hidden(u, n + 2)

            def p_scores(t):
                wait(h1_ready, t)
                transposes(6, hp, 2, h1T_ps)
                wait(h1T_ready, t)
                for c in range(DC):
                    for dc in range(DC):
                        last = nc.tensor.matmul(ps[:, 7, c * P:(c + 1) * P], wq1[:, dc, c * P:(c + 1) * P],
                                                hTp[:, dc, :], start=(dc == 0), stop=(dc == DC - 1))
                last.then_inc(qp_ps.sem, 1)
                wait(qp_ready, t)

                def each_piece(last, k):
                    last.then_inc(ctxT_used.sem, 1)

                wide_scores(qpT, each_piece)

            def p_mem(t):
                wait(mem_in, t)
                transposes(6, mem, 2, memT_ps)
                wait(memT_ready, t)
                wait(memTd_ready, t)
                for dc in range(DC):
                    nc.tensor.matmul(ps[:, 7, 0:P], wkrep[:, dc], memT[:, dc, :],
                                     start=(dc == 0), stop=(dc == DC - 1))
                for b in range(2):
                    for dc in range(DC):
                        last = nc.tensor.matmul(ps[:, 7, P + b * HD:P + (b + 1) * HD], memTd[:, dc, b], wv1[:, dc, :],
                                                start=(dc == 0), stop=(dc == DC - 1))
                last.then_inc(mkv_ps.sem, 1)

            def p_xattn_scores(t):
                wait(kbd1_ready, t)
                wait(vb1_ready, t)
                core_scores(qpT, kbd1, True, 6, s1_ps)

            def p_xattn_out(t):
                wait(e1_ready, t)
                core_transposes(P1, 6, pT1_ps)
                wait(pT1_act, t)
                wait(pT1_dve, t)
                core_values(PT1, vb1, True, 6, o1_ps)

            def p_xattn_proj(t):
                wait(o1_ready, t)
                transposes(7, hp, 2, o1T_ps)
                wait(o1T_ready, t)
                for dc in range(DC):
                    last = nc.tensor.matmul(ps[:, 6, 0:D], hTp[:, dc, :], wc1[:, dc, :],
                                            start=(dc == 0), stop=(dc == DC - 1))
                last.then_inc(xattn1_ps.sem, 1)

            def p_rot_proj(t):
                wait(hr_ready, t)
                transposes(7, hp, 2, hrT_ps)
                wait(hrT_ready, t)
                for dc in range(DC):
                    last = nc.tensor.matmul(ps[:, 6, :], hTp[:, dc, :], wqkv[:, dc, :],
                                            start=(dc == 0), stop=(dc == DC - 1))
                last.then_inc(qkv_ps.sem, 1)

            def p_rot_scores(t):
                wait(rot_ready, t)
                transposes(7, rot, 3, qkT_ps)
                wait(qkT_ready, t)
                wait(v1_ready, t)
                for b in range(2):
                    last = nc.tensor.matmul(ps[:, 6, b * N:(b + 1) * N], rqT[:, b].rearrange("p h n -> p (h n)"),
                                            rkT[:, b * N:(b + 1) * N], start=True, stop=True)
                last.then_inc(rs_ps.sem, 1)

            def p_rot_out(t):
                wait(rp_ready, t)
                nc.tensor.transpose(ps[:, 7, 0:P], P1[:, 0:P], ident).then_inc(rpT_ps.sem, 1)
                wait(rpT_ready, t)
                for b in range(2):
                    last = nc.tensor.matmul(ps[:, 6 + b, 0:P], vsb[b * N:(b + 1) * N, :],
                                            PT1[b * N:(b + 1) * N, 0, :], start=True, stop=True)
                last.then_inc(ro_ps.sem, 1)
                wait(ro_act, t)
                wait(ro_dve, t)
                for h in range(2):
                    last = nc.tensor.matmul(ps[:, 6, 0:D], PT1[:, 1 + h, :], wo[:, h, :], start=(h == 0), stop=(h == 1))
                last.then_inc(attn1_ps.sem, 1)

            def p_proto(t):
                wait(hg_ready, t)
                transposes(7, hp, 2, hgT_ps)
                wait(hgT_ready, t)
                for dc in range(DC):
                    last = nc.tensor.matmul(ps[:, 7, 2 * P:2 * P + PROTOS], hTp[:, dc, :], prot[:, dc, :],
                                            start=(dc == 0), stop=(dc == DC - 1))
                last.then_inc(dist_ps.sem, 1)
                for dc in range(DC):
                    last = nc.tensor.matmul(ps[:, 6, :], hTp[:, dc, :], bT[:, dc, :],
                                            start=(dc == 0), stop=(dc == DC - 1))
                last.then_inc(low_ps.sem, 1)

            def p_proto_out(t):
                wait(wt_ready, t)
                nc.tensor.transpose(ps[0:PROTOS, 7, 0:P], w32[:, :], ident).then_inc(wtT_ps.sem, 1)
                wait(wtT_ready, t)
                wait(low_ready, t)
                transposes(7, tmp1, 4, lowT_ps)
                wait(lowT_ready, t)
                nc.tensor.matmul(ps[:, 6, 0:D], wT32[:, :], pbias[:, :], start=True, stop=False)
                for c in range(4):
                    last = nc.tensor.matmul(ps[:, 6, 0:D], PT1[:, c, :], aT[:, c, :], start=False, stop=(c == 3))
                last.then_inc(ffn1_ps.sem, 1)

            def tile(t, u):
                if u is not None:
                    q_norm(u)
                if t is not None:
                    p_scores(t)
                if t is not None:
                    p_mem(t)
                if u is not None:
                    q_scores(u, t is None)
                if t is not None:
                    p_xattn_scores(t)
                if u is not None:
                    q_batt_max(u)
                    q_probT(u)
                if t is not None:
                    p_xattn_out(t)
                if u is not None:
                    q_batt_sum(u)
                    q_hq(u)
                    q_batt_mean(u)
                    q_hqT(u)
                if t is not None:
                    p_xattn_proj(t)
                if u is not None:
                    q_xattn_proj(u)
                if t is not None:
                    p_rot_proj(t)
                if u is not None:
                    q_attn_proj(u)
                if t is not None:
                    p_rot_scores(t)
                if u is not None:
                    q_attn_scores(u)
                if t is not None:
                    p_rot_out(t)
                if u is not None:
                    q_attn_out(u)
                    if t is None:
                        pe.wait_ge(ffn0_w_in.sem, 16 * 10)
                    q_route(u)
                if t is not None:
                    p_proto(t)
                if u is not None:
                    hidden(u, 0)
                    hidden(u, 1)
                    q_gates(u)
                    q_experts(u, 0, 3)
                if t is not None:
                    p_proto_out(t)
                if u is not None:
                    q_experts(u, 3, 9)

            setup_weights()
            setup_protos()
            tile(None, 0)
            pe.wait_ge(l1_w_in.sem, 16 * 17)
            with pe.Fori(0, TILES - 1) as t:
                tile(t, t + 1)
            tile(TILES - 1, None)

        @block.scalar
        def _(act):
            def wait(sig, tile, k=None):
                act.wait_ge(sig.sem, sig.at(tile, k))

            def copy(out, in_, sig):
                nc.scalar.copy(out, in_).then_inc(sig.sem, 1)

            def halves(bank):
                return ps[:, bank, 0:2 * P].rearrange("p (c n) -> p c n", c=2)

            def q_norm(u):
                wait(h0T_ps, u)
                copy(hT[:, :, :], halves(4), h0T_ready)

            def q_exp(u):
                wait(sim_max, u)
                nc.scalar.activation(prob, wide, ACT.Exp, bias=sq[:, 4:5], accum_out=sq[:, 5:6]).then_inc(prob_ready.sem, 1)

            def q_batt(u):
                wait(gmax_ready, u)
                nc.scalar.activation(sq[:, 8:9], sq[:, 6:7], ACT.Exp, bias=sq[:, 7:8]).then_inc(batt_ready.sem, 1)

            def q_probT(u):
                for n in (0, 2):
                    wait(probT_ps, u, n + 1)
                    copy(probT[:, 4 * n:4 * n + 4, :], ps[:, 2, :].rearrange("p (c n) -> p c n", c=4), probT_act)

            def q_attn_proj(u):
                wait(haT_ps, u)
                copy(hT[:, :, :], halves(4), haT_ready)
                wait(qk_ps, u)
                for c in range(DC):
                    nc.scalar.activation(kT0[:, c, :], ps[:, 5, (2 + c) * P:(3 + c) * P], ACT.Identity,
                                         bias=bqkp[:, 2 + c:3 + c]).then_inc(kT_ready.sem, 1)
                for c in range(DC):
                    nc.scalar.activation(qT0[:, c, :], ps[:, 5, c * P:(c + 1) * P], ACT.Identity,
                                         bias=bqkp[:, c:c + 1]).then_inc(qT_ready.sem, 1)

            def q_attn_scores(u):
                wait(d0_ready, u)
                nc.scalar.activation(P0, P0, ACT.Exp, scale=HD ** -0.5).then_inc(e0_ready.sem, 1)

            def q_attn_out(u):
                wait(pT0_ps, u, 1)
                copy(PT0[:, 0:4, :], ps[:, 2, :].rearrange("p (c n) -> p c n", c=4), pT0_act)

            def q_route(u):
                wait(hf0T_ps, u)
                copy(hT[:, :, :], halves(4), hf0T_ready)
                wait(rmax_ready, u)
                nc.scalar.activation(sq[:, 16:24], sq[:, 24:32], ACT.Exp, bias=sq[:, 4:5],
                                     accum_out=sq[:, 5:6]).then_inc(rexp_ready.sem, 1)

            def q_experts(u, first, end):
                for n in range(first, end):
                    wait(hid_ps, u, n + 1)
                    if n >= 2:
                        wait(eout_ps, u, n - 1)
                    for hc in range(HC):
                        k = n * HC + hc
                        last = nc.scalar.activation(h1T[:, n % 2, hc, :], ps[:, n % 2, hc * P:(hc + 1) * P], ACT.Gelu,
                                                    bias=hbias[:, k:k + 1])
                    last.then_inc(gelu_ready.sem, 1)

            def p_scores(t):
                wait(h1T_ps, t)
                copy(hTp[:, :, :], halves(6), h1T_ready)
                wait(qp_ps, t)
                copy(qpT[:, :, :], halves(7), qp_ready)

            def p_mem(t):
                wait(memT_ps, t)
                copy(memT[:, :, :], halves(6), memT_ready)

            def p_xattn_scores(t):
                wait(d1_ready, t)
                nc.scalar.activation(P1[:, :], P1[:, :], ACT.Exp, scale=HD ** -0.5).then_inc(e1_ready.sem, 1)

            def p_xattn_out(t):
                wait(pT1_ps, t, 1)
                copy(PT1[:, 0:4, :], ps[:, 6, :].rearrange("p (c n) -> p c n", c=4), pT1_act)

            def p_xattn_proj(t):
                wait(o1T_ps, t)
                copy(hTp[:, :, :], halves(7), o1T_ready)

            def p_rot_proj(t):
                wait(hrT_ps, t)
                copy(hTp[:, :, :], halves(7), hrT_ready)
                wait(rot_ready, t)
                copy(vsb[:, :], ps[:, 6, 384:512], v1_ready)

            def p_rot_scores(t):
                wait(qkT_ps, t)
                copy(rqT, ps[:, 7, 0:2 * P].rearrange("p (h b n) -> p b h n", h=2, b=2), qkT_ready)
                copy(rkT, ps[:, 7, 2 * P:3 * P], qkT_ready)
                wait(rd_ready, t)
                nc.scalar.activation(P1[:, 0:P], P1[:, 0:P], ACT.Exp, scale=K1 ** -0.5).then_inc(re_ready.sem, 1)

            def p_rot_out(t):
                wait(rpT_ps, t)
                copy(PT1[:, 0, :], ps[:, 7, 0:P], rpT_ready)
                wait(ro_ps, t)
                copy(PT1[:, 1:3, 0:N], ps[:, 6, 0:P].rearrange("p (h n) -> p h n", h=2), ro_act)

            def p_proto(t):
                wait(hgT_ps, t)
                copy(hTp[:, :, :], halves(7), hgT_ready)
                wait(fs_ready, t)
                nc.scalar.activation(w32[:, :], sp_[:, 0:PROTOS], ACT.Exp, bias=sp_[:, 40:41],
                                     accum_out=sp_[:, 41:42]).then_inc(fe_ready.sem, 1)

            def p_proto_out(t):
                wait(wtT_ps, t)
                copy(wT32[:, :], ps[0:PROTOS, 7, 0:P], wtT_ready)
                wait(lowT_ps, t)
                copy(PT1[:, 0:4, :], ps[:, 7, :].rearrange("p (c n) -> p c n", c=4), lowT_ready)

            def tile(t, u):
                if u is not None:
                    q_norm(u)
                if t is not None:
                    p_scores(t)
                if t is not None:
                    p_mem(t)
                    p_xattn_scores(t)
                if u is not None:
                    q_exp(u)
                    q_batt(u)
                    q_probT(u)
                if t is not None:
                    p_xattn_out(t)
                    p_xattn_proj(t)
                    p_rot_proj(t)
                if u is not None:
                    q_attn_proj(u)
                if t is not None:
                    p_rot_scores(t)
                if u is not None:
                    q_attn_scores(u)
                if t is not None:
                    p_rot_out(t)
                if u is not None:
                    q_attn_out(u)
                    q_route(u)
                if t is not None:
                    p_proto(t)
                if u is not None:
                    q_experts(u, 0, 5)
                if t is not None:
                    p_proto_out(t)
                if u is not None:
                    q_experts(u, 5, 9)

            act.wait_ge(const_in.sem, 16 * N_CONST)
            act.wait_ge(setup_done.sem, 1)
            tile(None, 0)
            with act.Fori(0, TILES - 1) as t:
                tile(t, t + 1)
            tile(TILES - 1, None)

        @block.vector
        def _(dve):
            v = nc.vector
            ql = Chain(dve, q_chain.sem, q_chain.per)
            pl = Chain(dve, p_chain.sem, p_chain.per)

            def wait(sig, tile, k=None):
                dve.wait_ge(sig.sem, sig.at(tile, k))

            def sync(ins, sig, tile, k=None):
                ins.then_inc(sig.sem, 1)
                wait(sig, tile, k)

            def layernorm(link, tile, col, x, h, var_sig, rstd_sig):
                link(v.bn_stats(col[:, 50:56], x), settle)
                link(v.bn_aggr(col[:, 56:58], col[:, 50:56]))
                v.tensor_scalar(col[:, 57:58], col[:, 57:58], EPS, None, ALU.add).then_inc(var_sig.sem, 1)
                wait(rstd_sig, tile)
                return v.tensor_scalar(h, x, col[:, 56:57], col[:, 58:59], ALU.subtract, ALU.mult)

            def heads(ap):
                return ap.rearrange("p (h m) -> p h m", h=HEADS)

            def each_head(col, n):
                return col[:, :].unsqueeze(2).to_broadcast([P, HEADS, n])

            def q_norm(u):
                ql.begin(u)
                wait(x_in, u)
                layernorm(ql, u, sq, xin[:, :], h0[:, :], x0_var, x0_rstd).then_inc(h0_ready.sem, 1)
                wait(h0T_ready, u)
                for dc in range(DC):
                    v.tensor_scalar(simq[:, dc, :], hT[:, dc, :], wsim[:, 4 + dc:5 + dc],
                                    wsim[:, 2 + dc:3 + dc], ALU.mult, ALU.add).then_inc(simq_ready.sem, 1)

            def q_scores(u):
                wait(sim_ps, u)
                ql(v.reduce_max(sq[:, 3:4], wide, AX.X))
                v.tensor_scalar(sq[:, 4:5], sq[:, 3:4], -1.0, None, ALU.mult).then_inc(sim_max.sem, 1)
                wait(own_ps, u)
                ql(v.tensor_scalar(sq[:, 6:7], ps[:, 4, 0:1], sq[:, 3:4], bsim, ALU.add, ALU.add))
                v.tensor_scalar(diag[:, :], ident, sq[:, 6:7], None, ALU.mult).then_inc(diag_ready.sem, 1)

            def q_batt_max(u):
                wait(rowmax_ps, u)
                for b in range(2):
                    i = slice(b * N, (b + 1) * N)
                    ql(v.reduce_max(sq[i, 9:10], ps[i, 5, b * N:(b + 1) * N], AX.X))
                v.tensor_scalar(sq[:, 7:8], sq[:, 9:10], -1.0, None, ALU.mult).then_inc(gmax_ready.sem, 1)

            def q_batt(u):
                wait(battz_ps, u)
                ql(v.reciprocal(sq[:, 10:11], ps[:, 5, P:P + 1]))
                ql(v.tensor_tensor(sq[:, 12:13], sq[:, 10:11], sq[:, 8:9], ALU.mult))
                v.tensor_scalar(diag[:, :], blockmask, sq[:, 12:13], None, ALU.mult).then_inc(battw_ready.sem, 1)

            def q_probT(u):
                wait(probT_ps, u, 2)
                v.tensor_copy(probT[:, 4:8, :], ps[:, 3, :].rearrange("p (c n) -> p c n", c=4)).then_inc(probT_dve.sem, 1)
                wait(probT_ps, u, 4)
                v.tensor_copy(probT[0:MT, MC - 1, :], ps[0:MT, 3, 0:P]).then_inc(probT_dve.sem, 1)

            def q_normalize(u):
                ql(v.reciprocal(sq[:, 11:12], sq[:, 5:6]))
                wait(hq_ps, u)
                v.tensor_scalar(tmp[:, :], ps[:, 0, 0:D], sq[:, 11:12], None, ALU.mult).then_inc(hqn_ready.sem, 1)

            def q_feats(u):
                hq = ps[:, 2, 0:2 * P].rearrange("p (c n) -> p c n", c=DC)
                hc = ps[:, 5, 2 * P:4 * P].rearrange("p (c n) -> p c n", c=DC)
                wait(hqT_ps, u)
                v.tensor_copy(featsT[:, 0:2, :], hq)
                v.tensor_tensor(featsT[:, 2:4, :], hq, hT[:, :, :], ALU.mult)
                wait(hc_ps, u)
                v.tensor_tensor(featsT[:, 4:6, :], hc, hT[:, :, :], ALU.mult).then_inc(feats_ready.sem, 1)

            def q_xattn_proj(u):
                wait(xattn0_ps, u)
                ql(v.tensor_tensor(tmp[:, :], ps[:, 1, 0:D], bqv, ALU.add))
                ql(v.tensor_tensor(xq[:, :], tmp[:, :], xin[:, :], ALU.add))

            def q_attn_proj(u):
                layernorm(ql, u, sq, xq[:, :], h0[:, :], xa_var, xa_rstd).then_inc(ha_ready.sem, 1)
                wait(haT_ready, u)
                for dc in range(DC):
                    src = hT[:, dc, :].rearrange("p (b n) -> p b n", b=2)
                    v.tensor_copy(hTd[:, dc], src.unsqueeze(2).to_broadcast([P, 2, 2, N])).then_inc(haTd_ready.sem, 1)
                wait(v_ps, u)
                for b in range(2):
                    src = ps[:, 4, b * D:(b + 1) * D].rearrange("p (g h e) -> p g h e", g=8, h=2)
                    v.tensor_tensor(vb0[:, b], src, halfmask.unsqueeze(1).unsqueeze(3).to_broadcast([P, 8, 2, HD]),
                                    ALU.mult).then_inc(vb0_ready.sem, 1)
                wait(kT_ready, u)
                block_keys(v, kbd0[:, 1], kT0[:, 1, :]).then_inc(kbd0_dve.sem, 1)

            def core_softmax(link, tile, s_sig, bank, mx, prb, d_sig):
                wait(s_sig, tile)
                sc = ps[:, bank:bank + 2, :].rearrange("p c (h m) -> p (c h) m", m=N)
                link(v.tensor_reduce(mx[:, :], sc, AX.X, ALU.max))
                v.tensor_tensor(heads(prb), sc, each_head(mx, N), ALU.subtract).then_inc(d_sig.sem, 1)

            def core_sums(link, tile, e_sig, prb, rs):
                wait(e_sig, tile)
                link(v.tensor_reduce(rs[:, :], heads(prb), AX.X, ALU.add))
                link(v.reciprocal(rs[:, :], rs[:, :]))

            def q_attn_scores(u):
                core_softmax(ql, u, s0_ps, 0, mx0, P0, d0_ready)

            def q_attn_out(u):
                core_sums(ql, u, e0_ready, P0, rs0)
                wait(pT0_ps, u, 2)
                v.tensor_copy(PT0[:, 4:8, :], ps[:, 3, :].rearrange("p (c n) -> p c n", c=4)).then_inc(pT0_dve.sem, 1)
                wait(o0_ps, u)
                ql(v.tensor_tensor(heads(tmp[:, :]), heads(ps[:, 4, 0:D]), each_head(rs0, HD), ALU.mult))
                ql(v.tensor_tensor(tmp[:, :], tmp[:, :], bv, ALU.add))
                ql(v.tensor_tensor(xq[:, :], xq[:, :], tmp[:, :], ALU.add))

            def top_two(link, values, ext, tp, tv, rst):
                link(v.max(tp[:, :], values))
                link(v.tensor_copy(tv[:, 0:2], tp[:, 0:2]), settle)
                link(v.match_replace(rst[:, :], tv[:, :], ext[:, :], 0.0))

            def q_route(u):
                layernorm(ql, u, sq, xq[:, :], h0[:, :], xf_var, xf_rstd).then_inc(hf0_ready.sem, 1)
                wait(router_ps, u)
                ql(v.tensor_tensor(sq[:, 24:32], ps[:, 5, 0:EXPERTS], rb, ALU.add))
                ql(v.reduce_max(sq[:, 3:4], sq[:, 24:32], AX.X))
                v.tensor_scalar(sq[:, 4:5], sq[:, 3:4], -1.0, None, ALU.mult).then_inc(rmax_ready.sem, 1)
                wait(rexp_ready, u)
                ql(v.reciprocal(sq[:, 10:11], sq[:, 5:6]))
                ql(v.tensor_scalar(pext[:, 0:8], sq[:, 16:24], sq[:, 10:11], None, ALU.mult), settle)
                top_two(ql, pext[:, 0:8], pext, top, topv, rest)

            def q_gates(u):
                sync(v.tensor_tensor(w9[:, 0:8], pext[:, 0:8], rest[:, 0:8], ALU.subtract), gate_ready, u)
                wait(gateT_ps, u)
                v.tensor_copy(wT9, ps[0:EXPERTS + 1, 5, 0:P]).then_inc(gateT_ready.sem, 1)

            def q_experts(u, first, end):
                for n in range(first, end):
                    wait(eout_ps, u, n + 1)
                    dst = xp if n == 8 else xq
                    bank = ps[:, 2 + n % 2, 0:D]
                    if n == 0:
                        ins = v.tensor_tensor(dst[:, :], bank, xq[:, :], ALU.add)
                    else:
                        ins = v.scalar_tensor_tensor(dst[:, :], bank, w9[:, n - 1:n], xq[:, :], ALU.mult, ALU.add)
                    sync(ins, eout_used, u, n + 1)

            def p_scores(t):
                pl.begin(t)
                layernorm(pl, t, sp_, xp[:, :], hp[:, :], x1_var, x1_rstd).then_inc(h1_ready.sem, 1)
                dve.wait_ge(ctxT_used.sem, settle(dve, ctxT_used.at(t)))
                pl(v.max(am[:, :], wide), settle)
                sync(v.max_index(ai[:, :], am[:, :], wide), amax_done, t)
                v.tensor_scalar(gidx[:, :], ai[:, 0:1], offs[:, 0:1], None, ALU.add).then_inc(gidx_ready.sem, 1)

            def p_mem(t):
                wait(gidx_ready, t)
                pl(v.tensor_scalar(offs[:, :], offs[:, :], float(2 * M), None, ALU.add))
                wait(memT_ready, t)
                for dc in range(DC):
                    src = memT[:, dc, :].rearrange("p (b n) -> p b n", b=2)
                    v.tensor_copy(memTd[:, dc], src.unsqueeze(2).to_broadcast([P, 2, 2, N])).then_inc(memTd_ready.sem, 1)
                wait(mkv_ps, t)
                src = ps[:, 7, P:P + 2 * HD].rearrange("p (b e) -> p b e", b=2)
                v.tensor_tensor(vb1[:, :, :, :], src.unsqueeze(2).to_broadcast([P, 2, 2, HD]),
                                halfmask.unsqueeze(1).unsqueeze(3).to_broadcast([P, 2, 2, HD]), ALU.mult
                                ).then_inc(vb1_ready.sem, 1)
                block_keys(v, kbd1, ps[:, 7, 0:P]).then_inc(kbd1_ready.sem, 1)

            def p_xattn_scores(t):
                core_softmax(pl, t, s1_ps, 6, mx1, P1[:, :], d1_ready)

            def p_xattn_out(t):
                core_sums(pl, t, e1_ready, P1[:, :], rs1)
                wait(pT1_ps, t, 2)
                v.tensor_copy(PT1[:, 4:8, :], ps[:, 7, :].rearrange("p (c n) -> p c n", c=4)).then_inc(pT1_dve.sem, 1)
                wait(o1_ps, t)
                v.tensor_tensor(heads(hp[:, :]), heads(ps[:, 6, 0:D]), each_head(rs1, HD), ALU.mult).then_inc(o1_ready.sem, 1)

            def p_xattn_proj(t):
                wait(xattn1_ps, t)
                pl(v.tensor_tensor(xp[:, :], ps[:, 6, 0:D], xp[:, :], ALU.add))

            def p_rot_proj(t):
                layernorm(pl, t, sp_, xp[:, :], hp[:, :], xr_var, xr_rstd).then_inc(hr_ready.sem, 1)
                wait(qkv_ps, t)
                qk = ps[:, 6, 0:384].rearrange("p (j k two) -> p j k two", j=3, two=2)
                other = tmp1[:, 0:384].rearrange("p (j k two) -> p j k two", j=3, two=2)
                sn = sin.rearrange("p (k two) -> p k two", two=2)
                for e in range(2):
                    v.tensor_tensor(other[:, :, :, e], qk[:, :, :, 1 - e],
                                    sn[:, :, e].unsqueeze(1).to_broadcast([P, 3, K1 // 2]), ALU.mult)
                pl(v.tensor_tensor(rot.rearrange("p (j k) -> p j k", j=3), ps[:, 6, 0:384].rearrange("p (j k) -> p j k", j=3),
                                   cos.unsqueeze(1).to_broadcast([P, 3, K1]), ALU.mult))
                v.tensor_tensor(rot, rot, tmp1[:, 0:384], ALU.add).then_inc(rot_ready.sem, 1)

            def p_rot_scores(t):
                wait(rs_ps, t)
                pl(v.tensor_tensor(rprob, ps[:, 6, 0:P].rearrange("p (b n) -> p b n", b=2),
                                   causal.unsqueeze(1).to_broadcast([P, 2, N]), ALU.add))
                pl(v.tensor_reduce(sp_[:, 0:2], rprob, AX.X, ALU.max))
                v.tensor_tensor(rprob, rprob, sp_[:, 0:2].unsqueeze(2).to_broadcast([P, 2, N]), ALU.subtract
                                ).then_inc(rd_ready.sem, 1)

            def p_rot_out(t):
                wait(re_ready, t)
                pl(v.tensor_reduce(sp_[:, 2:4], rprob, AX.X, ALU.add))
                pl(v.reciprocal(sp_[:, 4:6], sp_[:, 2:4]))
                v.tensor_tensor(rprob, rprob, sp_[:, 4:6].unsqueeze(2).to_broadcast([P, 2, N]), ALU.mult
                                ).then_inc(rp_ready.sem, 1)
                wait(ro_ps, t)
                v.tensor_copy(PT1[:, 1:3, N:2 * N], ps[:, 7, 0:P].rearrange("p (h n) -> p h n", h=2)).then_inc(ro_dve.sem, 1)
                wait(attn1_ps, t)
                pl(v.tensor_tensor(xp[:, :], ps[:, 6, 0:D], xp[:, :], ALU.add))

            def p_proto(t):
                sync(layernorm(pl, t, sp_, xp[:, :], hp[:, :], xg_var, xg_rstd), hg_ready, t)
                pl(v.tensor_tensor_reduce(tmp1[:, 0:D], hp[:, :], hp[:, :], 1.0, 0.0, ALU.mult, ALU.add, sp_[:, 42:43]))
                wait(dist_ps, t)
                dst = sp_[:, 0:PROTOS]
                pl(v.scalar_tensor_tensor(dst, ps[:, 7, 2 * P:2 * P + PROTOS], -2.0, p2[:, :], ALU.mult, ALU.add))
                v.tensor_scalar(dst, dst, sp_[:, 42:43], 0.0, ALU.add, ALU.max).then_inc(d2_ready.sem, 1)
                wait(root_ready, t)
                pl(v.tensor_scalar(dst, dst, tneg[:, 0:1], None, ALU.mult))
                pl(v.reduce_max(sp_[:, 43:44], dst, AX.X))
                v.tensor_scalar(sp_[:, 40:41], sp_[:, 43:44], -1.0, None, ALU.mult).then_inc(fs_ready.sem, 1)

            def p_proto_gates(t):
                wait(fe_ready, t)
                pl(v.reciprocal(sp_[:, 44:45], sp_[:, 41:42]))
                pl(v.tensor_scalar(wf[:, 0:PROTOS], w32[:, :], sp_[:, 44:45], None, ALU.mult), settle)
                top_two(pl, wf[:, 0:PROTOS], wf, topf, topvf, restf)
                pl(v.tensor_tensor(w32[:, :], wf[:, 0:PROTOS], restf[:, 0:PROTOS], ALU.subtract))
                pl(v.tensor_tensor(sp_[:, 45:46], topf[:, 0:1], topf[:, 1:2], ALU.add))
                pl(v.reciprocal(sp_[:, 46:47], sp_[:, 45:46]))
                sync(v.tensor_scalar(w32[:, :], w32[:, :], sp_[:, 46:47], None, ALU.mult), wt_ready, t)
                wait(low_ps, t)
                v.tensor_tensor(tmp1[:, :].rearrange("p (k r) -> p k r", r=RANK),
                                ps[:, 6, :].rearrange("p (k r) -> p k r", r=RANK),
                                w32[:, :].unsqueeze(2).to_broadcast([P, PROTOS, RANK]), ALU.mult).then_inc(low_ready.sem, 1)

            def p_proto_out(t):
                wait(ffn1_ps, t)
                v.tensor_tensor(xo[:, :], ps[:, 6, 0:D], xp[:, :], ALU.add).then_inc(out_ready.sem, 1)
                pl.end()

            def tile(t, u):
                if u is not None:
                    q_norm(u)
                if t is not None:
                    p_scores(t)
                if t is not None:
                    p_mem(t)
                if u is not None:
                    q_scores(u)
                if t is not None:
                    p_xattn_scores(t)
                if u is not None:
                    q_batt_max(u)
                    q_probT(u)
                if t is not None:
                    p_xattn_out(t)
                if u is not None:
                    q_batt(u)
                    q_normalize(u)
                if t is not None:
                    p_xattn_proj(t)
                if u is not None:
                    q_feats(u)
                if t is not None:
                    p_rot_proj(t)
                if u is not None:
                    q_xattn_proj(u)
                    q_attn_proj(u)
                if t is not None:
                    p_rot_scores(t)
                if u is not None:
                    q_attn_scores(u)
                if t is not None:
                    p_rot_out(t)
                if u is not None:
                    q_attn_out(u)
                    q_route(u)
                if t is not None:
                    p_proto(t)
                if u is not None:
                    q_gates(u)
                if t is not None:
                    p_proto_gates(t)
                if u is not None:
                    q_experts(u, 0, 3)
                if t is not None:
                    p_proto_out(t)
                if u is not None:
                    q_experts(u, 3, 9)
                    ql.end()

            v.memset(headw, 0.0).then_inc(headw_zero.sem, 1)
            v.memset(pext[:, :], -1.0)
            v.memset(topv[:, :], -1.0)
            v.memset(wf[:, :], -1.0)
            v.memset(topvf[:, :], -1.0)
            v.memset(w9[:, :], 1.0)
            v.memset(h0[:, :], 1.0).then_inc(sets_dve.sem, 1)
            dve.wait_ge(sets_dve.sem, 1)
            dve.wait_ge(const_in.sem, 16 * N_CONST)
            v.tensor_copy(offs[:, :], offs0)
            v.tensor_scalar(sp_[:, 1:2], temp, -1.0, None, ALU.mult).then_inc(sets_dve.sem, 1)
            dve.wait_ge(sets_dve.sem, 2)
            dve.wait_ge(l1_w_in.sem, 16 * 17)
            v.tensor_tensor(tmp1[:, 0:DC * PROTOS].rearrange("p (c n) -> p c n", c=DC), prot[:, :, :], prot[:, :, :],
                            ALU.mult).then_inc(sets_dve.sem, 1)
            dve.wait_ge(setup_mm.sem, 1)
            for w in range(2):
                v.tensor_copy(wqkp[:, :, w, :], ps[:, w, :].rearrange("p (c n) -> p c n", c=DC))
            v.tensor_copy(bqkp[:, :], ps[:, 2, 0:4])
            dve.wait_ge(setup_mm.sem, 2)
            v.tensor_copy(p2[:, :], ps[:, 3, 0:PROTOS]).then_inc(sets_dve.sem, 1)
            dve.wait_ge(sets_dve.sem, 4)
            v.tensor_tensor(sp_[:, 2:3], temp, sp_[:, 1:2], ALU.max).then_inc(sets_dve.sem, 1)
            dve.wait_ge(sets_dve.sem, 5)
            v.tensor_scalar(tneg[:, :], sp_[:, 2:3], 0.1, None, ALU.max).then_inc(sets_dve.sem, 1)
            dve.wait_ge(sets_dve.sem, 6)
            v.reciprocal(sp_[:, 0:1], tneg[:, :]).then_inc(sets_dve.sem, 1)
            dve.wait_ge(sets_dve.sem, 7)
            v.tensor_scalar(tneg[:, :], sp_[:, 0:1], -1.0, None, ALU.mult).then_inc(setup_done.sem, 1)
            tile(None, 0)
            with dve.Fori(0, TILES - 1) as t:
                tile(t, t + 1)
                wait(out_stored, t)
            tile(TILES - 1, None)

        @block.gpsimd
        def _(pool):
            def q_keys(u):
                pool.wait_ge(kT_ready.sem, kT_ready.at(u))
                block_keys(nc.gpsimd, kbd0[:, 0], kT0[:, 0, :]).then_inc(kbd0_pool.sem, 1)

            def p_gather(t):
                pool.wait_ge(gidx_ready.sem, settle(pool, gidx_ready.at(t)))
                pool.indirect_dma_start(mem[:, :], None, ctx_rows.rearrange("b m d -> (b m) d"),
                                        bass.IndirectOffsetOnAxis(gidx[:, 0:1], 0)).then_inc(mem_in.sem, 16)

            def rstd(col, tile, var_sig, rstd_sig):
                pool.wait_ge(var_sig.sem, var_sig.at(tile))
                nc.gpsimd.tensor_tensor(col[:, 58:59], col[:, 57:58], minus_half, ALU.pow).then_inc(rstd_sig.sem, 1)

            def p_root(t):
                pool.wait_ge(d2_ready.sem, d2_ready.at(t))
                nc.gpsimd.tensor_tensor(sp_[:, 0:PROTOS], sp_[:, 0:PROTOS], half.to_broadcast([P, PROTOS]),
                                        ALU.pow).then_inc(root_ready.sem, 1)

            def tile(t, u):
                if u is not None:
                    rstd(sq, u, x0_var, x0_rstd)
                if t is not None:
                    rstd(sp_, t, x1_var, x1_rstd)
                    p_gather(t)
                    rstd(sp_, t, xr_var, xr_rstd)
                if u is not None:
                    rstd(sq, u, xa_var, xa_rstd)
                    q_keys(u)
                    rstd(sq, u, xf_var, xf_rstd)
                if t is not None:
                    rstd(sp_, t, xg_var, xg_rstd)
                    p_root(t)

            pool.wait_ge(const_in.sem, 16 * N_CONST)
            tile(None, 0)
            with pool.Fori(0, TILES - 1) as t:
                tile(t, t + 1)
            tile(TILES - 1, None)


def constants():
    c = np.zeros((P, C_END), np.float32)
    p = np.arange(P)
    c[:, C_ID:C_ID + P] = np.eye(P)
    c[:, C_BLK:C_BLK + P] = p[:, None] // N == p[None] // N
    c[:, C_HEAD:C_HEAD + H8] = p[:, None] // HD == np.arange(H8)[None]
    c[:, C_HALF:C_HALF + 2] = p[:, None] // N == np.arange(2)[None]
    theta = np.float32(10000.0) ** (np.float32(-2.0) * np.arange(0, K1, 2, dtype=np.float32) / np.float32(K1))
    angle = (p % N).astype(np.float32)[:, None] * theta[None]
    c[:, C_COS:C_COS + K1] = np.repeat(np.cos(angle), 2, 1)
    c[:, C_SIN:C_SIN + K1] = np.stack([-np.sin(angle), np.sin(angle)], 2).reshape(P, K1)
    c[:, C_CAUSAL:C_CAUSAL + N] = np.where(np.arange(N)[None] <= (p % N)[:, None], 0.0, NEG)
    c[:, C_ONES:C_ONES + P] = 1.0
    c[:, C_OFFS] = p // N * M
    c[:, C_EXP:C_EXP + 2] = -0.5, 0.5
    return c


_AS_IS = ['x', 'ctx_1024', 'L0_xattn_W_qv', 'L0_attn_Wv', 'L0_attn_Wp', 'L0_ffn_router_w', 'L0_ffn_sw1', 'L0_ffn_sw2',
          'L0_ffn_rw1', 'L0_ffn_rw2', 'L1_ffn_bias']


def kernel(**inputs):
    import numpy as _np
    import concourse.bacc as _bacc
    from concourse import mybir as _mybir
    from concourse.bass_utils import run_bass_kernel_spmd as _run

    i = {k: _np.asarray(v) for k, v in inputs.items()}
    laid = {k: i[k] for k in _AS_IS}
    laid["consts"] = constants()
    laid["ctxT"] = i['ctx_1024'].transpose(0, 2, 1)
    hidden = _np.concatenate([i['L0_ffn_sb1'][None], i['L0_ffn_rb1']], 0)
    laid["cols"] = _np.concatenate([
        i['L0_xattn_w_sim'].reshape(6, P).T, i['L0_attn_bq'].reshape(2, P).T, i['L0_attn_bk'].reshape(2, P).T,
        _np.broadcast_to(i['L0_xattn_b_sim'].reshape(1, 1), (P, 1)), hidden.reshape(9 * HC, P).T,
        _np.broadcast_to(i['L1_ffn_temp'].reshape(1, 1), (P, 1))], 1)
    laid["rows"] = _np.broadcast_to(_np.concatenate([i['L0_xattn_b_qv'], i['L0_attn_bv'], i['L0_ffn_router_b']])[None],
                                    (P, 2 * D + EXPERTS))
    laid["ebias"] = _np.concatenate([i['L0_ffn_rb2'], i['L0_ffn_sb2'][None]], 0)
    laid["wq0T"], laid["wk0T"] = i['L0_attn_Wq'].T, i['L0_attn_Wk'].T
    laid["wq1T"], laid["wkv1T"], laid["wc1T"] = i['L1_xattn_Wq'].T, i['L1_xattn_Wkv'].T, i['L1_xattn_Wc'].T
    laid["wqkvT"] = _np.concatenate([i['L1_attn_Wq'].reshape(2 * K1, D), i['L1_attn_Wk'], i['L1_attn_Wv']], 0).T
    laid["woT"] = i['L1_attn_Wo'].T
    laid["protT"] = i['L1_ffn_prototypes'].T
    laid["bT"] = i['L1_ffn_B'].reshape(PROTOS * RANK, D).T
    laid["aT"] = i['L1_ffn_A'].transpose(0, 2, 1).reshape(PROTOS * RANK, D)

    nc = _bacc.Bacc("TRN2", target_bir_lowering=False, num_devices=1)
    arrays, aps = {}, {}
    for name, arr in laid.items():
        arr = _np.ascontiguousarray(arr)
        arrays[f"in_{name}"] = arr
        aps[name] = nc.dram_tensor(f"in_{name}", arr.shape, _mybir.dt.from_np(arr.dtype), kind="ExternalInput").ap()
    aps["out"] = nc.dram_tensor("out_0", (B, N, D), F32, kind="ExternalOutput").ap()
    build(nc, aps)
    r = _run(nc, [arrays], core_ids=[0])
    return r.results[0]["out_0"]
```

```python
from contextlib import ExitStack

import numpy as np
import concourse.bass as bass
from concourse import mybir

P = 128
B, N, D = 32, 64, 256
M = 1601
TILES = B * N // P
DC = D // P
MC = -(-M // P)
MT = M - (MC - 1) * P
BANK = 512
HEADS, HD = 16, 16
H8 = P // HD
EXPERTS, HID = 8, 512
HC = HID // P
PROTOS, RANK = 32, 16
K1 = 128
F32, U32 = mybir.dt.float32, mybir.dt.uint32
ALU, ACT, AX = mybir.AluOpType, mybir.ActivationFunctionType, mybir.AxisListType
EPS = 1e-5
NEG = -1.0e30

C_ID, C_BLK, C_HEAD, C_HALF = 0, 128, 256, 264
C_COS, C_SIN, C_CAUSAL, C_ONES, C_OFFS, C_EXP, C_END = 266, 266 + 128, 266 + 256, 266 + 320, 266 + 448, 266 + 449, 266 + 451


class Signal:

    def __init__(self, sem, per=1):
        self.sem, self.per = sem, per

    def at(self, tile, k=None):
        return tile * self.per + (self.per if k is None else k)


class Chain:

    def __init__(self, eng, sem, per):
        self.eng, self.sem, self.per, self.tile, self.n = eng, sem, per, None, 0

    def begin(self, tile):
        self.tile, self.n = tile, 0

    def __call__(self, ins, before_wait=None):
        self.n += 1
        ins.then_inc(self.sem, 1)
        value = self.tile * self.per + self.n
        if before_wait:
            value = before_wait(self.eng, value)
        self.eng.wait_ge(self.sem, value)

    def end(self):
        assert self.n == self.per, self.n


def build(nc, a):
    ctx = ExitStack()
    with ctx:
        def sb(name, shape, dt=F32):
            return ctx.enter_context(nc.sbuf_tensor(name, shape, dt))

        def S(name, per=1):
            return Signal(ctx.enter_context(nc.semaphore(name)), per)

        ps = ctx.enter_context(nc.psum_tensor("ps", [P, 8, BANK], F32))
        wide = ps[:, 0:4, :].rearrange("p a b -> p (a b)")[:, 0:M]

        con = sb("con", [P, C_END])
        ident, blockmask = con[:, C_ID:C_ID + P], con[:, C_BLK:C_BLK + P]
        headmask, halfmask = con[:, C_HEAD:C_HEAD + H8], con[:, C_HALF:C_HALF + 2]
        cos, sin = con[:, C_COS:C_COS + K1], con[:, C_SIN:C_SIN + K1]
        causal, ones = con[:, C_CAUSAL:C_CAUSAL + N], con[:, C_ONES:C_ONES + P]
        offs0 = con[:, C_OFFS:C_OFFS + 1]
        minus_half, half = con[:, C_EXP:C_EXP + 1], con[:, C_EXP + 1:C_EXP + 2]
        cols = sb("cols", [P, 6 + 4 + 1 + 36 + 1])
        wsim, bqk, bsim = cols[:, 0:6], cols[:, 6:10], cols[:, 10:11]
        hbias, temp = cols[:, 11:47], cols[:, 47:48]
        rows = sb("rows", [P, 2 * D + EXPERTS])
        bqv, bv, rb = rows[:, 0:D], rows[:, D:2 * D], rows[:, 2 * D:]
        wqv = sb("wqv", [P, 4 * DC, D])
        wqkp = sb("wqkp", [P, DC, 2, D])
        wv0 = sb("wv0", [P, DC, D])
        wrout = sb("wrout", [P, DC, EXPERTS])
        sw1 = sb("sw1", [P, DC, HID])
        sw2 = sb("sw2", [P, HC, D])
        rw1 = sb("rw1", [P, DC, EXPERTS, HID])
        rw2 = sb("rw2", [P, HC, EXPERTS, D])
        ebias = sb("ebias", [EXPERTS + 1, D])
        wq1 = sb("wq1", [P, DC, D])
        wkrep = sb("wkrep", [P, DC, H8, HD])
        wv1 = sb("wv1", [P, DC, HD])
        wc1 = sb("wc1", [P, DC, D])
        wqkv = sb("wqkv", [P, DC, 4 * K1])
        wo = sb("wo", [P, 2, D])
        prot = sb("prot", [P, DC, PROTOS])
        bT = sb("bT", [P, DC, PROTOS * RANK])
        aT = sb("aT", [P, 4, D])
        pbias = sb("pbias", [PROTOS, D])
        p2 = sb("p2", [P, PROTOS])
        tneg = sb("tneg", [P, 1])
        bqkp = sb("bqkp", [P, 4])

        ctxN = sb("ctxN", [P, 2, MC, D])
        ctxT = sb("ctxT", [P, DC, 2, M])
        share = sb("share", [P, M + MC * P])
        prob, probT = share[:, 0:M], share[:, M:].rearrange("p (c n) -> p c n", c=MC)
        P0, PT0 = share[:, 0:1024], share[:, 1024:2048].rearrange("p (g n) -> p g n", g=8)
        kbd0 = share[:, 1024:3072].rearrange("p (c b h n) -> p c b h n", c=DC, b=2, h=H8)
        hfT = sb("hfT", [P, DC, P])
        h1T = sb("h1T", [P, 2, HC, P])

        xin, xq, xf, xl, xp = (sb(n, [P, D]) for n in ("xin", "xq", "xf", "xl", "xp"))
        h0 = sb("h0", [P, D])
        hT = sb("hT", [P, DC, P])
        turns = sb("turns", [P, 8 * P])
        tmp = turns[:, 0:D]
        simq = turns[:, 0:DC * P].rearrange("p (c n) -> p c n", c=DC)
        featsT = turns[:, 2 * P:8 * P].rearrange("p (i n) -> p i n", i=6)
        hTd = turns[:, 0:4 * P].rearrange("p (c b e n) -> p c b e n", c=DC, b=2, e=2)
        qT0 = turns[:, 4 * P:6 * P].rearrange("p (c n) -> p c n", c=DC)
        kT0 = turns[:, 6 * P:8 * P].rearrange("p (c n) -> p c n", c=DC)
        vb0 = turns[:, 0:4 * P].rearrange("p (b g h e) -> p b g h e", b=2, g=8, h=2)
        diag = sb("diag", [P, P])
        sq = sb("sq", [P, 64])
        sp_ = sb("sp", [P, 64])
        mx0, rs0 = sb("mx0", [P, HEADS]), sq[:, 32:32 + HEADS]
        mx1, rs1 = sp_[:, 0:HEADS], sp_[:, HEADS:2 * HEADS]
        pext = sb("pext", [P, 16])
        top, topv = sb("top", [P, 8]), sb("topv", [P, 8])
        rest = sb("rest", [P, 16])
        w9 = sb("w9", [P, EXPERTS + 1])
        wT9 = sb("wT9", [EXPERTS + 1, P])

        hp, tmp1 = sb("hp", [P, D]), sb("tmp1", [P, 2 * D])
        xo = tmp1[:, 0:D]
        qpT = sb("qpT", [P, DC, P])
        am4, am, ai, gidx = sb("am4", [P, 32]), sb("am", [P, 8]), sb("ai", [P, 8], U32), sb("gidx", [P, 1], U32)
        offs = sb("offs", [P, 1])
        vb1 = sb("vb1", [P, 2, 2, HD])
        P1 = sb("P1", [P, 1024])
        kbd1 = P1[:, :].rearrange("p (b h n) -> p b h n", b=2, h=H8)
        rprob = P1[:, 0:P].rearrange("p (b n) -> p b n", b=2)
        rot, vsb = P1[:, P:4 * P], P1[:, 7 * P:8 * P]
        rqT = P1[:, 4 * P:6 * P].rearrange("p (b h n) -> p b h n", b=2, h=2)
        rkT = P1[:, 6 * P:7 * P]
        PT1 = sb("PT1", [P, 8, P])
        hTp = PT1[:, 4:6, :]
        pt1 = PT1[:, :, :].rearrange("p g n -> p (g n)")
        mem = pt1[:, 0:D]
        memT = pt1[:, D:2 * D].rearrange("p (c n) -> p c n", c=DC)
        memTd = pt1[:, 2 * D:4 * D].rearrange("p (c b e n) -> p c b e n", c=DC, b=2, e=2)
        w32 = sb("w32", [P, PROTOS])
        wf, restf = sb("wf", [P, PROTOS + 8]), sb("restf", [P, PROTOS + 8])
        topf, topvf = sb("topf", [P, 8]), sb("topvf", [P, 8])
        wT32 = sb("wT32", [PROTOS, P])
        setup = share[:, 0:2 * DC * D].rearrange("p (w c n) -> p w c n", w=2, c=DC)
        headw = share[:, 2 * DC * D:2 * DC * D + P]

        const_in, attn0_w_in, ffn0_w_in, l1_w_in = S("const_in"), S("attn0_w_in"), S("ffn0_w_in"), S("l1_w_in")
        headw_zero, headw_in = S("headw_zero"), S("headw_in")
        setup_mm, sets_dve = S("setup_mm"), S("sets_dve")
        x_in, ctx_in = S("x_in", 16), S("ctx_in", 64)
        ctxT_in, ctxT_used = [S(f"ctxT_in{k}", 32) for k in range(4)], S("ctxT_used", 4)
        out_stored = S("out_stored", 16)
        x0_var, x0_rstd = S("x0_var"), S("x0_rstd")
        xa_var, xa_rstd = S("xa_var"), S("xa_rstd")
        xf_var, xf_rstd = S("xf_var"), S("xf_rstd")
        x1_var, x1_rstd = S("x1_var"), S("x1_rstd")
        xr_var, xr_rstd = S("xr_var"), S("xr_rstd")
        xg_var, xg_rstd = S("xg_var"), S("xg_rstd")
        d2_ready, root_ready = S("d2_ready"), S("root_ready")
        h0_ready, h0T_ps, h0T_ready, simq_ready = S("h0_ready"), S("h0T_ps"), S("h0T_ready"), S("simq_ready", 2)
        sim_ps, sim_max, prob_ready = S("sim_ps"), S("sim_max"), S("prob_ready")
        hqn_ready, hqT_ps = S("hqn_ready"), S("hqT_ps")
        probT_ps, probT_act, probT_dve = S("probT_ps", 4), S("probT_act", 2), S("probT_dve", 2)
        hq_ps = S("hq_ps")
        diag_ready, rowmax_ps, gmax_ready = S("diag_ready"), S("rowmax_ps"), S("gmax_ready")
        batt_ready, battz_ps, battw_ready, hc_ps = S("batt_ready"), S("battz_ps"), S("battw_ready"), S("hc_ps")
        feats_ready = S("feats_ready")
        xattn0_ps = S("xattn0_ps")
        ha_ready, haT_ps, haT_ready, haTd_ready = S("ha_ready"), S("haT_ps"), S("haT_ready"), S("haTd_ready", 2)
        qk_ps, v_ps, qT_ready, kT_ready = S("qk_ps"), S("v_ps"), S("qT_ready", 2), S("kT_ready", 2)
        vb0_ready, kbd0_pool, kbd0_dve = S("vb0_ready", 2), S("kbd0_pool"), S("kbd0_dve")
        s0_ps, d0_ready, e0_ready = S("s0_ps"), S("d0_ready"), S("e0_ready")
        pT0_ps, pT0_act, pT0_dve, o0_ps, o0_used = S("pT0_ps", 2), S("pT0_act"), S("pT0_dve"), S("o0_ps"), S("o0_used")
        hf0_ready, hf0T_ps, hf0T_ready = S("hf0_ready"), S("hf0T_ps"), S("hf0T_ready")
        router_ps, rmax_ready, rexp_ready = S("router_ps"), S("rmax_ready"), S("rexp_ready")
        gate_ready, gateT_ps, gateT_ready = S("gate_ready"), S("gateT_ps"), S("gateT_ready")
        hid_ps, gelu_ready, eout_ps, eout_used = S("hid_ps", 9), S("gelu_ready", 9), S("eout_ps", 9), S("eout_used", 9)
        h1_ready, h1T_ps, h1T_ready = S("h1_ready"), S("h1T_ps"), S("h1T_ready")
        qp_ps, qp_ready, amax_done = S("qp_ps"), S("qp_ready"), S("amax_done")
        gidx_ready, mem_in = S("gidx_ready"), S("mem_in", 16)
        memT_ps, memT_ready, memTd_ready = S("memT_ps"), S("memT_ready"), S("memTd_ready", 2)
        mkv_ps, vb1_ready, kbd1_ready = S("mkv_ps"), S("vb1_ready"), S("kbd1_ready")
        s1_ps, d1_ready, e1_ready = S("s1_ps"), S("d1_ready"), S("e1_ready")
        pT1_ps, pT1_act, pT1_dve, o1_ps = S("pT1_ps", 2), S("pT1_act"), S("pT1_dve"), S("o1_ps")
        o1_ready, o1T_ps, o1T_ready, xattn1_ps = S("o1_ready"), S("o1T_ps"), S("o1T_ready"), S("xattn1_ps")
        hr_ready, hrT_ps, hrT_ready, qkv_ps = S("hr_ready"), S("hrT_ps"), S("hrT_ready"), S("qkv_ps")
        rot_ready, v1_ready, qkT_ps, qkT_ready = S("rot_ready"), S("v1_ready"), S("qkT_ps"), S("qkT_ready", 2)
        rs_ps, rd_ready, re_ready, rp_ready = S("rs_ps"), S("rd_ready"), S("re_ready"), S("rp_ready")
        rpT_ps, rpT_ready, ro_ps, ro_act, ro_dve = S("rpT_ps"), S("rpT_ready"), S("ro_ps"), S("ro_act"), S("ro_dve")
        attn1_ps = S("attn1_ps")
        hg_ready, hgT_ps, hgT_ready, dist_ps = S("hg_ready"), S("hgT_ps"), S("hgT_ready"), S("dist_ps")
        low_ps, fs_ready, fe_ready, wt_ready = S("low_ps"), S("fs_ready"), S("fe_ready"), S("wt_ready")
        wtT_ps, wtT_ready = S("wtT_ps"), S("wtT_ready")
        low_ready, lowT_ps, lowT_ready, ffn1_ps, out_ready = S("low_ready"), S("lowT_ps"), S("lowT_ready"), S("ffn1_ps"), S("out_ready")
        q_chain, r_chain, p_chain = S("q_chain", 17), S("r_chain", 9), S("p_chain", 31)

        ctx_rows = a["ctx_1024"]
        x_rows = a["x"].rearrange("b n d -> (b n) d")
        out_rows = a["out"].rearrange("b n d -> (b n) d")
        N_CONST, N_ATTN0, N_FFN0, N_L1 = 3, 5, 7, 10

        def chunked(ap, p=P):
            return ap.rearrange("(c p) n -> p c n", p=p)

        def settle(eng, value):
            if not isinstance(value, int):
                eng.lower_val(value)
            eng.wait_ge(const_in.sem, 16)
            return value

        def block_keys(eng, out, src):
            return eng.tensor_tensor(out, src.rearrange("p (b n) -> p b n", b=2).unsqueeze(2).to_broadcast([P, 2, H8, N]),
                                     headmask.unsqueeze(1).unsqueeze(3).to_broadcast([P, 2, H8, N]), ALU.mult)

        block = ctx.enter_context(nc.Block())

        @block.sync
        def _(sp):
            def load_ctx(u):
                for b in range(2):
                    src = ctx_rows[bass.ds(u * 2 + b, 1), :, :].rearrange("o m d -> (o m) d")
                    sp.dma_start(ctxN[:, b, 0:MC - 1, :], src[0:(MC - 1) * P, :].rearrange("(c p) d -> p c d", p=P)
                                 ).then_inc(ctx_in.sem, 16)
                    sp.dma_start(ctxN[0:MT, b, MC - 1, :], src[(MC - 1) * P:M, :]).then_inc(ctx_in.sem, 16)

            def load_ctxT(u, before=None):
                for k in range(4):
                    cols = slice(k * BANK, min((k + 1) * BANK, M))
                    if before is not None:
                        sp.wait_ge(ctxT_used.sem, ctxT_used.at(before, k + 1))
                    for b in range(2):
                        src = a["ctxT"][bass.ds(u * 2 + b, 1), :, :].rearrange("o (c p) m -> (o p) c m", p=P)
                        sp.dma_start(ctxT[:, :, b, cols], src[:, :, cols]).then_inc(ctxT_in[k].sem, 16)

            def load_x(u):
                sp.dma_start(xin[:, :], x_rows[bass.ds(u * P, P), :]).then_inc(x_in.sem, 16)

            for dst, src in ((con, a["consts"]), (cols, a["cols"]), (rows, a["rows"])):
                sp.dma_start(dst[:, :], src).then_inc(const_in.sem, 16)
            load_x(0)
            sp.dma_start(setup[:, 0], chunked(a["wq0T"])).then_inc(attn0_w_in.sem, 16)
            sp.dma_start(setup[:, 1], chunked(a["wk0T"])).then_inc(attn0_w_in.sem, 16)
            sp.wait_ge(headw_zero.sem, 1)
            for i in range(H8):
                sp.dma_start(headw[i * HD:(i + 1) * HD, i * HD:(i + 1) * HD], a["L0_attn_Wp"]).then_inc(headw_in.sem, 16)
            load_ctxT(0)
            load_ctx(0)
            sp.dma_start(wqv[:, :, :], chunked(a["L0_xattn_W_qv"])).then_inc(attn0_w_in.sem, 16)
            sp.dma_start(wv0[:, :, :], chunked(a["L0_attn_Wv"])).then_inc(attn0_w_in.sem, 16)
            sp.dma_start(wrout[:, :, :], chunked(a["L0_ffn_router_w"])).then_inc(ffn0_w_in.sem, 16)
            sp.dma_start(ebias[:, :], a["ebias"]).then_inc(ffn0_w_in.sem, 16)
            sp.dma_start(sw1[:, :, :], chunked(a["L0_ffn_sw1"])).then_inc(ffn0_w_in.sem, 16)
            sp.dma_start(sw2[:, :, :], chunked(a["L0_ffn_sw2"])).then_inc(ffn0_w_in.sem, 16)
            for dc in range(DC):
                sp.dma_start(rw1[:, dc], a["L0_ffn_rw1"].rearrange("e (c p) h -> p c e h", p=P)[:, dc]
                             ).then_inc(ffn0_w_in.sem, 16)
            for hc in range(HC):
                sp.dma_start(rw2[:, hc], a["L0_ffn_rw2"].rearrange("e (c p) d -> p c e d", p=P)[:, hc]
                             ).then_inc(ffn0_w_in.sem, 16)
            load_ctxT(1, 0)
            sp.dma_start(wq1[:, :, :], chunked(a["wq1T"])).then_inc(l1_w_in.sem, 16)
            for i in range(H8):
                sp.dma_start(wkrep[:, :, i, :], chunked(a["wkv1T"])[:, :, 0:HD]).then_inc(l1_w_in.sem, 16)
            sp.dma_start(wv1[:, :, :], chunked(a["wkv1T"])[:, :, HD:2 * HD]).then_inc(l1_w_in.sem, 16)
            sp.dma_start(wc1[:, :, :], chunked(a["wc1T"])).then_inc(l1_w_in.sem, 16)
            sp.dma_start(wqkv[:, :, :], chunked(a["wqkvT"])).then_inc(l1_w_in.sem, 16)
            sp.dma_start(wo[:, :, :], chunked(a["woT"])).then_inc(l1_w_in.sem, 16)
            sp.dma_start(prot[:, :, :], chunked(a["protT"])).then_inc(l1_w_in.sem, 16)
            sp.dma_start(bT[:, :, :], chunked(a["bT"])).then_inc(l1_w_in.sem, 16)
            sp.dma_start(aT[:, :, :], chunked(a["aT"])).then_inc(l1_w_in.sem, 16)
            sp.dma_start(pbias[:, :], a["L1_ffn_bias"]).then_inc(l1_w_in.sem, 16)

            def prefetch(u, before):
                sp.wait_ge(hq_ps.sem, hq_ps.at(before))
                load_ctx(u)
                sp.wait_ge(ha_ready.sem, ha_ready.at(before))
                load_x(u)

            def store(t):
                sp.wait_ge(out_ready.sem, out_ready.at(t))
                sp.dma_start(out_rows[bass.ds(t * P, P), :], xo).then_inc(out_stored.sem, 16)

            prefetch(1, 0)
            load_ctxT(0, 1)
            prefetch(2, 1)
            with sp.Fori(0, TILES - 3) as t:
                load_ctxT(t + 2, 2 * t + 2)
                load_ctxT(t + 1, 2 * t + 3)
                prefetch(t + 3, t + 2)
                store(t)
            load_ctxT(TILES - 1, 2 * TILES - 4)
            load_ctxT(TILES - 2, 2 * TILES - 3)
            store(TILES - 3)
            load_ctxT(TILES - 1, 2 * TILES - 2)
            store(TILES - 2)
            store(TILES - 1)
            sp.wait_ge(out_stored.sem, out_stored.at(TILES))

        @block.tensor
        def _(pe):
            def wait(sig, tile, k=None):
                pe.wait_ge(sig.sem, sig.at(tile, k))

            def transposes(bank, src, n, sig, width=P, col=0):
                for i in range(n):
                    last = nc.tensor.transpose(ps[0:width, bank, col + i * P:col + (i + 1) * P],
                                               src[:, i * width:(i + 1) * width], ident)
                last.then_inc(sig.sem, 1)

            def setup_weights():
                pe.wait_ge(const_in.sem, 16 * N_CONST)
                pe.wait_ge(attn0_w_in.sem, 16 * 2)
                pe.wait_ge(headw_in.sem, 16 * H8)
                for w in range(2):
                    for dc in range(DC):
                        for c in range(DC):
                            last = nc.tensor.matmul(ps[:, w, dc * D + c * P:dc * D + (c + 1) * P],
                                                    setup[:, w, c, dc * P:(dc + 1) * P], headw, start=True, stop=True)
                for k in range(4):
                    last = nc.tensor.matmul(ps[:, 2, k:k + 1], headw, bqk[:, k:k + 1], start=True, stop=True)
                last.then_inc(setup_mm.sem, 1)
                pe.wait_ge(sets_dve.sem, 2)

            def setup_protos():
                pe.wait_ge(sets_dve.sem, 4)
                for dc in range(DC):
                    last = nc.tensor.matmul(ps[:, 3, 0:PROTOS], ones, tmp1[:, dc * PROTOS:(dc + 1) * PROTOS],
                                            start=(dc == 0), stop=(dc == DC - 1))
                last.then_inc(setup_mm.sem, 1)
                pe.wait_ge(sets_dve.sem, 5)

            def wide_scores(q, each_piece):
                for k in range(4):
                    n = min(BANK, M - k * BANK)
                    for dc in range(DC):
                        for b in range(2):
                            last = nc.tensor.matmul(ps[b * N:(b + 1) * N, k, 0:n], q[:, dc, b * N:(b + 1) * N],
                                                    ctxT[:, dc, b, k * BANK:k * BANK + n],
                                                    start=(dc == 0), stop=(dc == DC - 1))
                    each_piece(last, k)

            def core_scores(qT, kbd, shared, bank, sig):
                for c in range(DC):
                    for b in range(2):
                        k = kbd[:, b] if shared else kbd[:, c, b]
                        last = nc.tensor.matmul(ps[b * N:(b + 1) * N, bank + c, :], qT[:, c, b * N:(b + 1) * N],
                                                k, start=True, stop=True)
                last.then_inc(sig.sem, 1)

            def core_transposes(src, bank, sig):
                for half in range(2):
                    transposes(bank + half, src[:, half * BANK:(half + 1) * BANK], 4, sig)

            def core_values(PT, vb, shared, bank, sig):
                for g in range(8):
                    for b in range(2):
                        v = vb[:, b] if shared else vb[:, b, g]
                        last = nc.tensor.matmul(ps[b * N:(b + 1) * N, bank, g * 32:(g + 1) * 32],
                                                PT[:, g, b * N:(b + 1) * N], v, start=True, stop=True)
                last.then_inc(sig.sem, 1)

            def q_norm_T(u, t):
                wait(h0_ready, u)
                if t is not None:
                    wait(qp_ready, t)
                transposes(7, h0[:, :], 2, h0T_ps, col=2 * P)

            def q_scores(u, load, t):
                wait(simq_ready, u)
                wait(ctxT_in[0], load)
                if t is not None:
                    wait(amax_done, t)

                def each_piece(last, k):
                    last.then_inc(ctxT_used.sem, 1)
                    if k < 3:
                        wait(ctxT_in[k + 1], load)

                wide_scores(simq, each_piece)
                for dc in range(DC):
                    last = nc.tensor.matmul(ps[:, 3, P:P + 1], hT[:, dc, :], wsim[:, dc:dc + 1],
                                            start=(dc == 0), stop=(dc == DC - 1))
                last.then_inc(sim_ps.sem, 1)

            def q_batt_max(u):
                wait(diag_ready, u)
                wait(prob_ready, u)
                nc.tensor.matmul(ps[:, 1, 0:P], ones, diag[:, :], start=True, stop=True).then_inc(rowmax_ps.sem, 1)

            def q_batt_sum(u):
                wait(batt_ready, u)
                nc.tensor.matmul(ps[:, 1, P:P + 1], blockmask, sq[:, 8:9], start=True, stop=True).then_inc(battz_ps.sem, 1)

            def q_batt_mean(u):
                wait(battw_ready, u)
                for dc in range(DC):
                    last = nc.tensor.matmul(ps[:, 1, 2 * P + dc * P:2 * P + (dc + 1) * P], h0[:, dc * P:(dc + 1) * P],
                                            diag[:, :], start=True, stop=True)
                last.then_inc(hc_ps.sem, 1)

            def q_probT_first(u):
                wait(prob_ready, u)
                transposes(2, prob[:, 0:BANK], 4, probT_ps)
                transposes(3, prob[:, BANK:2 * BANK], 4, probT_ps)

            def q_probT_last(u):
                wait(probT_act, u, 1)
                transposes(2, prob[:, 2 * BANK:3 * BANK], 4, probT_ps)
                wait(probT_dve, u, 1)
                nc.tensor.transpose(ps[0:MT, 3, 0:P], prob[:, 3 * BANK:M], ident).then_inc(probT_ps.sem, 1)

            def q_hq(u):
                wait(probT_act, u)
                wait(probT_dve, u)
                wait(ctx_in, u)
                for c in range(MC):
                    r = P if c < MC - 1 else MT
                    for b in range(2):
                        last = nc.tensor.matmul(ps[b * N:(b + 1) * N, 0, 0:D], probT[0:r, c, b * N:(b + 1) * N],
                                                ctxN[0:r, b, c, :], start=(c == 0), stop=(c == MC - 1))
                last.then_inc(hq_ps.sem, 1)

            def q_hqT(u):
                wait(hqn_ready, u)
                transposes(2, tmp, 2, hqT_ps)

            def q_xattn_proj(u):
                wait(feats_ready, u)
                for i in range(8):
                    src = hT[:, i] if i < 2 else featsT[:, i - 2]
                    last = nc.tensor.matmul(ps[:, 1, 0:D], src, wqv[:, i, :], start=(i == 0), stop=(i == 7))
                last.then_inc(xattn0_ps.sem, 1)

            def q_attn_T(u):
                wait(ha_ready, u)
                transposes(3, h0[:, :], 2, haT_ps)

            def q_attn_qk(u):
                wait(haT_ready, u)
                for w in range(2):
                    for c in range(DC):
                        for dc in range(DC):
                            last = nc.tensor.matmul(ps[:, 2, (2 * w + c) * P:(2 * w + c + 1) * P],
                                                    wqkp[:, dc, w, c * P:(c + 1) * P], hT[:, dc, :],
                                                    start=(dc == 0), stop=(dc == DC - 1))
                last.then_inc(qk_ps.sem, 1)

            def q_attn_v(u):
                wait(haTd_ready, u)
                for b in range(2):
                    for dc in range(DC):
                        last = nc.tensor.matmul(ps[:, 3, b * D:(b + 1) * D], hTd[:, dc, b], wv0[:, dc, :],
                                                start=(dc == 0), stop=(dc == DC - 1))
                last.then_inc(v_ps.sem, 1)

            def q_attn_scores(u):
                wait(qT_ready, u)
                wait(kbd0_pool, u)
                wait(kbd0_dve, u)
                wait(vb0_ready, u)
                core_scores(qT0, kbd0, False, 0, s0_ps)

            def q_attn_probT(u):
                wait(e0_ready, u)
                core_transposes(P0, 2, pT0_ps)

            def q_attn_values(u):
                wait(pT0_act, u)
                wait(pT0_dve, u)
                core_values(PT0, vb0, False, 0, o0_ps)

            def hidden(f, n):
                if n == 0:
                    wait(hf0T_ready, f)
                else:
                    wait(gelu_ready, f, n)
                for hc in range(HC):
                    for dc in range(DC):
                        w = sw1[:, dc, hc * P:(hc + 1) * P] if n == 0 else rw1[:, dc, n - 1, hc * P:(hc + 1) * P]
                        last = nc.tensor.matmul(ps[:, 4, hc * P:(hc + 1) * P], w, hfT[:, dc, :],
                                                start=(dc == 0), stop=(dc == DC - 1))
                last.then_inc(hid_ps.sem, 1)

            def output(f, n):
                if n >= 1:
                    wait(eout_used, f, n)
                wait(gelu_ready, f, n + 1)
                if n == 0:
                    wait(gateT_ready, f)
                    nc.tensor.matmul(ps[:, 5, 0:D], wT9[:, :], ebias[:, :], start=True, stop=False)
                for hc in range(HC):
                    w = sw2[:, hc, :] if n == 0 else rw2[:, hc, n - 1, :]
                    last = nc.tensor.matmul(ps[:, 5, 0:D], h1T[:, n % 2, hc, :], w,
                                            start=(hc == 0 and n > 0), stop=(hc == HC - 1))
                last.then_inc(eout_ps.sem, 1)

            def q_route_T(f):
                wait(hf0_ready, f)
                transposes(4, h0[:, :], 2, hf0T_ps)

            def q_route_logits(f):
                wait(hf0T_ready, f)
                for dc in range(DC):
                    last = nc.tensor.matmul(ps[:, 5, 0:EXPERTS], hfT[:, dc, :], wrout[:, dc, :],
                                            start=(dc == 0), stop=(dc == DC - 1))
                last.then_inc(router_ps.sem, 1)

            def q_gates(f):
                wait(gate_ready, f)
                nc.tensor.transpose(ps[0:EXPERTS + 1, 5, 0:P], w9[:, :], ident).then_inc(gateT_ps.sem, 1)

            def p_query_T(t):
                wait(h1_ready, t)
                transposes(6, hp, 2, h1T_ps)

            def p_query_proj(t):
                wait(h1T_ready, t)
                for c in range(DC):
                    for dc in range(DC):
                        last = nc.tensor.matmul(ps[:, 7, c * P:(c + 1) * P], wq1[:, dc, c * P:(c + 1) * P],
                                                hTp[:, dc, :], start=(dc == 0), stop=(dc == DC - 1))
                last.then_inc(qp_ps.sem, 1)

            def p_scores(t, f, load):
                wait(qp_ready, t)
                if f is not None:
                    wait(o0_used, f)
                wait(ctxT_in[0], load)

                def each_piece(last, k):
                    last.then_inc(ctxT_used.sem, 1)
                    if k < 3:
                        wait(ctxT_in[k + 1], load)

                wide_scores(qpT, each_piece)

            def p_mem_T(t):
                wait(mem_in, t)
                transposes(6, mem, 2, memT_ps)

            def p_mem_proj(t, u):
                wait(memT_ready, t)
                wait(memTd_ready, t)
                if u is not None:
                    wait(h0T_ready, u)
                for dc in range(DC):
                    nc.tensor.matmul(ps[:, 7, 0:P], wkrep[:, dc], memT[:, dc, :],
                                     start=(dc == 0), stop=(dc == DC - 1))
                for b in range(2):
                    for dc in range(DC):
                        last = nc.tensor.matmul(ps[:, 7, P + b * HD:P + (b + 1) * HD], memTd[:, dc, b], wv1[:, dc, :],
                                                start=(dc == 0), stop=(dc == DC - 1))
                last.then_inc(mkv_ps.sem, 1)

            def p_xattn_scores(t):
                wait(kbd1_ready, t)
                wait(vb1_ready, t)
                core_scores(qpT, kbd1, True, 6, s1_ps)

            def p_xattn_probT(t):
                wait(e1_ready, t)
                core_transposes(P1, 6, pT1_ps)

            def p_xattn_values(t):
                wait(pT1_act, t)
                wait(pT1_dve, t)
                core_values(PT1, vb1, True, 6, o1_ps)

            def p_xattn_T(t):
                wait(o1_ready, t)
                transposes(7, hp, 2, o1T_ps)

            def p_xattn_proj(t):
                wait(o1T_ready, t)
                for dc in range(DC):
                    last = nc.tensor.matmul(ps[:, 6, 0:D], hTp[:, dc, :], wc1[:, dc, :],
                                            start=(dc == 0), stop=(dc == DC - 1))
                last.then_inc(xattn1_ps.sem, 1)

            def p_rot_T(t):
                wait(hr_ready, t)
                transposes(7, hp, 2, hrT_ps)

            def p_rot_proj(t):
                wait(hrT_ready, t)
                for dc in range(DC):
                    last = nc.tensor.matmul(ps[:, 6, :], hTp[:, dc, :], wqkv[:, dc, :],
                                            start=(dc == 0), stop=(dc == DC - 1))
                last.then_inc(qkv_ps.sem, 1)

            def p_rot_qkT(t):
                wait(rot_ready, t)
                transposes(7, rot, 3, qkT_ps)

            def p_rot_scores(t):
                wait(qkT_ready, t)
                wait(v1_ready, t)
                for b in range(2):
                    last = nc.tensor.matmul(ps[:, 6, b * N:(b + 1) * N], rqT[:, b].rearrange("p h n -> p (h n)"),
                                            rkT[:, b * N:(b + 1) * N], start=True, stop=True)
                last.then_inc(rs_ps.sem, 1)

            def p_rot_probT(t):
                wait(rp_ready, t)
                nc.tensor.transpose(ps[:, 7, 0:P], P1[:, 0:P], ident).then_inc(rpT_ps.sem, 1)

            def p_rot_values(t):
                wait(rpT_ready, t)
                for b in range(2):
                    last = nc.tensor.matmul(ps[:, 6 + b, 0:P], vsb[b * N:(b + 1) * N, :],
                                            PT1[b * N:(b + 1) * N, 0, :], start=True, stop=True)
                last.then_inc(ro_ps.sem, 1)

            def p_rot_out(t):
                wait(ro_act, t)
                wait(ro_dve, t)
                for h in range(2):
                    last = nc.tensor.matmul(ps[:, 6, 0:D], PT1[:, 1 + h, :], wo[:, h, :], start=(h == 0), stop=(h == 1))
                last.then_inc(attn1_ps.sem, 1)

            def p_proto_T(t):
                wait(hg_ready, t)
                transposes(7, hp, 2, hgT_ps)

            def p_proto_dots(t):
                wait(hgT_ready, t)
                for dc in range(DC):
                    last = nc.tensor.matmul(ps[:, 7, 2 * P:2 * P + PROTOS], hTp[:, dc, :], prot[:, dc, :],
                                            start=(dc == 0), stop=(dc == DC - 1))
                last.then_inc(dist_ps.sem, 1)
                for dc in range(DC):
                    last = nc.tensor.matmul(ps[:, 6, :], hTp[:, dc, :], bT[:, dc, :],
                                            start=(dc == 0), stop=(dc == DC - 1))
                last.then_inc(low_ps.sem, 1)

            def p_gates_T(t):
                wait(wt_ready, t)
                nc.tensor.transpose(ps[0:PROTOS, 7, 0:P], w32[:, :], ident).then_inc(wtT_ps.sem, 1)

            def p_low_T(t):
                wait(wtT_ready, t)
                wait(low_ready, t)
                transposes(7, tmp1, 4, lowT_ps)

            def p_proto_out(t):
                wait(lowT_ready, t)
                nc.tensor.matmul(ps[:, 6, 0:D], wT32[:, :], pbias[:, :], start=True, stop=False)
                for c in range(4):
                    last = nc.tensor.matmul(ps[:, 6, 0:D], PT1[:, c, :], aT[:, c, :], start=False, stop=(c == 3))
                last.then_inc(ffn1_ps.sem, 1)

            def tile(t, f, u, p_load, q_load):
                if t is not None:
                    p_query_T(t)
                if t is None and f is not None:
                    pe.wait_ge(ffn0_w_in.sem, 16 * 10)
                if f is not None:
                    q_route_T(f)
                if t is not None:
                    p_query_proj(t)
                if f is not None:
                    q_route_logits(f)
                    hidden(f, 0)
                if t is not None:
                    p_scores(t, f, p_load)
                if f is not None:
                    q_gates(f)
                    hidden(f, 1)
                    output(f, 0)
                    hidden(f, 2)
                    output(f, 1)
                if u is not None:
                    q_norm_T(u, t)
                if f is not None:
                    hidden(f, 3)
                if t is not None:
                    p_mem_T(t)
                if f is not None:
                    output(f, 2)
                if t is not None:
                    p_mem_proj(t, u)
                if f is not None:
                    hidden(f, 4)
                if t is not None:
                    p_xattn_scores(t)
                if u is not None:
                    q_scores(u, q_load, t)
                if t is not None:
                    p_xattn_probT(t)
                if f is not None:
                    output(f, 3)
                    hidden(f, 5)
                if u is not None:
                    q_batt_max(u)
                if t is not None:
                    p_xattn_values(t)
                if u is not None:
                    q_probT_first(u)
                if t is not None:
                    p_xattn_T(t)
                if u is not None:
                    q_probT_last(u)
                    q_batt_sum(u)
                if t is not None:
                    p_xattn_proj(t)
                if u is not None:
                    q_hq(u)
                if t is not None:
                    p_rot_T(t)
                if u is not None:
                    q_batt_mean(u)
                if t is not None:
                    p_rot_proj(t)
                if f is not None:
                    output(f, 4)
                if u is not None:
                    q_hqT(u)
                if t is not None:
                    p_rot_qkT(t)
                if f is not None:
                    hidden(f, 6)
                if t is not None:
                    p_rot_scores(t)
                if t is None and f is None:
                    pe.wait_ge(attn0_w_in.sem, 16 * 4)
                if u is not None:
                    q_xattn_proj(u)
                if t is not None:
                    p_rot_probT(t)
                if f is not None:
                    output(f, 5)
                if t is not None:
                    p_rot_values(t)
                if u is not None:
                    q_attn_T(u)
                if t is not None:
                    p_rot_out(t)
                if u is not None:
                    q_attn_qk(u)
                    q_attn_v(u)
                if t is not None:
                    p_proto_T(t)
                    p_proto_dots(t)
                if u is not None:
                    q_attn_scores(u)
                if f is not None:
                    hidden(f, 7)
                    output(f, 6)
                    hidden(f, 8)
                    output(f, 7)
                if u is not None:
                    q_attn_probT(u)
                if t is not None:
                    p_gates_T(t)
                if f is not None:
                    output(f, 8)
                if t is not None:
                    p_low_T(t)
                if u is not None:
                    q_attn_values(u)
                if t is not None:
                    p_proto_out(t)
            setup_weights()
            tile(None, None, 0, None, 0)
            tile(None, 0, 1, None, 1)
            pe.wait_ge(l1_w_in.sem, 16 * 17)
            setup_protos()
            with pe.Fori(0, TILES - 2) as t:
                tile(t, t + 1, t + 2, 2 * t + 2, 2 * t + 3)
            tile(TILES - 2, TILES - 1, None, 2 * TILES - 2, None)
            tile(TILES - 1, None, None, 2 * TILES - 1, None)

        @block.scalar
        def _(act):
            def wait(sig, tile, k=None):
                act.wait_ge(sig.sem, sig.at(tile, k))

            def copy(out, in_, sig):
                nc.scalar.copy(out, in_).then_inc(sig.sem, 1)

            def halves(bank):
                return ps[:, bank, 0:2 * P].rearrange("p (c n) -> p c n", c=2)

            def q_norm_T(u):
                wait(h0T_ps, u)
                copy(hT[:, :, :], ps[:, 7, 2 * P:4 * P].rearrange("p (c n) -> p c n", c=2), h0T_ready)

            def q_exp(u):
                wait(sim_max, u)
                nc.scalar.activation(prob, wide, ACT.Exp, bias=sq[:, 4:5], accum_out=sq[:, 5:6]).then_inc(prob_ready.sem, 1)

            def q_batt(u):
                wait(gmax_ready, u)
                nc.scalar.activation(sq[:, 8:9], sq[:, 6:7], ACT.Exp, bias=sq[:, 7:8]).then_inc(batt_ready.sem, 1)

            def q_probT_first(u):
                wait(probT_ps, u, 1)
                copy(probT[:, 0:4, :], ps[:, 2, :].rearrange("p (c n) -> p c n", c=4), probT_act)

            def q_probT_last(u):
                wait(probT_ps, u, 3)
                copy(probT[:, 8:12, :], ps[:, 2, :].rearrange("p (c n) -> p c n", c=4), probT_act)

            def q_attn_T(u):
                wait(haT_ps, u)
                copy(hT[:, :, :], halves(3), haT_ready)

            def q_attn_qk(u):
                wait(qk_ps, u)
                for c in range(DC):
                    nc.scalar.activation(kT0[:, c, :], ps[:, 2, (2 + c) * P:(3 + c) * P], ACT.Identity,
                                         bias=bqkp[:, 2 + c:3 + c]).then_inc(kT_ready.sem, 1)
                for c in range(DC):
                    nc.scalar.activation(qT0[:, c, :], ps[:, 2, c * P:(c + 1) * P], ACT.Identity,
                                         bias=bqkp[:, c:c + 1]).then_inc(qT_ready.sem, 1)

            def q_attn_scores(u):
                wait(d0_ready, u)
                nc.scalar.activation(P0, P0, ACT.Exp, scale=HD ** -0.5).then_inc(e0_ready.sem, 1)

            def q_attn_probT(u):
                wait(pT0_ps, u, 1)
                copy(PT0[:, 0:4, :], ps[:, 2, :].rearrange("p (c n) -> p c n", c=4), pT0_act)

            def q_route_T(f):
                wait(hf0T_ps, f)
                copy(hfT[:, :, :], halves(4), hf0T_ready)

            def q_route_exp(f):
                wait(rmax_ready, f)
                nc.scalar.activation(sq[:, 16:24], sq[:, 24:32], ACT.Exp, bias=sq[:, 4:5],
                                     accum_out=sq[:, 5:6]).then_inc(rexp_ready.sem, 1)

            def gelu(f, n):
                wait(hid_ps, f, n + 1)
                if n >= 2:
                    wait(eout_ps, f, n - 1)
                for hc in range(HC):
                    k = n * HC + hc
                    last = nc.scalar.activation(h1T[:, n % 2, hc, :], ps[:, 4, hc * P:(hc + 1) * P], ACT.Gelu,
                                                bias=hbias[:, k:k + 1])
                last.then_inc(gelu_ready.sem, 1)

            def p_query_T(t):
                wait(h1T_ps, t)
                copy(hTp, halves(6), h1T_ready)

            def p_query_proj(t):
                wait(qp_ps, t)
                copy(qpT[:, :, :], halves(7), qp_ready)

            def p_mem_T(t):
                wait(memT_ps, t)
                copy(memT[:, :, :], halves(6), memT_ready)

            def p_xattn_scores(t):
                wait(d1_ready, t)
                nc.scalar.activation(P1[:, :], P1[:, :], ACT.Exp, scale=HD ** -0.5).then_inc(e1_ready.sem, 1)

            def p_xattn_probT(t):
                wait(pT1_ps, t, 1)
                copy(PT1[:, 0:4, :], ps[:, 6, :].rearrange("p (c n) -> p c n", c=4), pT1_act)

            def p_xattn_T(t):
                wait(o1T_ps, t)
                copy(hTp, halves(7), o1T_ready)

            def p_rot_T(t):
                wait(hrT_ps, t)
                copy(hTp, halves(7), hrT_ready)

            def p_rot_proj(t):
                wait(rot_ready, t)
                copy(vsb[:, :], ps[:, 6, 384:512], v1_ready)

            def p_rot_qkT(t):
                wait(qkT_ps, t)
                copy(rqT, ps[:, 7, 0:2 * P].rearrange("p (h b n) -> p b h n", h=2, b=2), qkT_ready)
                copy(rkT, ps[:, 7, 2 * P:3 * P], qkT_ready)

            def p_rot_scores(t):
                wait(rd_ready, t)
                nc.scalar.activation(P1[:, 0:P], P1[:, 0:P], ACT.Exp, scale=K1 ** -0.5).then_inc(re_ready.sem, 1)

            def p_rot_probT(t):
                wait(rpT_ps, t)
                copy(PT1[:, 0, :], ps[:, 7, 0:P], rpT_ready)

            def p_rot_values(t):
                wait(ro_ps, t)
                copy(PT1[:, 1:3, 0:N], ps[:, 6, 0:P].rearrange("p (h n) -> p h n", h=2), ro_act)

            def p_proto_T(t):
                wait(hgT_ps, t)
                copy(hTp, halves(7), hgT_ready)

            def p_proto_exp(t):
                wait(fs_ready, t)
                nc.scalar.activation(w32[:, :], sp_[:, 0:PROTOS], ACT.Exp, bias=sp_[:, 40:41],
                                     accum_out=sp_[:, 41:42]).then_inc(fe_ready.sem, 1)

            def p_gates_T(t):
                wait(wtT_ps, t)
                copy(wT32[:, :], ps[0:PROTOS, 7, 0:P], wtT_ready)

            def p_low_T(t):
                wait(lowT_ps, t)
                copy(PT1[:, 0:4, :], ps[:, 7, :].rearrange("p (c n) -> p c n", c=4), lowT_ready)

            def tile(t, f, u, p_load, q_load):
                if t is not None:
                    p_query_T(t)
                if f is not None:
                    q_route_T(f)
                if t is not None:
                    p_query_proj(t)
                if f is not None:
                    q_route_exp(f)
                    gelu(f, 0)
                    gelu(f, 1)
                    gelu(f, 2)
                if u is not None:
                    q_norm_T(u)
                if t is not None:
                    p_mem_T(t)
                if f is not None:
                    gelu(f, 3)
                    gelu(f, 4)
                if t is not None:
                    p_xattn_scores(t)
                    p_xattn_probT(t)
                if u is not None:
                    q_exp(u)
                    q_batt(u)
                    q_probT_first(u)
                if t is not None:
                    p_xattn_T(t)
                if u is not None:
                    q_probT_last(u)
                if t is not None:
                    p_rot_T(t)
                if f is not None:
                    gelu(f, 5)
                if t is not None:
                    p_rot_proj(t)
                    p_rot_qkT(t)
                    p_rot_scores(t)
                if f is not None:
                    gelu(f, 6)
                if t is not None:
                    p_rot_probT(t)
                    p_rot_values(t)
                if u is not None:
                    q_attn_T(u)
                    q_attn_qk(u)
                if t is not None:
                    p_proto_T(t)
                if f is not None:
                    gelu(f, 7)
                if u is not None:
                    q_attn_scores(u)
                if t is not None:
                    p_proto_exp(t)
                if f is not None:
                    gelu(f, 8)
                if u is not None:
                    q_attn_probT(u)
                if t is not None:
                    p_gates_T(t)
                    p_low_T(t)
            act.wait_ge(const_in.sem, 16 * N_CONST)
            act.wait_ge(sets_dve.sem, 2)
            tile(None, None, 0, None, 0)
            tile(None, 0, 1, None, 1)
            with act.Fori(0, TILES - 2) as t:
                tile(t, t + 1, t + 2, 2 * t + 2, 2 * t + 3)
            tile(TILES - 2, TILES - 1, None, 2 * TILES - 2, None)
            tile(TILES - 1, None, None, 2 * TILES - 1, None)

        @block.vector
        def _(dve):
            v = nc.vector
            ql = Chain(dve, q_chain.sem, q_chain.per)
            rl = Chain(dve, r_chain.sem, r_chain.per)
            pl = Chain(dve, p_chain.sem, p_chain.per)

            def wait(sig, tile, k=None):
                dve.wait_ge(sig.sem, sig.at(tile, k))

            def sync(ins, sig, tile, k=None):
                ins.then_inc(sig.sem, 1)
                wait(sig, tile, k)

            def variance(link, col, x, var_sig):
                link(v.bn_stats(col[:, 50:56], x), settle)
                link(v.bn_aggr(col[:, 56:58], col[:, 50:56]))
                v.tensor_scalar(col[:, 57:58], col[:, 57:58], EPS, None, ALU.add).then_inc(var_sig.sem, 1)

            def normalized(tile, col, x, h, rstd_sig):
                wait(rstd_sig, tile)
                return v.tensor_scalar(h, x, col[:, 56:57], col[:, 58:59], ALU.subtract, ALU.mult)

            def heads(ap):
                return ap.rearrange("p (h m) -> p h m", h=HEADS)

            def each_head(col, n):
                return col[:, :].unsqueeze(2).to_broadcast([P, HEADS, n])

            def q_norm(u):
                ql.begin(u)
                wait(x_in, u)
                variance(ql, sq, xin[:, :], x0_var)

            def q_normed(u):
                normalized(u, sq, xin[:, :], h0[:, :], x0_rstd).then_inc(h0_ready.sem, 1)

            def q_norm_T(u):
                wait(h0T_ready, u)
                for dc in range(DC):
                    v.tensor_scalar(simq[:, dc, :], hT[:, dc, :], wsim[:, 4 + dc:5 + dc],
                                    wsim[:, 2 + dc:3 + dc], ALU.mult, ALU.add).then_inc(simq_ready.sem, 1)

            def q_scores(u):
                wait(sim_ps, u)
                ql(v.reduce_max(sq[:, 3:4], wide, AX.X))
                v.tensor_scalar(sq[:, 4:5], sq[:, 3:4], -1.0, None, ALU.mult)
                sync(v.tensor_scalar(sq[:, 6:7], ps[:, 3, P:P + 1], sq[:, 3:4], bsim, ALU.add, ALU.add), sim_max, u)
                v.tensor_scalar(diag[:, :], ident, sq[:, 6:7], None, ALU.mult).then_inc(diag_ready.sem, 1)

            def q_batt_max(u):
                wait(rowmax_ps, u)
                for b in range(2):
                    i = slice(b * N, (b + 1) * N)
                    ql(v.reduce_max(sq[i, 9:10], ps[i, 1, b * N:(b + 1) * N], AX.X))
                v.tensor_scalar(sq[:, 7:8], sq[:, 9:10], -1.0, None, ALU.mult).then_inc(gmax_ready.sem, 1)

            def q_batt_sum(u):
                wait(battz_ps, u)
                ql(v.reciprocal(sq[:, 10:11], ps[:, 1, P:P + 1]))
                ql(v.tensor_tensor(sq[:, 12:13], sq[:, 10:11], sq[:, 8:9], ALU.mult))
                v.tensor_scalar(diag[:, :], blockmask, sq[:, 12:13], None, ALU.mult).then_inc(battw_ready.sem, 1)

            def q_probT_first(u):
                wait(probT_ps, u, 2)
                v.tensor_copy(probT[:, 4:8, :], ps[:, 3, :].rearrange("p (c n) -> p c n", c=4)).then_inc(probT_dve.sem, 1)

            def q_probT_last(u):
                wait(probT_ps, u, 4)
                v.tensor_copy(probT[0:MT, MC - 1, :], ps[0:MT, 3, 0:P]).then_inc(probT_dve.sem, 1)

            def q_hq(u):
                ql(v.reciprocal(sq[:, 11:12], sq[:, 5:6]))
                wait(hq_ps, u)
                v.tensor_scalar(tmp, ps[:, 0, 0:D], sq[:, 11:12], None, ALU.mult).then_inc(hqn_ready.sem, 1)

            def q_hqT(u):
                hq = ps[:, 2, 0:2 * P].rearrange("p (c n) -> p c n", c=DC)
                wait(hqT_ps, u)
                v.tensor_copy(featsT[:, 0:2, :], hq)
                v.tensor_tensor(featsT[:, 2:4, :], hq, hT[:, :, :], ALU.mult)
                hc = ps[:, 1, 2 * P:4 * P].rearrange("p (c n) -> p c n", c=DC)
                wait(hc_ps, u)
                v.tensor_tensor(featsT[:, 4:6, :], hc, hT[:, :, :], ALU.mult).then_inc(feats_ready.sem, 1)

            def q_xattn_proj(u):
                wait(xattn0_ps, u)
                ql(v.tensor_tensor(tmp, ps[:, 1, 0:D], bqv, ALU.add))
                ql(v.tensor_tensor(xq[:, :], tmp, xin[:, :], ALU.add))

            def q_attn_norm(u):
                variance(ql, sq, xq[:, :], xa_var)

            def q_attn_normed(u):
                normalized(u, sq, xq[:, :], h0[:, :], xa_rstd).then_inc(ha_ready.sem, 1)

            def q_attn_T(u):
                wait(haT_ready, u)
                for dc in range(DC):
                    src = hT[:, dc, :].rearrange("p (b n) -> p b n", b=2)
                    v.tensor_copy(hTd[:, dc], src.unsqueeze(2).to_broadcast([P, 2, 2, N])).then_inc(haTd_ready.sem, 1)

            def q_attn_v(u):
                wait(v_ps, u)
                for b in range(2):
                    src = ps[:, 3, b * D:(b + 1) * D].rearrange("p (g h e) -> p g h e", g=8, h=2)
                    v.tensor_tensor(vb0[:, b], src, halfmask.unsqueeze(1).unsqueeze(3).to_broadcast([P, 8, 2, HD]),
                                    ALU.mult).then_inc(vb0_ready.sem, 1)

            def q_attn_keys(u):
                wait(kT_ready, u)
                block_keys(v, kbd0[:, 1], kT0[:, 1, :]).then_inc(kbd0_dve.sem, 1)

            def core_softmax(link, tile, s_sig, bank, mx, prb, d_sig):
                wait(s_sig, tile)
                sc = ps[:, bank:bank + 2, :].rearrange("p c (h m) -> p (c h) m", m=N)
                link(v.tensor_reduce(mx[:, :], sc, AX.X, ALU.max))
                v.tensor_tensor(heads(prb), sc, each_head(mx, N), ALU.subtract).then_inc(d_sig.sem, 1)

            def core_sums(link, prb, rs):
                link(v.tensor_reduce(rs[:, :], heads(prb), AX.X, ALU.add))
                link(v.reciprocal(rs[:, :], rs[:, :]))

            def q_attn_scores(u):
                core_softmax(ql, u, s0_ps, 0, mx0, P0, d0_ready)

            def q_attn_probT(u):
                wait(pT0_ps, u, 2)
                v.tensor_copy(PT0[:, 4:8, :], ps[:, 3, :].rearrange("p (c n) -> p c n", c=4)).then_inc(pT0_dve.sem, 1)

            def q_attn_sums(u):
                wait(e0_ready, u)
                core_sums(ql, P0, rs0)

            def q_attn_values(u):
                wait(o0_ps, u)
                sync(v.tensor_tensor(heads(tmp), heads(ps[:, 0, 0:D]), each_head(rs0, HD), ALU.mult), o0_used, u)
                ql(v.tensor_tensor(tmp, tmp, bv, ALU.add))
                ql(v.tensor_tensor(xq[:, :], xq[:, :], tmp, ALU.add))
                ql.end()

            def top_two(link, values, ext, tp, tv, rst):
                link(v.max(tp[:, :], values))
                link(v.tensor_copy(tv[:, 0:2], tp[:, 0:2]), settle)
                link(v.match_replace(rst[:, :], tv[:, :], ext[:, :], 0.0))

            def q_route_norm(f):
                rl.begin(f)
                variance(rl, sq, xq[:, :], xf_var)

            def q_route_normed(f):
                normalized(f, sq, xq[:, :], h0[:, :], xf_rstd).then_inc(hf0_ready.sem, 1)

            def q_route_logits(f):
                wait(router_ps, f)
                rl(v.tensor_tensor(sq[:, 24:32], ps[:, 5, 0:EXPERTS], rb, ALU.add))
                rl(v.reduce_max(sq[:, 3:4], sq[:, 24:32], AX.X))
                v.tensor_scalar(sq[:, 4:5], sq[:, 3:4], -1.0, None, ALU.mult).then_inc(rmax_ready.sem, 1)

            def q_route_gates(f):
                wait(rexp_ready, f)
                rl(v.reciprocal(sq[:, 10:11], sq[:, 5:6]))
                rl(v.tensor_scalar(pext[:, 0:8], sq[:, 16:24], sq[:, 10:11], None, ALU.mult), settle)
                top_two(rl, pext[:, 0:8], pext, top, topv, rest)
                v.tensor_tensor(w9[:, 0:8], pext[:, 0:8], rest[:, 0:8], ALU.subtract).then_inc(gate_ready.sem, 1)

            def q_gates(f):
                wait(gateT_ps, f)
                v.tensor_copy(wT9[:, :], ps[0:EXPERTS + 1, 5, 0:P]).then_inc(gateT_ready.sem, 1)
                rl.end()

            def weigh(f, n):
                wait(eout_ps, f, n + 1)
                bank = ps[:, 5, 0:D]
                if n == 0:
                    ins = v.tensor_tensor(xf[:, :], bank, xq[:, :], ALU.add)
                else:
                    ins = v.scalar_tensor_tensor((xl if n == EXPERTS else xf)[:, :], bank, w9[:, n - 1:n], xf[:, :],
                                                 ALU.mult, ALU.add)
                sync(ins, eout_used, f, n + 1)

            def p_norm(t):
                pl.begin(t)
                variance(pl, sp_, xl[:, :], x1_var)

            def p_normed(t):
                normalized(t, sp_, xl[:, :], hp[:, :], x1_rstd).then_inc(h1_ready.sem, 1)

            def p_maxima(t, load):
                for k in range(4):
                    dve.wait_ge(ctxT_used.sem, settle(dve, ctxT_used.at(load, k + 1)))
                    ins = v.max(am4[:, 8 * k:8 * k + 8], ps[:, k, 0:min(BANK, M - k * BANK)])
                pl(ins, settle)
                pl(v.max(am[:, :], am4[:, :]), settle)

            def p_argmax(t):
                sync(v.max_index(ai[:, :], am[:, :], wide), amax_done, t)
                v.tensor_scalar(gidx[:, :], ai[:, 0:1], offs[:, 0:1], None, ALU.add).then_inc(gidx_ready.sem, 1)

            def p_mem_T(t):
                wait(gidx_ready, t)
                pl(v.tensor_scalar(offs[:, :], offs[:, :], float(2 * M), None, ALU.add))
                wait(memT_ready, t)
                for dc in range(DC):
                    src = memT[:, dc, :].rearrange("p (b n) -> p b n", b=2)
                    v.tensor_copy(memTd[:, dc], src.unsqueeze(2).to_broadcast([P, 2, 2, N])).then_inc(memTd_ready.sem, 1)

            def p_mem_proj(t):
                wait(mkv_ps, t)
                src = ps[:, 7, P:P + 2 * HD].rearrange("p (b e) -> p b e", b=2)
                v.tensor_tensor(vb1[:, :, :, :], src.unsqueeze(2).to_broadcast([P, 2, 2, HD]),
                                halfmask.unsqueeze(1).unsqueeze(3).to_broadcast([P, 2, 2, HD]), ALU.mult
                                ).then_inc(vb1_ready.sem, 1)
                block_keys(v, kbd1, ps[:, 7, 0:P]).then_inc(kbd1_ready.sem, 1)

            def p_xattn_scores(t):
                core_softmax(pl, t, s1_ps, 6, mx1, P1[:, :], d1_ready)

            def p_xattn_probT(t):
                wait(pT1_ps, t, 2)
                v.tensor_copy(PT1[:, 4:8, :], ps[:, 7, :].rearrange("p (c n) -> p c n", c=4)).then_inc(pT1_dve.sem, 1)

            def p_xattn_sums(t):
                wait(e1_ready, t)
                core_sums(pl, P1[:, :], rs1)

            def p_xattn_values(t):
                wait(o1_ps, t)
                v.tensor_tensor(heads(hp[:, :]), heads(ps[:, 6, 0:D]), each_head(rs1, HD), ALU.mult).then_inc(o1_ready.sem, 1)

            def p_xattn_proj(t):
                wait(xattn1_ps, t)
                pl(v.tensor_tensor(xp[:, :], ps[:, 6, 0:D], xl[:, :], ALU.add))

            def p_rot_norm(t):
                variance(pl, sp_, xp[:, :], xr_var)

            def p_rot_normed(t):
                normalized(t, sp_, xp[:, :], hp[:, :], xr_rstd).then_inc(hr_ready.sem, 1)

            def p_rot_proj(t):
                wait(qkv_ps, t)
                wait(out_stored, t)
                qk = ps[:, 6, 0:384].rearrange("p (j k two) -> p j k two", j=3, two=2)
                other = tmp1[:, 0:384].rearrange("p (j k two) -> p j k two", j=3, two=2)
                sn = sin.rearrange("p (k two) -> p k two", two=2)
                for e in range(2):
                    v.tensor_tensor(other[:, :, :, e], qk[:, :, :, 1 - e],
                                    sn[:, :, e].unsqueeze(1).to_broadcast([P, 3, K1 // 2]), ALU.mult)
                pl(v.tensor_tensor(rot.rearrange("p (j k) -> p j k", j=3), ps[:, 6, 0:384].rearrange("p (j k) -> p j k", j=3),
                                   cos.unsqueeze(1).to_broadcast([P, 3, K1]), ALU.mult))
                v.tensor_tensor(rot, rot, tmp1[:, 0:384], ALU.add).then_inc(rot_ready.sem, 1)

            def p_rot_scores(t):
                wait(rs_ps, t)
                pl(v.tensor_tensor(rprob, ps[:, 6, 0:P].rearrange("p (b n) -> p b n", b=2),
                                   causal.unsqueeze(1).to_broadcast([P, 2, N]), ALU.add))
                pl(v.tensor_reduce(sp_[:, 0:2], rprob, AX.X, ALU.max))
                v.tensor_tensor(rprob, rprob, sp_[:, 0:2].unsqueeze(2).to_broadcast([P, 2, N]), ALU.subtract
                                ).then_inc(rd_ready.sem, 1)

            def p_rot_probs(t):
                wait(re_ready, t)
                pl(v.tensor_reduce(sp_[:, 2:4], rprob, AX.X, ALU.add))
                pl(v.reciprocal(sp_[:, 4:6], sp_[:, 2:4]))
                v.tensor_tensor(rprob, rprob, sp_[:, 4:6].unsqueeze(2).to_broadcast([P, 2, N]), ALU.mult
                                ).then_inc(rp_ready.sem, 1)

            def p_rot_values(t):
                wait(ro_ps, t)
                v.tensor_copy(PT1[:, 1:3, N:2 * N], ps[:, 7, 0:P].rearrange("p (h n) -> p h n", h=2)).then_inc(ro_dve.sem, 1)

            def p_rot_out(t):
                wait(attn1_ps, t)
                pl(v.tensor_tensor(xp[:, :], ps[:, 6, 0:D], xp[:, :], ALU.add))

            def p_proto_norm(t):
                variance(pl, sp_, xp[:, :], xg_var)

            def p_proto_normed(t):
                sync(normalized(t, sp_, xp[:, :], hp[:, :], xg_rstd), hg_ready, t)
                pl(v.tensor_tensor_reduce(tmp1[:, 0:D], hp[:, :], hp[:, :], 1.0, 0.0, ALU.mult, ALU.add, sp_[:, 42:43]))

            def p_proto_dots(t):
                wait(dist_ps, t)
                dst = sp_[:, 0:PROTOS]
                pl(v.scalar_tensor_tensor(dst, ps[:, 7, 2 * P:2 * P + PROTOS], -2.0, p2[:, :], ALU.mult, ALU.add))
                v.tensor_scalar(dst, dst, sp_[:, 42:43], 0.0, ALU.add, ALU.max).then_inc(d2_ready.sem, 1)

            def p_proto_root(t):
                dst = sp_[:, 0:PROTOS]
                wait(root_ready, t)
                pl(v.tensor_scalar(dst, dst, tneg[:, 0:1], None, ALU.mult))
                pl(v.reduce_max(sp_[:, 43:44], dst, AX.X))
                v.tensor_scalar(sp_[:, 40:41], sp_[:, 43:44], -1.0, None, ALU.mult).then_inc(fs_ready.sem, 1)

            def p_proto_gates(t):
                wait(fe_ready, t)
                pl(v.reciprocal(sp_[:, 44:45], sp_[:, 41:42]))
                pl(v.tensor_scalar(wf[:, 0:PROTOS], w32[:, :], sp_[:, 44:45], None, ALU.mult), settle)
                top_two(pl, wf[:, 0:PROTOS], wf, topf, topvf, restf)
                pl(v.tensor_tensor(w32[:, :], wf[:, 0:PROTOS], restf[:, 0:PROTOS], ALU.subtract))
                pl(v.tensor_tensor(sp_[:, 45:46], topf[:, 0:1], topf[:, 1:2], ALU.add))
                pl(v.reciprocal(sp_[:, 46:47], sp_[:, 45:46]))
                sync(v.tensor_scalar(w32[:, :], w32[:, :], sp_[:, 46:47], None, ALU.mult), wt_ready, t)

            def p_low(t):
                wait(low_ps, t)
                v.tensor_tensor(tmp1[:, :].rearrange("p (k r) -> p k r", r=RANK),
                                ps[:, 6, :].rearrange("p (k r) -> p k r", r=RANK),
                                w32[:, :].unsqueeze(2).to_broadcast([P, PROTOS, RANK]), ALU.mult).then_inc(low_ready.sem, 1)

            def p_proto_out(t):
                wait(ffn1_ps, t)
                v.tensor_tensor(xo, ps[:, 6, 0:D], xp[:, :], ALU.add).then_inc(out_ready.sem, 1)
                pl.end()

            def tile(t, f, u, p_load, q_load):
                if t is not None:
                    p_norm(t)
                if f is not None:
                    q_route_norm(f)
                if t is not None:
                    p_normed(t)
                if f is not None:
                    q_route_normed(f)
                    q_route_logits(f)
                    q_route_gates(f)
                    q_gates(f)
                if t is not None:
                    p_maxima(t, p_load)
                    p_argmax(t)
                if u is not None:
                    q_norm(u)
                if f is not None:
                    weigh(f, 0)
                if u is not None:
                    q_normed(u)
                if f is not None:
                    weigh(f, 1)
                if u is not None:
                    q_norm_T(u)
                if t is not None:
                    p_mem_T(t)
                if f is not None:
                    weigh(f, 2)
                if t is not None:
                    p_mem_proj(t)
                    p_xattn_scores(t)
                if u is not None:
                    q_scores(u)
                if t is not None:
                    p_xattn_probT(t)
                    p_xattn_sums(t)
                if u is not None:
                    q_batt_max(u)
                if t is not None:
                    p_xattn_values(t)
                if u is not None:
                    q_probT_first(u)
                    q_probT_last(u)
                if t is not None:
                    p_xattn_proj(t)
                    p_rot_norm(t)
                if u is not None:
                    q_batt_sum(u)
                if t is not None:
                    p_rot_normed(t)
                if f is not None:
                    weigh(f, 3)
                if u is not None:
                    q_hq(u)
                if t is not None:
                    p_rot_proj(t)
                if f is not None:
                    weigh(f, 4)
                if u is not None:
                    q_hqT(u)
                if t is not None:
                    p_rot_scores(t)
                    p_rot_probs(t)
                if u is not None:
                    q_xattn_proj(u)
                    q_attn_norm(u)
                    q_attn_normed(u)
                if t is not None:
                    p_rot_values(t)
                    p_rot_out(t)
                if u is not None:
                    q_attn_T(u)
                if t is not None:
                    p_proto_norm(t)
                    p_proto_normed(t)
                if u is not None:
                    q_attn_v(u)
                    q_attn_keys(u)
                if t is not None:
                    p_proto_dots(t)
                if f is not None:
                    weigh(f, 5)
                if u is not None:
                    q_attn_scores(u)
                if t is not None:
                    p_proto_root(t)
                if f is not None:
                    weigh(f, 6)
                if t is not None:
                    p_proto_gates(t)
                if f is not None:
                    weigh(f, 7)
                if t is not None:
                    p_low(t)
                if u is not None:
                    q_attn_probT(u)
                    q_attn_sums(u)
                if f is not None:
                    weigh(f, 8)
                if u is not None:
                    q_attn_values(u)
                if t is not None:
                    p_proto_out(t)
            v.memset(headw, 0.0).then_inc(headw_zero.sem, 1)
            v.memset(pext[:, :], -1.0)
            v.memset(topv[:, :], -1.0)
            v.memset(wf[:, :], -1.0)
            v.memset(topvf[:, :], -1.0)
            v.memset(w9[:, :], 1.0)
            v.memset(h0[:, :], 1.0).then_inc(sets_dve.sem, 1)
            dve.wait_ge(sets_dve.sem, 1)
            dve.wait_ge(const_in.sem, 16 * N_CONST)
            v.tensor_copy(offs[:, :], offs0)
            dve.wait_ge(setup_mm.sem, 1)
            for w in range(2):
                v.tensor_copy(wqkp[:, :, w, :], ps[:, w, :].rearrange("p (c n) -> p c n", c=DC))
            v.tensor_copy(bqkp[:, :], ps[:, 2, 0:4]).then_inc(sets_dve.sem, 1)
            tile(None, None, 0, None, 0)
            tile(None, 0, 1, None, 1)
            v.tensor_scalar(sp_[:, 1:2], temp, -1.0, None, ALU.mult).then_inc(sets_dve.sem, 1)
            dve.wait_ge(sets_dve.sem, 3)
            dve.wait_ge(l1_w_in.sem, 16 * 17)
            v.tensor_tensor(tmp1[:, 0:DC * PROTOS].rearrange("p (c n) -> p c n", c=DC), prot[:, :, :], prot[:, :, :],
                            ALU.mult).then_inc(sets_dve.sem, 1)
            dve.wait_ge(setup_mm.sem, 2)
            v.tensor_copy(p2[:, :], ps[:, 3, 0:PROTOS]).then_inc(sets_dve.sem, 1)
            v.tensor_tensor(sp_[:, 2:3], temp, sp_[:, 1:2], ALU.max).then_inc(sets_dve.sem, 1)
            dve.wait_ge(sets_dve.sem, 6)
            v.tensor_scalar(tneg[:, :], sp_[:, 2:3], 0.1, None, ALU.max).then_inc(sets_dve.sem, 1)
            dve.wait_ge(sets_dve.sem, 7)
            v.reciprocal(sp_[:, 0:1], tneg[:, :]).then_inc(sets_dve.sem, 1)
            dve.wait_ge(sets_dve.sem, 8)
            v.tensor_scalar(tneg[:, :], sp_[:, 0:1], -1.0, None, ALU.mult).then_inc(sets_dve.sem, 1)
            dve.wait_ge(sets_dve.sem, 9)
            v.tensor_copy(sp_[:, 0:1], tneg[:, :]).then_inc(out_stored.sem, 16)
            with dve.Fori(0, TILES - 2) as t:
                tile(t, t + 1, t + 2, 2 * t + 2, 2 * t + 3)
            tile(TILES - 2, TILES - 1, None, 2 * TILES - 2, None)
            tile(TILES - 1, None, None, 2 * TILES - 1, None)

        @block.gpsimd
        def _(pool):
            def q_keys(u):
                pool.wait_ge(kT_ready.sem, kT_ready.at(u))
                block_keys(nc.gpsimd, kbd0[:, 0], kT0[:, 0, :]).then_inc(kbd0_pool.sem, 1)

            def p_gather(t):
                pool.wait_ge(gidx_ready.sem, settle(pool, gidx_ready.at(t)))
                pool.indirect_dma_start(mem[:, :], None, ctx_rows.rearrange("b m d -> (b m) d"),
                                        bass.IndirectOffsetOnAxis(gidx[:, 0:1], 0)).then_inc(mem_in.sem, 16)

            def rstd(col, tile, var_sig, rstd_sig):
                pool.wait_ge(var_sig.sem, var_sig.at(tile))
                nc.gpsimd.tensor_tensor(col[:, 58:59], col[:, 57:58], minus_half, ALU.pow).then_inc(rstd_sig.sem, 1)

            def p_root(t):
                pool.wait_ge(d2_ready.sem, d2_ready.at(t))
                nc.gpsimd.tensor_tensor(sp_[:, 0:PROTOS], sp_[:, 0:PROTOS], half.to_broadcast([P, PROTOS]),
                                        ALU.pow).then_inc(root_ready.sem, 1)

            def tile(t, f, u, p_load, q_load):
                if t is not None:
                    rstd(sp_, t, x1_var, x1_rstd)
                if f is not None:
                    rstd(sq, f, xf_var, xf_rstd)
                if t is not None:
                    p_gather(t)
                if u is not None:
                    rstd(sq, u, x0_var, x0_rstd)
                if t is not None:
                    rstd(sp_, t, xr_var, xr_rstd)
                if u is not None:
                    rstd(sq, u, xa_var, xa_rstd)
                if t is not None:
                    rstd(sp_, t, xg_var, xg_rstd)
                if u is not None:
                    q_keys(u)
                if t is not None:
                    p_root(t)

            pool.wait_ge(const_in.sem, 16 * N_CONST)
            tile(None, None, 0, None, 0)
            tile(None, 0, 1, None, 1)
            with pool.Fori(0, TILES - 2) as t:
                tile(t, t + 1, t + 2, 2 * t + 2, 2 * t + 3)
            tile(TILES - 2, TILES - 1, None, 2 * TILES - 2, None)
            tile(TILES - 1, None, None, 2 * TILES - 1, None)


def constants():
    c = np.zeros((P, C_END), np.float32)
    p = np.arange(P)
    c[:, C_ID:C_ID + P] = np.eye(P)
    c[:, C_BLK:C_BLK + P] = p[:, None] // N == p[None] // N
    c[:, C_HEAD:C_HEAD + H8] = p[:, None] // HD == np.arange(H8)[None]
    c[:, C_HALF:C_HALF + 2] = p[:, None] // N == np.arange(2)[None]
    theta = np.float32(10000.0) ** (np.float32(-2.0) * np.arange(0, K1, 2, dtype=np.float32) / np.float32(K1))
    angle = (p % N).astype(np.float32)[:, None] * theta[None]
    c[:, C_COS:C_COS + K1] = np.repeat(np.cos(angle), 2, 1)
    c[:, C_SIN:C_SIN + K1] = np.stack([-np.sin(angle), np.sin(angle)], 2).reshape(P, K1)
    c[:, C_CAUSAL:C_CAUSAL + N] = np.where(np.arange(N)[None] <= (p % N)[:, None], 0.0, NEG)
    c[:, C_ONES:C_ONES + P] = 1.0
    c[:, C_OFFS] = p // N * M
    c[:, C_EXP:C_EXP + 2] = -0.5, 0.5
    return c


_AS_IS = ['x', 'ctx_1024', 'L0_xattn_W_qv', 'L0_attn_Wv', 'L0_attn_Wp', 'L0_ffn_router_w', 'L0_ffn_sw1', 'L0_ffn_sw2',
          'L0_ffn_rw1', 'L0_ffn_rw2', 'L1_ffn_bias']


def kernel(**inputs):
    import numpy as _np
    import concourse.bacc as _bacc
    from concourse import mybir as _mybir
    from concourse.bass_utils import run_bass_kernel_spmd as _run

    i = {k: _np.asarray(v) for k, v in inputs.items()}
    laid = {k: i[k] for k in _AS_IS}
    laid["consts"] = constants()
    laid["ctxT"] = i['ctx_1024'].transpose(0, 2, 1)
    hidden = _np.concatenate([i['L0_ffn_sb1'][None], i['L0_ffn_rb1']], 0)
    laid["cols"] = _np.concatenate([
        i['L0_xattn_w_sim'].reshape(6, P).T, i['L0_attn_bq'].reshape(2, P).T, i['L0_attn_bk'].reshape(2, P).T,
        _np.broadcast_to(i['L0_xattn_b_sim'].reshape(1, 1), (P, 1)), hidden.reshape(9 * HC, P).T,
        _np.broadcast_to(i['L1_ffn_temp'].reshape(1, 1), (P, 1))], 1)
    laid["rows"] = _np.broadcast_to(_np.concatenate([i['L0_xattn_b_qv'], i['L0_attn_bv'], i['L0_ffn_router_b']])[None],
                                    (P, 2 * D + EXPERTS))
    laid["ebias"] = _np.concatenate([i['L0_ffn_rb2'], i['L0_ffn_sb2'][None]], 0)
    laid["wq0T"], laid["wk0T"] = i['L0_attn_Wq'].T, i['L0_attn_Wk'].T
    laid["wq1T"], laid["wkv1T"], laid["wc1T"] = i['L1_xattn_Wq'].T, i['L1_xattn_Wkv'].T, i['L1_xattn_Wc'].T
    laid["wqkvT"] = _np.concatenate([i['L1_attn_Wq'].reshape(2 * K1, D), i['L1_attn_Wk'], i['L1_attn_Wv']], 0).T
    laid["woT"] = i['L1_attn_Wo'].T
    laid["protT"] = i['L1_ffn_prototypes'].T
    laid["bT"] = i['L1_ffn_B'].reshape(PROTOS * RANK, D).T
    laid["aT"] = i['L1_ffn_A'].transpose(0, 2, 1).reshape(PROTOS * RANK, D)

    nc = _bacc.Bacc("TRN2", target_bir_lowering=False, num_devices=1)
    arrays, aps = {}, {}
    for name, arr in laid.items():
        arr = _np.ascontiguousarray(arr)
        arrays[f"in_{name}"] = arr
        aps[name] = nc.dram_tensor(f"in_{name}", arr.shape, _mybir.dt.from_np(arr.dtype), kind="ExternalInput").ap()
    aps["out"] = nc.dram_tensor("out_0", (B, N, D), F32, kind="ExternalOutput").ap()
    build(nc, aps)
    r = _run(nc, [arrays], core_ids=[0])
    return r.results[0]["out_0"]
```
